# Optimizing a Trainium2 kernel written in Bass

```python
import numpy as np
import jax
import jax.numpy as jnp

def _softmax(x, axis=-1):
    return jax.nn.softmax(x, axis=axis)

def _gelu(x):
    return jax.nn.gelu(x, approximate=True)

def _silu(x):
    return jax.nn.silu(x)

def _sigmoid(x):
    return jax.nn.sigmoid(x)

def _layernorm(x, axis=-1, eps=1e-05):
    m = jnp.mean(x, axis=axis, keepdims=True)
    v = jnp.var(x, axis=axis, keepdims=True)
    return (x - m) / jnp.sqrt(v + eps)

def _scatter_add(tgt, idx, src, axis=0):
    return tgt.at[idx].add(src)

def _segment_sum(src, seg, n):
    return jax.ops.segment_sum(src, seg, n)
kernel_name = 'mk_xattn_ffn_d2_seqx_r8_bb6372'

def setup_inputs(seed: int=0):
    np.random.seed(seed)
    _w = jnp.asarray

    def _rec_inputs():
        import jax
        import jax.numpy as jnp
        _rk = jax.random.key(seed)
        x = -0.000125 + 0.9999 * jax.random.normal(jax.random.fold_in(_rk, 1), (32, 64, 512), jnp.float32)
        _lenS = 64 - jax.random.randint(jax.random.fold_in(_rk, 7), (32,), 0, max(1, 64 // 4) + 1, jnp.int32)
        _lenS2 = 64 - jax.random.randint(jax.random.fold_in(_rk, 8), (32,), 0, max(1, 64 // 4) + 1, jnp.int32)
        _ctx_4096P = jax.random.normal(jax.random.fold_in(_rk, 11), (32, 16, 512), jnp.float32)
        _ctx_4096c = jax.random.dirichlet(jax.random.fold_in(_rk, 511), 0.3 * jnp.ones((16,), jnp.float32), (32, 64))
        _ctx_4096t = jnp.einsum('bsk,bkd->bsd', _ctx_4096c, _ctx_4096P)
        _ctx_4096t = _ctx_4096t * jax.lax.rsqrt(jnp.mean(jnp.square(_ctx_4096t)) + 1e-12) * 0.953939
        ctx_4096 = -1.52775e-05 + 0.999936 * (_ctx_4096t + 0.3 * jax.random.normal(jax.random.fold_in(_rk, 611), (32, 64, 512), jnp.float32))
        return (x, ctx_4096)
    x, ctx_4096 = _rec_inputs()

    def _L0_xattn_setup():
        import jax, jax.numpy as jnp
        import numpy as np
        NUM_HEADS = 8

        def _proj(W, b, x):
            return jnp.einsum('oi,bil->bol', W, x) + b[:, None]
        key = jax.random.key(seed)
        ks = jax.random.split(key, 11)
        B, D, L = (16, 64, 512)
        s = 1.0 / np.sqrt(D).astype(np.float32)
        return {'x_query': jax.random.normal(ks[0], (B, D, L), jnp.float32), 'x_key': jax.random.normal(ks[1], (B, D, L), jnp.float32), 'x_value': jax.random.normal(ks[2], (B, D, L), jnp.float32), 'Wq': jax.random.normal(ks[3], (D, D), jnp.float32) * s, 'bq': jax.random.normal(ks[4], (D,), jnp.float32) * 0.01, 'Wk': jax.random.normal(ks[5], (D, D), jnp.float32) * s, 'bk': jax.random.normal(ks[6], (D,), jnp.float32) * 0.01, 'Wv': jax.random.normal(ks[7], (D, D), jnp.float32) * s, 'bv': jax.random.normal(ks[8], (D,), jnp.float32) * 0.01, 'Wo': jax.random.normal(ks[9], (D, D), jnp.float32) * s, 'bo': jax.random.normal(ks[10], (D,), jnp.float32) * 0.01}
    _L0_xattn_all = _L0_xattn_setup()
    _L0_xattn_in = {k: v for k, v in _L0_xattn_all.items() if k in ('Wq', 'bq', 'Wk', 'bk', 'Wv', 'bv', 'Wo', 'bo')}
    del _L0_xattn_all

    def _L0_ffn_setup():
        import jax, jax.numpy as jnp
        import numpy as np
        import math
        SQRT7 = math.sqrt(7.0)
        EPS = 1e-05

        def int4_quant(x):
            beta = jnp.mean(jnp.abs(x), axis=-1, keepdims=True)
            x_q = jnp.clip(jnp.round(x * SQRT7 / (beta + EPS)), -8, 7)
            return x_q * (beta * SQRT7) / SQRT7

        def int8_quant(x):
            gamma = jnp.max(jnp.abs(x), axis=-1, keepdims=True)
            x_q = jnp.clip(jnp.round(x * 127.0 / (gamma + EPS)), -128, 127)
            return x_q * gamma / 127.0

        def bitlinear(x, w, scale):
            w_mean = jnp.mean(jnp.abs(w))
            w_q = jnp.clip(jnp.round(w / (w_mean + EPS)), -1.0, 1.0)
            w_eff = w_q * w_mean * scale
            return jnp.einsum('...i,oi->...o', x, w_eff)
        key = jax.random.key(seed)
        ks = jax.random.split(key, 4)
        H, I = (512, 1376)
        B, S = (2, 256)
        x = jax.random.normal(ks[0], (B, S, H), dtype=jnp.float32)
        w_gate = jax.random.uniform(ks[1], (I, H), jnp.float32, -1.0, 1.0) / np.sqrt(H)
        w_up = jax.random.uniform(ks[2], (I, H), jnp.float32, -1.0, 1.0) / np.sqrt(H)
        w_down = jax.random.uniform(ks[3], (H, I), jnp.float32, -1.0, 1.0) / np.sqrt(I)
        ones = jnp.ones((1,), jnp.float32)
        return {'x': x, 'w_gate': w_gate, 'w_up': w_up, 'w_down': w_down, 's_gate': ones, 's_up': ones, 's_down': ones}
    _L0_ffn_all = _L0_ffn_setup()
    _L0_ffn_in = {k: v for k, v in _L0_ffn_all.items() if k in ('w_gate', 'w_up', 'w_down', 's_gate', 's_up', 's_down')}
    del _L0_ffn_all

    def _L1_xattn_setup():
        import jax, jax.numpy as jnp
        import numpy as np
        DIM = 64
        HEADS = 8
        DIM_HEAD = 64
        HIDDEN = HEADS * DIM_HEAD
        SCALE = DIM_HEAD ** (-0.5)
        key = jax.random.key(seed)
        ks = jax.random.split(key, 9)
        b, n = (8, 512)
        std = 1.0 / np.sqrt(DIM)
        return {'q': jax.random.normal(ks[0], (b, DIM, n), jnp.float32), 'k': jax.random.normal(ks[1], (b, DIM, n), jnp.float32), 'v': jax.random.normal(ks[2], (b, DIM, n), jnp.float32), 'Wq': jax.random.normal(ks[3], (HIDDEN, DIM), jnp.float32) * std, 'Wk': jax.random.normal(ks[4], (HIDDEN, DIM), jnp.float32) * std, 'Wv': jax.random.normal(ks[5], (HIDDEN, DIM), jnp.float32) * std, 'Wo': jax.random.normal(ks[6], (DIM, HIDDEN), jnp.float32) * (1.0 / np.sqrt(HIDDEN)), 'bo': jax.random.normal(ks[7], (DIM,), jnp.float32) * 0.01, 'g': jnp.ones((1, DIM, 1), jnp.float32)}
    _L1_xattn_all = _L1_xattn_setup()
    _L1_xattn_in = {k: v for k, v in _L1_xattn_all.items() if k in ('Wq', 'Wk', 'Wv', 'Wo', 'bo', 'g')}
    del _L1_xattn_all

    def _L1_ffn_setup():
        import jax, jax.numpy as jnp
        import numpy as np
        NUM_EXPERTS = 8
        RANK = 32
        ALPHA = 16.0
        TOP_K = 2
        TEMPERATURE = 1.0
        GAMMA = 0.5
        SOFT_TOPK_TEMP = 0.5
        N_GRAM = 2
        EPS = 1e-06
        key = jax.random.key(seed)
        ks = jax.random.split(key, 6)
        d_in, d_out = (512, 512)
        Bsz, T = (4, 256)
        x = jax.random.normal(ks[0], (Bsz, T, d_in), dtype=jnp.float32)
        W = jax.random.normal(ks[1], (d_out, d_in), dtype=jnp.float32) / np.sqrt(d_in)
        b = jax.random.normal(ks[2], (d_out,), dtype=jnp.float32) * 0.01
        A = jax.random.normal(ks[3], (d_in, RANK), dtype=jnp.float32) / np.sqrt(d_in)
        Bmat = jax.random.normal(ks[4], (RANK, d_out), dtype=jnp.float32) * 0.01
        LiMEs = jax.random.normal(ks[5], (NUM_EXPERTS, RANK), dtype=jnp.float32) * 0.1
        return {'x': x, 'W': W, 'b': b, 'A': A, 'Bmat': Bmat, 'LiMEs': LiMEs}
    _L1_ffn_all = _L1_ffn_setup()
    _L1_ffn_in = {k: v for k, v in _L1_ffn_all.items() if k in ('W', 'b', 'A', 'Bmat', 'LiMEs')}
    del _L1_ffn_all
    return {'x': x, 'ctx_4096': ctx_4096, 'L0_xattn_Wq': _L0_xattn_in['Wq'], 'L0_xattn_bq': _L0_xattn_in['bq'], 'L0_xattn_Wk': _L0_xattn_in['Wk'], 'L0_xattn_bk': _L0_xattn_in['bk'], 'L0_xattn_Wv': _L0_xattn_in['Wv'], 'L0_xattn_bv': _L0_xattn_in['bv'], 'L0_xattn_Wo': _L0_xattn_in['Wo'], 'L0_xattn_bo': _L0_xattn_in['bo'], 'L0_ffn_w_gate': _L0_ffn_in['w_gate'], 'L0_ffn_w_up': _L0_ffn_in['w_up'], 'L0_ffn_w_down': _L0_ffn_in['w_down'], 'L0_ffn_s_gate': _L0_ffn_in['s_gate'], 'L0_ffn_s_up': _L0_ffn_in['s_up'], 'L0_ffn_s_down': _L0_ffn_in['s_down'], 'L1_xattn_Wq': _L1_xattn_in['Wq'], 'L1_xattn_Wk': _L1_xattn_in['Wk'], 'L1_xattn_Wv': _L1_xattn_in['Wv'], 'L1_xattn_Wo': _L1_xattn_in['Wo'], 'L1_xattn_bo': _L1_xattn_in['bo'], 'L1_xattn_g': _L1_xattn_in['g'], 'L1_ffn_W': _L1_ffn_in['W'], 'L1_ffn_b': _L1_ffn_in['b'], 'L1_ffn_A': _L1_ffn_in['A'], 'L1_ffn_Bmat': _L1_ffn_in['Bmat'], 'L1_ffn_LiMEs': _L1_ffn_in['LiMEs']}

def reference(x, ctx_4096, L0_xattn_Wq, L0_xattn_bq, L0_xattn_Wk, L0_xattn_bk, L0_xattn_Wv, L0_xattn_bv, L0_xattn_Wo, L0_xattn_bo, L0_ffn_w_gate, L0_ffn_w_up, L0_ffn_w_down, L0_ffn_s_gate, L0_ffn_s_up, L0_ffn_s_down, L1_xattn_Wq, L1_xattn_Wk, L1_xattn_Wv, L1_xattn_Wo, L1_xattn_bo, L1_xattn_g, L1_ffn_W, L1_ffn_b, L1_ffn_A, L1_ffn_Bmat, L1_ffn_LiMEs):
    import jax
    import jax.numpy as jnp

    def _L0_xattn_ref(x_query, x_key, x_value, Wq, bq, Wk, bk, Wv, bv, Wo, bo):
        import jax, jax.numpy as jnp
        import numpy as np
        NUM_HEADS = 8

        def _proj(W, b, x):
            return jnp.einsum('oi,bil->bol', W, x) + b[:, None]
        B, D, L = x_query.shape
        h = NUM_HEADS
        Lh = L // h
        q = _proj(Wq, bq, x_query)
        k = _proj(Wk, bk, x_key)
        v = _proj(Wv, bv, x_value)
        qh = q.reshape(B, D, h, Lh).transpose(2, 0, 1, 3)
        kh = k.reshape(B, D, h, Lh).transpose(2, 0, 1, 3)
        vh = v.reshape(B, D, h, Lh).transpose(2, 0, 1, 3)
        scale = 1.0 / jnp.sqrt(jnp.asarray(Lh, x_query.dtype))
        scores = jnp.einsum('hbdk,hbek->hbde', qh, kh) * scale
        p = jax.nn.softmax(scores, axis=-1)
        xh = jnp.einsum('hbde,hbek->hbdk', p, vh)
        x = xh.transpose(1, 2, 0, 3).reshape(B, D, L)
        return _proj(Wo, bo, x)

    def _L0_ffn_ref(x, w_gate, w_up, w_down, s_gate, s_up, s_down):
        import jax, jax.numpy as jnp
        import numpy as np
        import math
        SQRT7 = math.sqrt(7.0)
        EPS = 1e-05

        def int4_quant(x):
            beta = jnp.mean(jnp.abs(x), axis=-1, keepdims=True)
            x_q = jnp.clip(jnp.round(x * SQRT7 / (beta + EPS)), -8, 7)
            return x_q * (beta * SQRT7) / SQRT7

        def int8_quant(x):
            gamma = jnp.max(jnp.abs(x), axis=-1, keepdims=True)
            x_q = jnp.clip(jnp.round(x * 127.0 / (gamma + EPS)), -128, 127)
            return x_q * gamma / 127.0

        def bitlinear(x, w, scale):
            w_mean = jnp.mean(jnp.abs(w))
            w_q = jnp.clip(jnp.round(w / (w_mean + EPS)), -1.0, 1.0)
            w_eff = w_q * w_mean * scale
            return jnp.einsum('...i,oi->...o', x, w_eff)
        xq = int4_quant(x)
        gate = bitlinear(xq, w_gate, s_gate)
        up = bitlinear(xq, w_up, s_up)
        gate = jnp.square(jax.nn.relu(gate))
        inter = int8_quant(up * gate)
        return bitlinear(inter, w_down, s_down)

    def _L1_xattn_ref(q, k, v, Wq, Wk, Wv, Wo, bo, g):
        import jax, jax.numpy as jnp
        import numpy as np
        DIM = 64
        HEADS = 8
        DIM_HEAD = 64
        HIDDEN = HEADS * DIM_HEAD
        SCALE = DIM_HEAD ** (-0.5)
        b = q.shape[0]
        qh = jnp.einsum('bcn,oc->bon', q, Wq).reshape(b, HEADS, DIM_HEAD, -1)
        kh = jnp.einsum('bcn,oc->bon', k, Wk).reshape(b, HEADS, DIM_HEAD, -1)
        vh = jnp.einsum('bcn,oc->bon', v, Wv).reshape(b, HEADS, DIM_HEAD, -1)
        qh = jax.nn.softmax(qh, axis=-2) * SCALE
        kh = jax.nn.softmax(kh, axis=-1)
        context = jnp.einsum('bhdn,bhen->bhde', kh, vh)
        out = jnp.einsum('bhde,bhdn->bhen', context, qh)
        out = out.reshape(b, HIDDEN, -1)
        out = jnp.einsum('bcn,oc->bon', out, Wo) + bo[None, :, None]
        norm = jnp.maximum(jnp.sqrt(jnp.sum(out * out, axis=1, keepdims=True)), 1e-12)
        return out / norm * g * np.sqrt(DIM)

    def _L1_ffn_ref(x, W, b, A, Bmat, LiMEs):
        import jax, jax.numpy as jnp
        import numpy as np
        NUM_EXPERTS = 8
        RANK = 32
        ALPHA = 16.0
        TOP_K = 2
        TEMPERATURE = 1.0
        GAMMA = 0.5
        SOFT_TOPK_TEMP = 0.5
        N_GRAM = 2
        EPS = 1e-06
        Bsz, T, d_in = x.shape
        E = LiMEs.shape[0]
        scaling = ALPHA / RANK
        H = jnp.einsum('btd,od->bto', x, W) + b
        z = jnp.einsum('btd,dr->btr', x, A)
        anchors = jnp.arange(N_GRAM - 1, T, N_GRAM)
        H_slice = H[:, anchors, :E]
        delta_slice = jnp.einsum('bar,er->bae', z[:, anchors], LiMEs)
        H_scale = jnp.maximum(jnp.max(jnp.abs(H_slice)), EPS)
        d_scale = jnp.maximum(jnp.max(jnp.abs(delta_slice)), EPS)
        logits = ((1.0 - GAMMA) * (H_slice / H_scale) + GAMMA * (delta_slice / d_scale)) / TEMPERATURE
        probs = jax.nn.softmax(logits, axis=-1)
        topk_vals, _ = jax.lax.top_k(probs, TOP_K)
        thresh = topk_vals[..., -1:]
        mask = jax.nn.sigmoid((probs - thresh) / SOFT_TOPK_TEMP)
        weights = probs * mask
        weights = weights / (jnp.sum(weights, axis=-1, keepdims=True) + 1e-09)
        weights_full = jnp.repeat(weights, N_GRAM, axis=1)
        p_mix = jnp.einsum('bte,er->btr', weights_full, LiMEs)
        delta = jnp.einsum('btr,ro->bto', z * p_mix, Bmat) * scaling
        return H + delta
    x = x + _L0_xattn_ref(_layernorm(x, axis=-1), ctx_4096, ctx_4096, L0_xattn_Wq, L0_xattn_bq, L0_xattn_Wk, L0_xattn_bk, L0_xattn_Wv, L0_xattn_bv, L0_xattn_Wo, L0_xattn_bo)
    x = x + _L0_ffn_ref(_layernorm(x, axis=-1), L0_ffn_w_gate, L0_ffn_w_up, L0_ffn_w_down, L0_ffn_s_gate, L0_ffn_s_up, L0_ffn_s_down)
    x = x + _L1_xattn_ref(_layernorm(x, axis=-1), ctx_4096, ctx_4096, L1_xattn_Wq, L1_xattn_Wk, L1_xattn_Wv, L1_xattn_Wo, L1_xattn_bo, L1_xattn_g)
    x = x + _L1_ffn_ref(_layernorm(x, axis=-1), L1_ffn_W, L1_ffn_b, L1_ffn_A, L1_ffn_Bmat, L1_ffn_LiMEs)
    return x

_drawn_inputs = setup_inputs


def setup_inputs(seed=0):
    import zlib

    import numpy as np

    out = dict(_drawn_inputs(seed))
    spreads = {'L1_xattn_g': (1.0, 0.535)}
    factors = {'L0_xattn_bq': 2.692,
     'L0_xattn_bv': 3.089,
     'L0_xattn_bo': 28.997,
     'L1_ffn_b': 32.236,
     'L1_ffn_A': 8.0,
     'L1_ffn_Bmat': 8.0,
     'L1_ffn_LiMEs': 8.0}
    for name, (base, spread) in spreads.items():
        noise = np.random.default_rng([zlib.crc32(name.encode()), seed]).standard_normal(out[name].shape)
        drawn = base * np.exp(spread * noise) if base else spread * noise
        out[name] = jnp.asarray(drawn.astype(out[name].dtype))
    for name, factor in factors.items():
        out[name] = (out[name] * factor).astype(out[name].dtype)
    return out
```

```python
import math
from contextlib import ExitStack

import concourse.bass as bass
from concourse import mybir
from concourse.alu_op_type import AluOpType as ALU

F32, F16, BF16 = mybir.dt.float32, mybir.dt.float16, mybir.dt.bfloat16
ACT = mybir.ActivationFunctionType
X = mybir.AxisListType.X

P = 128
D = 64
L = 512
HEADS = L // D
NC = L // P
BATCHES = 32
TILES = BATCHES * D // P
HALF = (slice(0, D), slice(D, P))
FF = 1376
FFC = (FF + P - 1) // P
FFB = [(a, min(a + 512, FF)) for a in range(0, FF, 512)]
RANK, EXPERTS = 32, 8
EPS = 1e-5
ROUND = 12582912.0
SQRT7 = math.sqrt(7.0)
LN_SCALE = 24


def chunk(ap, c, n=P):
    return ap[:, c * n:(c + 1) * n]


def exists(i, n):
    return not isinstance(i, int) or 0 <= i < n


def wait(eng, sem, value):
    if not isinstance(value, int) or value > 0:
        eng.wait_ge(sem, value)


def hold(eng, sem, value, passed):
    if not isinstance(value, int) or value > 0:
        eng.wait_ge(sem, value)
        eng.sem_inc(passed, 1)


def sweep(eng, step, n, tail):
    step(0, 0, 0)
    step(1, 1, 0)
    with eng.Fori(1, n // 2 - 1) as j:
        step(2 * j, 0, j)
        step(2 * j + 1, 1, j)
    for i in range(n - 2, n + tail):
        step(i, i % 2, i // 2)


class Shared:
    pass


class Scope:

    def __init__(self, nc, ctx, tag):
        self.nc, self.ctx, self.tag = nc, ctx, tag

    def sb(self, name, shape, dt=F32):
        return self.ctx.enter_context(self.nc.sbuf_tensor(f"{self.tag}_{name}", shape, dt))

    def ps(self, name, shape, dt=F32):
        return self.ctx.enter_context(self.nc.psum_tensor(f"{self.tag}_{name}", shape, dt))

    def sem(self, name):
        return self.ctx.enter_context(self.nc.semaphore(f"{self.tag}_{name}"))

    def block(self):
        return self.ctx.enter_context(self.nc.Block())


def row_stats(dve, k, t, stats, x_ok, st_ok, ag_ok, mv_ok):
    six, two = stats
    hold(dve, x_ok, t + 1, k.passed)
    dve.bn_stats(six[:, :], k.x[:, t, :]).then_inc(st_ok, 1)
    hold(dve, st_ok, t + 1, k.passed)
    hold(dve, mv_ok, t, k.passed)
    dve.bn_aggr(two[:, :], six[:, :]).then_inc(ag_ok, 1)
    hold(dve, ag_ok, t + 1, k.passed)
    dve.tensor_copy(k.mv[:, t, :], two[:, :]).then_inc(mv_ok, 1)


def row_rstd(k, n, start):
    r = k.rs

    def on_vector(dve):
        start(dve)
        dve.tensor_scalar(r.v[:, :], k.mv[:, :, 1], EPS, None, ALU.add).then_inc(r.v_ok, 1)
        dve.wait_ge(r.y_ok, n + 1)
        dve.tensor_tensor(r.t[:, :], r.y[:, :], r.y[:, :], ALU.mult).then_inc(r.t_ok, 1)
        dve.wait_ge(r.t_ok, 3 * n + 1)
        dve.tensor_tensor(r.t[:, :], r.t[:, :], r.v[:, :], ALU.mult).then_inc(r.t_ok, 1)
        dve.wait_ge(r.t_ok, 3 * n + 2)
        dve.tensor_scalar(r.t[:, :], r.t[:, :], -0.5, 1.5, ALU.mult, ALU.add).then_inc(r.t_ok, 1)
        dve.wait_ge(r.t_ok, 3 * n + 3)
        dve.tensor_tensor(k.rstd[:, :], r.y[:, :], r.t[:, :], ALU.mult).then_inc(r.rstd_ok, 1)
        dve.wait_ge(r.rstd_ok, n + 1)

    def on_scalar(act):
        act.wait_ge(r.v_ok, n + 1)
        act.activation(r.ln[:, :], r.v[:, :], ACT.Ln).then_inc(r.ln_ok, 1)
        act.wait_ge(r.ln_ok, n + 1)
        act.activation(r.y[:, :], r.ln[:, :], ACT.Exp, scale=-0.5).then_inc(r.y_ok, 1)

    return on_vector, on_scalar


def setup(nc, a, k):
    with ExitStack() as ctx:
        s = Scope(nc, ctx, "setup")
        wbd = s.sb("wbd", [P, 4, P])
        wdup = s.sb("wdup", [P, 2, NC, P])
        wo1 = s.sb("wo1", [D, L])
        wv1 = s.sb("wv1", [P, NC, D])
        wo1T = s.sb("wo1T", [P, NC, D])
        w_nat = s.sb("w_nat", [P, NC, L])
        brow = s.sb("brow", [1, 3, L])
        bsmall = s.sb("bsmall", [1, 2, D])
        part = s.sb("part", [1, 3, L], BF16)
        rest = s.sb("rest", [1, 3, L])
        bm = s.sb("bm", [P, L])
        stats = s.sb("stats", [P, TILES, 6])
        ps = [s.ps(f"ps{i}", [P, 512]) for i in range(8)]

        zero_ok = s.sem("zero_ok")
        ident_ok = s.sem("ident_ok")
        const_ok = s.sem("const_ok")
        x_in = [s.sem(f"x_in{i}") for i in range(4)]
        w_in = s.sem("w_in")
        stat_ok = s.sem("stat_ok")
        mv_ok = s.sem("mv_ok")
        tr = s.sem("tr")
        out0 = s.sem("out0")
        out1 = s.sem("out1")
        row_ok = s.sem("row_ok")
        vec_x, act_x = row_rstd(k, 0, lambda e: e.wait_ge(mv_ok, TILES))
        block = s.block()
        loads = []

        @block.sync
        def _(sp):
            xv = a["x"].rearrange("(t b) d l -> (b d) t l", b=2)
            g = TILES // 4
            for i in range(4):
                sp.dma_start(k.x[:, g * i:g * i + g, :], xv[:, g * i:g * i + g, :]).then_inc(x_in[i], 16)
            sp.wait_ge(zero_ok, 3)
            for n, w in enumerate((a["Wq0"], a["Wk0"], a["Wv0"], a["Wo0"])):
                for h in range(2):
                    sp.dma_start(wbd[HALF[h], n, h * D:(h + 1) * D], w).then_inc(w_in, 16)
                    loads.append(1)

        @block.scalar
        def _(act):
            def load(dst, src):
                act.dma_start(dst, src).then_inc(w_in, 16)
                loads.append(1)

            load(bsmall[0:1, 0, :], a["bq0"].unsqueeze(0))
            load(bsmall[0:1, 1, :], a["bk0"].unsqueeze(0))
            load(brow[0:1, 2, :], a["b1"].unsqueeze(0))
            for h in range(2):
                load(k.bv2[HALF[h], :], a["bv0"].unsqueeze(1))
                load(k.bo2[HALF[h], :], a["bo0"].unsqueeze(1))
                load(k.bo1[HALF[h], :], a["bo1"].unsqueeze(1))
                load(k.g8[HALF[h], :], a["g1"].rearrange("a d b -> (a d) b"))
            for n, w in enumerate((a["Wq1"], a["Wk1"])):
                for h in range(2):
                    load(wdup[:, n, :, h * D:(h + 1) * D], w.rearrange("(c p) d -> p c d", p=P))
            load(wv1[:, :, :], a["Wv1"].rearrange("(c p) d -> p c d", p=P))
            load(wo1[:, :], a["Wo1"])
            load(w_nat[:, :, :], a["W1"].rearrange("(c p) d -> p c d", p=P))
            for q in range(4):
                load(k.A4[:, :, q * RANK:(q + 1) * RANK], a["A1"].rearrange("(c p) r -> p c r", p=P))
                load(bm[q * RANK:(q + 1) * RANK, :], a["Bm1"])
                load(k.limes4[q * RANK:q * RANK + EXPERTS, :, :],
                     a["Li1"].unsqueeze(1).broadcast_to([EXPERTS, 4, RANK]))
            with nc.allow_non_contiguous_dma(reason="256 numbers"):
                load(k.limesT[:, :], a["Li1"].rearrange("e r -> r e"))
            for n, w in enumerate((a["sg"], a["su"], a["sd"])):
                load(k.ffs[:, n:n + 1], w.unsqueeze(0).broadcast_to([P, 1]))
            n_in = 16 * (8 + len(loads))
            for n, w in enumerate((k.wq_hi, k.wk_hi)):
                act.wait_ge(tr, 3 + n)
                act.activation(w[:, :], ps[2 + n][:, :], ACT.Copy).then_inc(out1, 1)
            act_x(act)
            for i in range(NC):
                act.wait_ge(tr, 6 + i)
                act.activation(k.WT[:, i, :], ps[(5, 6, 7, 0)[i]][:, :], ACT.Copy).then_inc(out1, 1)

        n_in = 16 * (8 + 3 + 8 + 4 + 3 + 12 + 1 + 3)

        @block.gpsimd
        def _(pool):
            pool.memset(k.ident[:, :], 0.0).then_inc(zero_ok, 1)
            pool.memset(wbd[:, :, :], 0.0).then_inc(zero_ok, 1)
            pool.memset(k.ind[:, :], 0.0).then_inc(zero_ok, 1)
            pool.wait_ge(zero_ok, 3)
            pool.affine_select(out=k.ident[:, :], in_=k.ident[:, :], compare_op=ALU.not_equal, fill=1.0, base=0,
                               pattern=[[-1, P]], channel_multiplier=1).then_inc(ident_ok, 1)
            iv = k.ind[0:32, :].rearrange("p (h d) -> p h d", h=HEADS)
            pool.affine_select(out=iv, in_=iv, compare_op=ALU.not_equal, fill=1.0, base=0,
                               pattern=[[-1, HEADS], [0, D]], channel_multiplier=1).then_inc(ident_ok, 1)

        @block.vector
        def _(dve):
            for buf, value in ((k.ones, 1.0), (k.bias_rows[0], 0.0), (k.bias_rows[1], 0.0), (k.bias_rows[2], 0.0),
                               (k.blk, 0.0), (k.m_round, ROUND), (k.m_minus, -ROUND), (k.half_ln, 0.5 * LN_SCALE * math.log(2.0)),
                               (k.wv_wo, 0.0)):
                ap = buf[:, :] if len(buf.shape) == 2 else buf[:, :, :]
                dve.memset(ap, value).then_inc(const_ok, 1)
            dve.wait_ge(const_ok, 9)
            for h in range(2):
                dve.memset(k.blk[HALF[h], h * D:(h + 1) * D], 1.0).then_inc(const_ok, 1)
            dve.memset(k.wv_wo[D:D + 1, :, D:D + 1], 1.0).then_inc(const_ok, 1)
            dve.wait_ge(ident_ok, 2)
            dve.tensor_copy(k.ident16[:, :], k.ident[:, :]).then_inc(const_ok, 1)
            for g in (1, 2):
                dve.tensor_copy(k.ind[32 * g:32 * g + 32, :], k.ind[0:32, :]).then_inc(const_ok, 1)
            dve.tensor_reduce(k.odd[:, :], k.ident[:, :].rearrange("p (n two) -> p two n", two=2)[:, 1, :], X,
                              ALU.add).then_inc(const_ok, 1)
            for t in range(TILES):
                if t % 4 == 0:
                    dve.wait_ge(x_in[t // 4], 16)
                dve.bn_stats(stats[:, t, :], k.x[:, t, :]).then_inc(stat_ok, 1)
            for t in range(TILES):
                dve.wait_ge(stat_ok, t + 1)
                dve.bn_aggr(k.mv[:, t, :], stats[:, t, :]).then_inc(mv_ok, 1)
            vec_x(dve)
            dve.wait_ge(w_in, n_in)
            dve.tensor_scalar(k.g8[:, :], k.g8[:, :], math.sqrt(D), None, ALU.mult).then_inc(row_ok, 1)
            for n in range(2):
                dve.tensor_copy(brow[0:1, n, :].rearrange("p (c d) -> p c d", d=D),
                                bsmall[0:1, n, :].unsqueeze(1).broadcast_to([1, L // D, D])).then_inc(row_ok, 1)
            dve.wait_ge(row_ok, 3)
            dve.tensor_copy(part[:, :, :], brow[:, :, :]).then_inc(row_ok, 1)
            dve.wait_ge(row_ok, 4)
            dve.tensor_tensor(rest[:, :, :], brow[:, :, :], part[:, :, :], ALU.subtract).then_inc(row_ok, 1)
            for n in range(3):
                dve.tensor_copy(k.bias_rows[n][0:1, :], part[0:1, n, :]).then_inc(row_ok, 1)
            dve.wait_ge(row_ok, 8)
            dve.tensor_copy(part[:, :, :], rest[:, :, :]).then_inc(row_ok, 1)
            dve.wait_ge(row_ok, 9)
            for n in range(3):
                dve.tensor_copy(k.bias_rows[n][32:33, :], part[0:1, n, :]).then_inc(row_ok, 1)
                dve.tensor_tensor(k.bias_rows[n][64:65, :], rest[0:1, n, :], part[0:1, n, :],
                                  ALU.subtract).then_inc(row_ok, 1)
            dve.tensor_scalar(bm[:, :], bm[:, :], 16.0 / RANK, None, ALU.mult).then_inc(row_ok, 1)
            dve.wait_ge(row_ok, 16)
            dve.tensor_copy(k.bm_parts[:, :], bm[:, :]).then_inc(row_ok, 1)
            dve.wait_ge(row_ok, 17)
            dve.tensor_tensor(k.bm_parts[D:P, :], bm[D:P, :], k.bm_parts[D:P, :], ALU.subtract).then_inc(row_ok, 1)
            dve.wait_ge(tr, 1)
            dve.tensor_copy(k.wT0[:, :, :], ps[0][:, :].rearrange("p (n m) -> p n m", n=4)).then_inc(out0, 1)
            dve.wait_ge(tr, 2)
            dve.tensor_copy(wo1T[:, :, :], ps[1][:, 0:NC * D].rearrange("p (n m) -> p n m", n=NC)).then_inc(out0, 1)
            for n, (hi, lo) in enumerate(((k.wq_hi, k.wq_lo), (k.wk_hi, k.wk_lo))):
                dve.wait_ge(out1, n + 1)
                dve.tensor_tensor(lo[:, :], ps[2 + n][:, :], hi[:, :], ALU.subtract).then_inc(out0, 1)
            dve.wait_ge(tr, 5)
            for r in range(2):
                dve.tensor_scalar(k.wv_wo[0:D, r:HEADS:2, 0:D],
                                  ps[(4, 1)[r]][0:D, :].rearrange("p (h m) -> p h m", h=HEADS)[:, r:HEADS:2, :],
                                  D ** -0.5, None, ALU.mult).then_inc(out0, 1)

        @block.tensor
        def _(pe):
            pe.wait_ge(ident_ok, 1)
            pe.wait_ge(w_in, n_in)
            for n in range(4):
                mm = pe.transpose(chunk(ps[0], n), wbd[:, n, :], k.ident[:, :])
            mm.then_inc(tr, 1)
            for c in range(NC):
                mm = pe.transpose(ps[1][:, c * D:(c + 1) * D], chunk(wo1, c), k.ident[0:D, 0:D])
            mm.then_inc(tr, 1)
            for n in range(2):
                for c in range(NC):
                    mm = pe.transpose(chunk(ps[2 + n], c), wdup[:, n, c, :], k.ident[:, :])
                mm.then_inc(tr, 1)
            pe.wait_ge(out0, 2)
            for h in range(HEADS):
                r = HALF[h % 2]
                mm = pe.matmul(ps[(4, 1)[h % 2]][0:D, h * D:(h + 1) * D], wv1[r, h // 2, :], wo1T[r, h // 2, :],
                               start=True, stop=True)
            mm.then_inc(tr, 1)
            for i in range(NC):
                if i == 3:
                    pe.wait_ge(out0, 1)
                for o in range(NC):
                    mm = pe.transpose(chunk(ps[(5, 6, 7, 0)[i]], o), w_nat[:, o, i * P:(i + 1) * P], k.ident[:, :])
                mm.then_inc(tr, 1)


def attention0(nc, a, k):
    with ExitStack() as ctx:
        s = Scope(nc, ctx, "att0")
        ctx_n = [s.sb(f"ctx_n{p}", [P, L]) for p in range(2)]
        ctx_h = [s.sb(f"ctx_h{p}", [P, 2, NC, D]) for p in range(2)]
        xn = [s.sb(f"xn{p}", [P, L]) for p in range(2)]
        q_t = s.sb("q_t", [P, L])
        k_t = s.sb("k_t", [P, 2, NC, 2, D])
        v_h = [s.sb(f"v_h{p}", [P, 2, NC, 2, D]) for p in range(2)]
        mx = s.sb("mx", [P, HEADS])
        sh = s.sb("sh", [P, L])
        ex = s.sb("ex", [P, L])
        sm = s.sb("sm", [P, HEADS])
        rs = s.sb("rs", [P, HEADS])
        pn = s.sb("pn", [P, L])
        wp = s.sb("wp", [P, L])
        dump = s.sb("dump", [P, L])
        stats = (s.sb("stats", [P, 6]), s.sb("mean_var", [P, 2]))
        ag_ok = s.sem("ag_ok")
        psQ, psK, psV, psS, psW, psO = (s.ps("ps" + n, [P, 512]) for n in "QKVSWO")
        (zero_ok, xn_ok, q_ps, k_ps, v_ps, s_ps, w_ps, o_ps, q_ok, k_ok, v_ok, mx_ok, sh_ok, ex_ok, sm_ok, rs_ok, pn_ok,
         wp_ok, x_ok, st_ok, mv_ok, ab_ok) = (s.sem(n) for n in (
             "zero_ok xn_ok q_ps k_ps v_ps s_ps w_ps o_ps q_ok k_ok v_ok mx_ok sh_ok ex_ok sm_ok rs_ok pn_ok "
             "wp_ok x_ok st_ok mv_ok ab_ok").split())
        ctx_in = [s.sem(f"ctx_in{p}") for p in range(2)]
        block = s.block()
        nat = a["ctx"].rearrange("(t b) d l -> t (b d) l", b=2)
        par = a["ctx"].rearrange("(t b) d (c r k) -> t r d b c k", b=2, r=2, k=D)

        @block.sync
        def _(sp):
            def step(i, p, j):
                wait(sp, v_ps, i - 1)
                sp.dma_start(ctx_n[p][:, :], nat[i]).then_inc(ctx_in[p], 16)
                for r in range(2):
                    for b in range(2):
                        sp.dma_start(ctx_h[p][HALF[r], b], par[i, r, :, b]).then_inc(ctx_in[p], 16)

            sweep(sp, step, TILES, 0)

        @block.gpsimd
        def _(pool):
            for buf in (k_t, v_h[0], v_h[1]):
                pool.memset(buf[:, :, :, :, :], 0.0).then_inc(zero_ok, 1)

            def step(i, p, j):
                pool.wait_ge(rs_ok, i + 1)
                pool.tensor_tensor(pn[:, :].rearrange("p (h e) -> p h e", h=HEADS),
                                   ex[:, :].rearrange("p (h e) -> p h e", h=HEADS),
                                   rs[:, :].unsqueeze(2).broadcast_to([P, HEADS, D]), ALU.mult).then_inc(pn_ok, 1)

            sweep(pool, step, TILES, 0)

        @block.vector
        def _(dve):
            def normed(i, p):
                dve.tensor_scalar(xn[p][:, :], k.x[:, i, :], k.mv[:, i, 0:1], k.rstd[:, bass.ds(i, 1)], ALU.subtract,
                                  ALU.mult).then_inc(xn_ok, 1)

            def step(i, p, j):
                t = i - 1
                if exists(t, TILES):
                    dve.wait_ge(s_ps, t + 1)
                    s3 = psS[:, :].rearrange("p (h e) -> p h e", h=HEADS)
                    dve.tensor_reduce(mx[:, :], s3, X, ALU.max).then_inc(mx_ok, 1)
                    dve.wait_ge(mx_ok, t + 1)
                    dve.tensor_tensor(sh[:, :].rearrange("p (h e) -> p h e", h=HEADS), s3,
                                      mx[:, :].unsqueeze(2).broadcast_to([P, HEADS, D]), ALU.subtract).then_inc(sh_ok, 1)
                if exists(i, TILES):
                    dve.wait_ge(k_ps, i + 1)
                    wait(dve, k_ok, 2 * i)
                    dve.wait_ge(zero_ok, 3)
                    for r in range(2):
                        dve.tensor_copy(k_t[HALF[r], :, :, r, :],
                                        psK[HALF[r], :].rearrange("p (c b e) -> p b c e", b=2, e=D)).then_inc(k_ok, 1)
                if exists(t, TILES):
                    dve.wait_ge(ex_ok, t + 1)
                    dve.tensor_reduce(sm[:, :], ex[:, :].rearrange("p (h e) -> p h e", h=HEADS), X,
                                      ALU.add).then_inc(sm_ok, 1)
                    dve.wait_ge(sm_ok, t + 1)
                    dve.reciprocal(rs[:, :], sm[:, :]).then_inc(rs_ok, 1)
                if exists(i + 1, TILES):
                    normed(i + 1, 1 - p)
                if exists(t, TILES):
                    dve.wait_ge(o_ps, t + 1)
                    dve.scalar_tensor_tensor(out=k.x[:, t, :], in0=psO[:, :], scalar=k.bo2[:, :], in1=k.x[:, t, :],
                                             op0=ALU.add, op1=ALU.add).then_inc(x_ok, 1)
                    row_stats(dve, k, t, stats, x_ok, st_ok, ag_ok, mv_ok)

            normed(0, 0)
            sweep(dve, step, TILES, 1)

        @block.scalar
        def _(act):
            def step(i, p, j):
                t = i - 1
                if exists(t, TILES):
                    act.wait_ge(sh_ok, t + 1)
                    wait(act, pn_ok, t)
                    act.activation(ex[:, :], sh[:, :], ACT.Exp, scale=D ** -0.5).then_inc(ex_ok, 1)
                if exists(i, TILES):
                    act.wait_ge(q_ps, i + 1)
                    act.activation(q_t[:, :], psQ[:, :], ACT.Copy).then_inc(q_ok, 1)
                    act.wait_ge(v_ps, i + 1)
                    act.wait_ge(zero_ok, 3)
                    for r in range(2):
                        act.activation(v_h[p][HALF[r], :, :, r, :],
                                       psV[HALF[r], :].rearrange("p (b c e) -> p b c e", b=2, e=D), ACT.Identity,
                                       bias=k.bv2[HALF[r], :]).then_inc(v_ok, 1)
                if exists(t, TILES):
                    act.wait_ge(w_ps, t + 1)
                    act.activation(wp[:, :], psW[:, :], ACT.Copy).then_inc(wp_ok, 1)
                    act.wait_ge(mv_ok, t + 1)
                    hold(act, ab_ok, t, k.passed)
                    act.activation(dump[:, :], k.x[:, t, :], ACT.Abs, scale=-1.0, bias=k.mv[:, t, 0:1],
                                   accum_out=k.xabs[:, bass.ds(t, 1)]).then_inc(ab_ok, 1)

            sweep(act, step, TILES, 1)

        @block.tensor
        def _(pe):
            def step(i, p, j):
                t = i - 1
                if exists(i, TILES):
                    pe.wait_ge(xn_ok, i + 1)
                    wait(pe, q_ok, i)
                    pe.matmul(psQ[:, :], k.ones[:, :], k.bias_rows[0][:, :], start=True, stop=True)
                    for c in range(NC):
                        mm = pe.matmul(chunk(psQ, c), chunk(xn[p], c), k.wT0[:, 0, :], start=False, stop=True,
                                       skip_group_check=True)
                    mm.then_inc(q_ps, 1)
                    pe.wait_ge(ctx_in[p], 80 * j + 80)
                    wait(pe, k_ok, 2 * i)
                    pe.matmul(psK[:, :], k.ones[:, :], k.bias_rows[1][:, :], start=True, stop=True)
                    for c in range(NC):
                        mm = pe.matmul(chunk(psK, c), chunk(ctx_n[p], c), k.wT0[:, 1, :], start=False,
                                       stop=True, skip_group_check=True)
                    mm.then_inc(k_ps, 1)
                    wait(pe, v_ok, 2 * i)
                    pe.matmul(psV[:, :], k.wT0[:, 2, :], ctx_h[p][:, :, :, :].rearrange("p b c k -> p (b c k)"),
                              start=True, stop=True).then_inc(v_ps, 1)
                if exists(t, TILES):
                    pe.wait_ge(pn_ok, t + 1)
                    for c in range(NC):
                        mm = pe.matmul(chunk(psW, c), chunk(pn, c), k.wT0[:, 3, :], start=True, stop=True)
                    mm.then_inc(w_ps, 1)
                if exists(i, TILES):
                    pe.wait_ge(q_ok, i + 1)
                    pe.wait_ge(k_ok, 2 * i + 2)
                    wait(pe, sh_ok, i)
                    for c in range(NC):
                        for b in range(2):
                            mm = pe.matmul(psS[HALF[b], c * P:(c + 1) * P], q_t[:, c * P + b * D:c * P + b * D + D],
                                           k_t[:, b, c, :, :], start=True, stop=True)
                    mm.then_inc(s_ps, 1)
                if exists(t, TILES):
                    pe.wait_ge(wp_ok, t + 1)
                    pe.wait_ge(v_ok, 2 * t + 2)
                    wait(pe, x_ok, t)
                    for c in range(NC):
                        for b in range(2):
                            mm = pe.matmul(psO[HALF[b], c * P:(c + 1) * P], wp[:, c * P + b * D:c * P + b * D + D],
                                           v_h[1 - p][:, b, c, :, :], start=True, stop=True)
                    mm.then_inc(o_ps, 1)

            sweep(pe, step, TILES, 1)


def ternary_weights(nc, a, k, raw, raw_in):
    with ExitStack() as ctx:
        s = Scope(nc, ctx, "tern")
        dump = s.sb("dumpw", [P, FFC * L], BF16)
        asum = s.sb("asum", [P, 3])
        mean = s.sb("mean", [P, 3])
        den = s.sb("den", [P, 3])
        inv = s.sb("inv", [P, 3])
        t0 = s.sb("t0", [P, TILES])
        beta = s.sb("beta", [P, TILES])
        ones32 = s.sb("ones32", [P, P])
        psM = s.ps("psM", [P, 512])
        psT = [s.ps(f"psT{i}", [P, 512]) for i in range(6)]
        (abs_ok, pad_ok, sum_ps, mean_ok, den_ok, inv_ok, q1_ok, q2_ok, t_ps, ev_v, ev_a, sc_ok) = (s.sem(n) for n in (
            "abs_ok pad_ok sum_ps mean_ok den_ok inv_ok q1_ok q2_ok t_ps ev_v ev_a sc_ok").split())
        vec_x, act_x = row_rstd(k, 1, lambda e: None)
        block = s.block()
        flat = [raw[0][:, :, :].rearrange("p a b -> p (a b)"), raw[1][:, :, :].rearrange("p a b -> p (a b)"),
                raw[2][:, :, :].rearrange("p a b -> p (a b)")]
        groups = []
        for n, dst in ((0, k.wgT), (1, k.wuT)):
            for c in range(NC):
                for f in range(0, FFC, 4):
                    js = range(f, min(f + 4, FFC))
                    blocks = [(raw[n][0:min(P, FF - j * P), j, c * P:(c + 1) * P], (j - f) * P, min(P, FF - j * P))
                              for j in js]
                    width = min(FF, (f + 4) * P) - f * P
                    groups.append((n, blocks, P, dst[:, c, f * P:f * P + width], width))
        for j in range(FFC):
            rows = min(P, FF - j * P)
            blocks = [(raw[2][:, c, j * P:j * P + rows], c * P, P) for c in range(NC)]
            groups.append((2, blocks, rows, k.wdT[0:rows, j, :], L))

        @block.gpsimd
        def _(pool):
            for n in range(3):
                pool.wait_ge(inv_ok, 1)
                pool.tensor_scalar(flat[n], flat[n], inv[:, n:n + 1], ROUND, ALU.mult, ALU.add).then_inc(q1_ok, 1)

        @block.scalar
        def _(act):
            act.wait_ge(pad_ok, 2)
            for n in range(3):
                act.wait_ge(raw_in[n], 32 if n < 2 else 16)
                wait(act, abs_ok, n)
                act.activation(dump[:, 0:flat[n].shape[1]], flat[n], ACT.Abs, accum_out=asum[:, n:n + 1]).then_inc(abs_ok, 1)
            act_x(act)
            for g, (n, blocks, rows, dst, width) in enumerate(groups):
                if g % 2:
                    act.wait_ge(t_ps, g + 1)
                    act.activation(dst, psT[g % 6][0:rows, 0:width], ACT.Identity,
                                   bias=k.m_minus[0:rows, :]).then_inc(ev_a, 1)

        @block.tensor
        def _(pe):
            pe.wait_ge(abs_ok, 3)
            pe.wait_ge(pad_ok, 3)
            pe.matmul(psM[:, 0:3], ones32[:, :], asum[:, :], start=True, stop=True).then_inc(sum_ps, 1)
            for g, (n, blocks, rows, dst, width) in enumerate(groups):
                pe.wait_ge(q2_ok, n + 1)
                if g >= 6:
                    pe.wait_ge(ev_a if g % 2 else ev_v, (g - 6) // 2 + 1)
                for src, at, wide in blocks:
                    mm = pe.transpose(psT[g % 6][0:rows, at:at + wide], src, k.ident[0:src.shape[0], 0:src.shape[0]])
                mm.then_inc(t_ps, 1)

        @block.vector
        def _(dve):
            for n in range(2):
                dve.memset(raw[n][FF - (FFC - 1) * P:P, FFC - 1, :], 0.0).then_inc(pad_ok, 1)
            dve.memset(ones32[:, :], 1.0).then_inc(pad_ok, 1)
            vec_x(dve)
            dve.wait_ge(sum_ps, 1)
            dve.tensor_scalar(mean[:, :], psM[:, 0:3], 1.0 / (FF * L), None, ALU.mult).then_inc(mean_ok, 1)
            dve.wait_ge(mean_ok, 1)
            dve.tensor_scalar(den[:, :], mean[:, :], EPS, None, ALU.add).then_inc(den_ok, 1)
            dve.wait_ge(den_ok, 1)
            dve.reciprocal(inv[:, :], den[:, :]).then_inc(inv_ok, 1)
            n = [0]

            def link(ins):
                n[0] += 1
                ins.then_inc(sc_ok, 1)
                dve.wait_ge(sc_ok, n[0])

            w = k.ffw
            link(dve.tensor_tensor(w[:, :], mean[:, :], k.ffs[:, :], ALU.mult))
            link(dve.tensor_tensor(t0[:, :], k.xabs[:, :], k.rstd[:, :], ALU.mult))
            link(dve.tensor_scalar(beta[:, :], t0[:, :], 1.0 / L, None, ALU.mult))
            link(dve.tensor_scalar(t0[:, :], beta[:, :], EPS, None, ALU.add))
            link(dve.reciprocal(k.s4[:, :], t0[:, :]))
            link(dve.scalar_tensor_tensor(out=k.s4[:, :], in0=k.s4[:, :], scalar=SQRT7, in1=k.rstd[:, :], op0=ALU.mult,
                                          op1=ALU.mult))
            link(dve.tensor_scalar(k.sg[:, :], beta[:, :], w[:, 0:1], None, ALU.mult))
            link(dve.tensor_scalar(k.su[:, :], beta[:, :], w[:, 1:2], None, ALU.mult))
            link(dve.tensor_scalar(t0[:, :], k.su[:, :], -1.0, None, ALU.mult))
            link(dve.tensor_tensor(k.su_abs[:, :], k.su[:, :], t0[:, :], ALU.max))
            link(dve.tensor_scalar(k.sd[:, :], k.su_abs[:, :], w[:, 2:3], 1.0 / 127.0, ALU.mult, ALU.mult))
            link(dve.tensor_scalar(k.su[:, :], k.su[:, :], 127.0, None, ALU.mult))
            for m in range(3):
                dve.wait_ge(q1_ok, m + 1)
                dve.tensor_scalar(flat[m], flat[m], ROUND + 1.0, ROUND - 1.0, ALU.min, ALU.max).then_inc(q2_ok, 1)
            for g, (m, blocks, rows, dst, width) in enumerate(groups):
                if g % 2 == 0:
                    dve.wait_ge(t_ps, g + 1)
                    dve.tensor_scalar(dst, psT[g % 6][0:rows, 0:width], ROUND, None, ALU.subtract).then_inc(ev_v, 1)


def feed_forward(nc, a, k):
    with ExitStack() as ctx:
        s = Scope(nc, ctx, "ff")
        y = s.sb("y", [P, L])
        yr = [s.sb(f"yr{p}", [P, L]) for p in range(2)]
        xq = [s.sb(f"xq{p}", [P, L], BF16) for p in range(2)]
        r1 = [s.sb(f"r1_{p}", [P, 512]) for p in range(2)]
        r2 = [s.sb(f"r2_{p}", [P, 512]) for p in range(2)]
        h = s.sb("h", [P, FF])
        hr = s.sb("hr", [P, FF])
        hq = s.sb("hq", [P, FFC, P], BF16)
        gm = s.sb("gm", [P, 1])
        gd = s.sb("gd", [P, 1])
        gi = s.sb("gi", [P, 1])
        qs = s.sb("qs", [P, 1])
        os_ = [s.sb(f"os{p}", [P, 1]) for p in range(2)]
        stats = (s.sb("stats", [P, 6]), s.sb("mean_var", [P, 2]))
        ag_ok = s.sem("ag_ok")
        psX = s.ps("psX", [P, 512])
        psG = [s.ps(f"psG{i}", [P, 512]) for i in range(2)]
        psU = [s.ps(f"psU{i}", [P, 512]) for i in range(2)]
        psT = [s.ps(f"psT{i}", [P, 512]) for i in range(2)]
        psD = s.ps("psD", [P, 512])
        (y_ok, yr_ok, x_ps, xq_ok, g_ps, u_ps, r1_ok, r2_ok, h_ok, gm_ok, gd_ok, gi_ok, qs_ok, os_ok, hr_ok, t_ps, hq_a,
         hq_v, d_ps, x_ok, st_ok, mv_ok) = (s.sem(n) for n in (
             "y_ok yr_ok x_ps xq_ok g_ps u_ps r1_ok r2_ok h_ok gm_ok gd_ok gi_ok qs_ok os_ok hr_ok t_ps hq_a "
             "hq_v d_ps x_ok st_ok mv_ok").split())
        block = s.block()
        NB = len(FFB)
        TG = [range(f, min(f + 4, FFC)) for f in range(0, FFC, 4)]
        NG = len(TG)

        @block.vector
        def _(dve):
            def quantise(i, p):
                wait(dve, yr_ok, i)
                dve.tensor_scalar(y[:, :], k.x[:, i, :], k.mv[:, i, 0:1], k.s4[:, bass.ds(i, 1)], ALU.subtract,
                                  ALU.mult).then_inc(y_ok, 1)
                dve.wait_ge(y_ok, i + 1)
                wait(dve, x_ps, i - 1)
                dve.tensor_scalar(yr[p][:, :], y[:, :], ROUND, ROUND + 7.0, ALU.add, ALU.min).then_inc(yr_ok, 1)

            def take_x(i, p):
                dve.wait_ge(x_ps, i + 1)
                dve.tensor_scalar(xq[p][:, :], psX[:, :], ROUND, -8.0, ALU.subtract, ALU.max).then_inc(xq_ok, 1)

            def step(i, p, j):
                t = i - 1
                if exists(i, TILES):
                    for n, (f0, f1) in enumerate(FFB):
                        dve.wait_ge(r2_ok, NB * i + n + 1)
                        dve.wait_ge(u_ps, NB * i + n + 1)
                        if n == 0:
                            wait(dve, hr_ok, i)
                        q = (NB * p + n) % 2
                        dve.tensor_tensor(h[:, f0:f1], psU[q][:, 0:f1 - f0], r2[q][:, 0:f1 - f0],
                                          ALU.mult).then_inc(h_ok, 1)
                if exists(i + 1, TILES):
                    take_x(i + 1, 1 - p)
                if exists(t, TILES):
                    for n in (1, 2):
                        js = TG[n]
                        w = P * len(js)
                        dve.wait_ge(t_ps, NG * t + n + 1)
                        if n == 1:
                            dve.tensor_scalar(hq[:, js[0]:js[0] + 4, :].rearrange("p a b -> p (a b)"),
                                              psT[(NG * (1 - p) + n) % 2][:, 0:w], ROUND, None, ALU.subtract).then_inc(hq_v, 1)
                        else:
                            q = psT[(NG * (1 - p) + n) % 2]
                            dve.tensor_scalar(hq[:, js[0]:js[0] + 2, :].rearrange("p a b -> p (a b)"), q[:, 0:2 * P],
                                              ROUND, None, ALU.subtract).then_inc(hq_v, 1)
                            last = FF - (FFC - 1) * P
                            dve.tensor_scalar(hq[0:last, FFC - 1, :], q[0:last, 2 * P:3 * P], ROUND, None,
                                              ALU.subtract).then_inc(hq_v, 1)
                if exists(i, TILES):
                    dve.wait_ge(h_ok, NB * i + NB)
                    dve.tensor_reduce(gm[:, :], h[:, :], X, ALU.max, apply_absolute_value=True).then_inc(gm_ok, 1)
                    dve.wait_ge(gm_ok, i + 1)
                    dve.tensor_scalar(gd[:, :], gm[:, :], k.su_abs[:, bass.ds(i, 1)], EPS, ALU.mult, ALU.add).then_inc(gd_ok, 1)
                    wait(dve, x_ok, i - 1)
                    dve.tensor_scalar(os_[p][:, :], gm[:, :], k.sd[:, bass.ds(i, 1)], None, ALU.mult).then_inc(os_ok, 1)
                    dve.wait_ge(gd_ok, i + 1)
                    dve.reciprocal(gi[:, :], gd[:, :]).then_inc(gi_ok, 1)
                    dve.wait_ge(gi_ok, i + 1)
                    dve.tensor_scalar(qs[:, :], gi[:, :], k.su[:, bass.ds(i, 1)], None, ALU.mult).then_inc(qs_ok, 1)
                if exists(i + 2, TILES):
                    quantise(i + 2, p)
                if exists(t, TILES):
                    dve.wait_ge(d_ps, t + 1)
                    dve.wait_ge(os_ok, t + 1)
                    dve.scalar_tensor_tensor(out=k.x[:, t, :], in0=psD[:, :], scalar=os_[1 - p][:, :],
                                             in1=k.x[:, t, :], op0=ALU.mult, op1=ALU.add).then_inc(x_ok, 1)
                    row_stats(dve, k, t, stats, x_ok, st_ok, ag_ok, mv_ok)

            quantise(0, 0)
            quantise(1, 1)
            take_x(0, 0)
            sweep(dve, step, TILES, 1)

        @block.scalar
        def _(act):
            def step(i, p, j):
                t = i - 1
                if exists(i, TILES):
                    for n, (f0, f1) in enumerate(FFB):
                        q = (NB * p + n) % 2
                        hold(act, g_ps, NB * i + n + 1, k.passed)
                        act.activation(r1[q][:, 0:f1 - f0], psG[q][:, 0:f1 - f0], ACT.Relu,
                                       scale=k.sg[:, bass.ds(i, 1)]).then_inc(r1_ok, 1)
                        act.wait_ge(r1_ok, NB * i + n + 1)
                        wait(act, h_ok, NB * i + n - 1)
                        act.activation(r2[q][:, 0:f1 - f0], r1[q][:, 0:f1 - f0], ACT.Square).then_inc(r2_ok, 1)
                if exists(t, TILES):
                    act.wait_ge(t_ps, NG * t + 1)
                    act.activation(hq[:, 0:4, :].rearrange("p a b -> p (a b)"), psT[(NG * (1 - p)) % 2][:, :],
                                   ACT.Identity, bias=k.m_minus[:, :]).then_inc(hq_a, 1)
                if exists(i, TILES):
                    act.wait_ge(qs_ok, i + 1)
                    wait(act, t_ps, NG * i)
                    act.activation(hr[:, :], h[:, :], ACT.Identity, scale=qs[:, :],
                                   bias=k.m_round[:, :]).then_inc(hr_ok, 1)

            sweep(act, step, TILES, 1)

        @block.tensor
        def _(pe):
            def x_up(i, p):
                pe.wait_ge(yr_ok, i + 1)
                wait(pe, xq_ok, i)
                for c in range(NC):
                    mm = pe.transpose(chunk(psX, c), chunk(yr[p], c), k.ident[:, :])
                mm.then_inc(x_ps, 1)

            def step(i, p, j):
                t = i - 1
                if exists(i, TILES):
                    pe.wait_ge(xq_ok, i + 1)
                    for n, (f0, f1) in enumerate(FFB):
                        q = (NB * p + n) % 2
                        wait(pe, r1_ok, NB * i + n - 1)
                        for c in range(NC):
                            mm = pe.matmul(psG[q][:, 0:f1 - f0], chunk(xq[p], c), k.wgT[:, c, f0:f1], start=c == 0,
                                           stop=c == NC - 1)
                        mm.then_inc(g_ps, 1)
                        wait(pe, h_ok, NB * i + n - 1)
                        for c in range(NC):
                            mm = pe.matmul(psU[q][:, 0:f1 - f0], chunk(xq[p], c), k.wuT[:, c, f0:f1], start=c == 0,
                                           stop=c == NC - 1)
                        mm.then_inc(u_ps, 1)
                if exists(i + 1, TILES):
                    x_up(i + 1, 1 - p)
                if exists(t, TILES):
                    pe.wait_ge(hr_ok, t + 1)
                    for n, js in enumerate(TG):
                        if n == 0:
                            wait(pe, hq_v, 3 * t - 2)
                        elif n == 1:
                            wait(pe, hq_v, 3 * t)
                        else:
                            pe.wait_ge(hq_a, t + 1)
                        for m in js:
                            w = min(P, FF - m * P)
                            mm = pe.transpose(psT[(NG * (1 - p) + n) % 2][0:w, (m - js[0]) * P:(m - js[0] + 1) * P],
                                              hr[:, m * P:m * P + w], k.ident[:, :])
                        mm.then_inc(t_ps, 1)
                    wait(pe, x_ok, t)
                    pe.wait_ge(hq_a, t + 1)
                    pe.wait_ge(hq_v, 3 * t + 3)
                    for m in range(FFC):
                        w = min(P, FF - m * P)
                        mm = pe.matmul(psD[:, :], hq[0:w, m, :], k.wdT[0:w, m, :], start=m == 0, stop=m == FFC - 1)
                    mm.then_inc(d_ps, 1)

            x_up(0, 0)
            sweep(pe, step, TILES, 1)


def split_shift(dve, m, part, rest, sems, n):
    p_ok, r_ok = sems
    w = m.shape[2]
    dve.tensor_scalar(part[:, :, 0:w], m, -1.0, None, ALU.mult).then_inc(p_ok, 1)
    dve.wait_ge(p_ok, 3 * n + 1)
    dve.scalar_tensor_tensor(out=rest, in0=m, scalar=-1.0, in1=part[:, :, 0:w], op0=ALU.mult,
                             op1=ALU.subtract).then_inc(r_ok, 1)
    dve.wait_ge(r_ok, n + 1)
    dve.tensor_copy(part[:, :, 32:32 + w], rest).then_inc(p_ok, 1)
    dve.wait_ge(p_ok, 3 * n + 2)
    dve.tensor_tensor(part[:, :, 64:64 + w], rest, part[:, :, 32:32 + w], ALU.subtract).then_inc(p_ok, 1)


def key_side(nc, a, k):
    with ExitStack() as ctx:
        s = Scope(nc, ctx, "keys")
        cf = s.sb("cf", [P, L])
        cs = [s.sb(f"cs{h}", [P, L], F16) for h in range(2)]
        cT = s.sb("cT", [P, NC, 2, D + 1])
        mk = s.sb("mk", [P, NC, 1])
        mpart = s.sb("mpart", [P, NC, 96], BF16)
        mrest = s.sb("mrest", [P, NC, 1])
        mT = s.sb("mT", [96, L], BF16)
        ek = [s.sb(f"ek{i}", [P, L]) for i in range(NC)]
        gT = s.sb("gT", [D + 1, L])
        rl = s.sb("rl", [P, NC])
        psC = s.ps("psC", [P, 512])
        ps1 = [s.ps(f"ps1_{i}", [P, 512]) for i in range(2)]
        ps2 = [s.ps(f"ps2_{i}", [P, 512]) for i in range(2)]
        psG = s.ps("psG", [P, 512])
        psM = s.ps("psM", [P, NC, P])
        psR = s.ps("psR", [P, 1024], BF16)
        (init_ok, c_in, hi_ok, lo_ok, c_ps, cT_ok, k1_ps, mk_ok, part_ok, rest_ok, r_ps, mT_ok, k2_ps, ek_ok, g_ps,
         gT_ok, m_ps, rl_ok, M_ok) = (s.sem(n) for n in (
             "init_ok c_in hi_ok lo_ok c_ps cT_ok k1_ps mk_ok part_ok rest_ok r_ps mT_ok k2_ps ek_ok g_ps "
             "gT_ok m_ps rl_ok M_ok").split())
        block = s.block()
        nat = a["ctx"].rearrange("(t b) d l -> t (b d) l", b=2)

        @block.sync
        def _(sp):
            def step(t, p, j):
                wait(sp, lo_ok, 2 * t)
                wait(sp, c_ps, t)
                sp.dma_start(cf[:, :], nat[t]).then_inc(c_in, 16)

            sweep(sp, step, TILES, 0)

        @block.gpsimd
        def _(pool):
            def step(b, h, t):
                pool.wait_ge(c_in, 16 * t + 16)
                r = HALF[h]
                hold(pool, k2_ps, NC * (b - 1), k.passed)
                pool.tensor_scalar(cs[h][r, :], cf[r, :], 1.0, 0.0, ALU.mult, ALU.add).then_inc(hi_ok, 1)

            sweep(pool, step, BATCHES, 0)

        @block.vector
        def _(dve):
            dve.memset(mpart[:, :, :], 0.0).then_inc(init_ok, 1)
            dve.memset(cT[:, :, :, D:D + 1], 1.0).then_inc(init_ok, 1)
            dve.wait_ge(init_ok, 1)

            def keys_max(b):
                for c in range(NC):
                    dve.wait_ge(k1_ps, NC * b + c + 1)
                    wait(dve, rest_ok, b)
                    dve.tensor_reduce(mk[:, c, :], ps1[c % 2][:, :], X, ALU.max).then_inc(mk_ok, 1)
                dve.wait_ge(mk_ok, NC * b + NC)
                wait(dve, r_ps, b)
                split_shift(dve, mk[:, :, :], mpart, mrest[:, :, :], (part_ok, rest_ok), b)

            def low(b, h):
                dve.wait_ge(hi_ok, b + 1)
                dve.tensor_tensor(cs[h][HALF[1 - h], :], cf[HALF[h], :], cs[h][HALF[h], :],
                                  ALU.subtract).then_inc(lo_ok, 1)

            def step(b, h, t):
                if exists(b + 1, BATCHES):
                    keys_max(b + 1)
                if exists(b + 2, BATCHES):
                    low(b + 2, h)
                dve.wait_ge(m_ps, b + 1)
                dve.reciprocal(rl[:, :], psM[:, :, D]).then_inc(rl_ok, 1)
                dve.wait_ge(rl_ok, b + 1)
                dve.tensor_tensor(k.M[:, b, :, :], psM[:, :, 0:D], rl[:, :].unsqueeze(2).broadcast_to([P, NC, D]),
                                  ALU.mult).then_inc(M_ok, 1)

            low(0, 0)
            low(1, 1)
            keys_max(0)
            sweep(dve, step, BATCHES, 0)

        @block.scalar
        def _(act):
            act.wait_ge(init_ok, 2)

            def transposed(t):
                act.wait_ge(c_ps, t + 1)
                act.activation(cT[:, :, :, 0:D], psC[:, :].rearrange("p (c b d) -> p c b d", c=NC, b=2),
                               ACT.Copy).then_inc(cT_ok, 1)

            def shift(b):
                act.wait_ge(r_ps, b + 1)
                act.activation(mT[:, :], psR[0:96, 0:L], ACT.Copy).then_inc(mT_ok, 1)

            def step(b, h, t):
                for c in range(NC):
                    act.wait_ge(k2_ps, NC * b + c + 1)
                    act.activation(ek[c][:, :], ps2[c % 2][:, :], ACT.Exp).then_inc(ek_ok, 1)
                act.wait_ge(g_ps, b + 1)
                act.activation(gT[:, :], psG[0:D + 1, :], ACT.Copy).then_inc(gT_ok, 1)
                if exists(b + 1, BATCHES):
                    if h == 1:
                        transposed(t + 1)
                    shift(b + 1)

            transposed(0)
            shift(0)
            sweep(act, step, BATCHES, 0)

        @block.tensor
        def _(pe):
            def context(t):
                pe.wait_ge(c_in, 16 * t + 16)
                for c in range(NC):
                    mm = pe.transpose(chunk(psC, c), chunk(cf, c), k.ident[:, :])
                mm.then_inc(c_ps, 1)

            def keys_for_max(b, h):
                pe.wait_ge(lo_ok, b + 1)
                for c in range(NC):
                    wait(pe, mk_ok, NC * b + c - 1)
                    pe.matmul(ps1[c % 2][:, :], chunk(k.wk_hi, c), cs[h][:, :], start=True, stop=False)
                    pe.matmul(ps1[c % 2][:, :], chunk(k.wk_lo, c), cs[h][:, :], start=False,
                              stop=True).then_inc(k1_ps, 1)

            def shift(b):
                pe.wait_ge(part_ok, 3 * b + 3)
                for c in range(NC):
                    mm = pe.transpose(psR[0:96, c * P:(c + 1) * P], mpart[:, c, :], k.ident16[:, :])
                mm.then_inc(r_ps, 1)

            def step(b, h, t):
                pe.wait_ge(mT_ok, b + 1)
                if h == 0:
                    pe.wait_ge(cT_ok, t + 1)
                for c in range(NC + 1):
                    if c < NC:
                        wait(pe, ek_ok, NC * b + c - 1)
                        pe.matmul(ps2[c % 2][:, :], k.ones[0:96, :], mT[:, :], start=True, stop=False)
                        pe.matmul(ps2[c % 2][:, :], chunk(cs[h], c), k.wk_hi[:, :], start=False, stop=False)
                        pe.matmul(ps2[c % 2][:, :], chunk(cs[h], c), k.wk_lo[:, :], start=False,
                                  stop=True).then_inc(k2_ps, 1)
                    if c > 0:
                        pe.wait_ge(ek_ok, NC * b + c)
                        if c == 1:
                            wait(pe, gT_ok, b)
                        mm = pe.matmul(psG[0:D + 1, :], cT[:, c - 1, h, :], ek[c - 1][:, :], start=c == 1, stop=c == NC)
                mm.then_inc(g_ps, 1)
                if exists(b + 1, BATCHES):
                    if h == 1:
                        context(t + 1)
                    keys_for_max(b + 1, 1 - h)
                pe.wait_ge(gT_ok, b + 1)
                wait(pe, M_ok, b)
                for n in range(HEADS):
                    mm = pe.matmul(psM[HALF[n % 2], n // 2, 0:D + 1], gT[:, n * D:(n + 1) * D], k.wv_wo[:, n, :],
                                   start=True, stop=True)
                    if n == HEADS // 2 - 1 and exists(b + 1, BATCHES):
                        shift(b + 1)
                mm.then_inc(m_ps, 1)

            context(0)
            keys_for_max(0, 0)
            shift(0)
            sweep(pe, step, BATCHES, 0)


def query_side(nc, a, k):
    with ExitStack() as ctx:
        s = Scope(nc, ctx, "query")
        xn = s.sb("xn", [P, L])
        xs = [s.sb(f"xs{h}", [P, L], F16) for h in range(2)]
        mq = s.sb("mq", [P, NC, HEADS])
        mpart = s.sb("mpart", [P, NC, 96], BF16)
        mrest = s.sb("mrest", [P, NC, HEADS])
        mT = s.sb("mT", [96, L], BF16)
        eq = [s.sb(f"eq{i}", [P, L]) for i in range(NC)]
        qn = [s.sb(f"qn{i}", [P, L]) for i in range(NC)]
        lq = s.sb("lq", [P, NC, HEADS])
        rq = s.sb("rq", [P, NC, HEADS])
        qT = s.sb("qT", [P, NC, L])
        m_sb = [s.sb(f"m_sb{h}", [P, NC, D]) for h in range(2)]
        y = s.sb("y", [P, L])
        sq = s.sb("sq", [P, L])
        ln = s.sb("ln", [P, L])
        inv = s.sb("inv", [P, L])
        z = s.sb("z", [P, L])
        stats = (s.sb("stats", [P, 6]), s.sb("mean_var", [P, 2]))
        ag_ok = s.sem("ag_ok")
        psQ = [s.ps(f"psQ{i}", [P, 512]) for i in range(NC)]
        psR = s.ps("psR", [P, 1024], BF16)
        psX = [s.ps(f"psX{i}", [P, 512]) for i in range(2)]
        psF = s.ps("psF", [P, 512])
        (init_ok, xn_ok, hi_ok, lo_ok, q_ps, mq_ok, part_ok, rest_ok, r_ps, mT_ok, f_ps, eq_ok, lq_ok, rq_ok, qn_ok,
         x_ps, qT_ok, msb_ok, o_ps, y_ok, sq_ok, ss_ps, ln_ok, inv_ok, z_ok, x_ok, st_ok, mv_ok) = (s.sem(n) for n in (
             "init_ok xn_ok hi_ok lo_ok q_ps mq_ok part_ok rest_ok r_ps mT_ok f_ps eq_ok lq_ok rq_ok qn_ok "
             "x_ps qT_ok msb_ok o_ps y_ok sq_ok ss_ps ln_ok inv_ok z_ok x_ok st_ok mv_ok").split())
        vec_x, act_x = row_rstd(k, 2, lambda e: None)
        block = s.block()

        def heads(ap):
            return ap.rearrange("p (h d) -> p h d", h=HEADS)

        @block.vector
        def _(dve):
            def low(b, h):
                dve.wait_ge(hi_ok, b + 1)
                dve.tensor_tensor(xs[h][HALF[1 - h], :], xn[HALF[h], :], xs[h][HALF[h], :],
                                  ALU.subtract).then_inc(lo_ok, 1)

            def queries_max(b):
                for c in range(NC):
                    dve.wait_ge(q_ps, NC * b + c + 1)
                    dve.tensor_reduce(mq[:, c, :], heads(psQ[c][:, :]), X, ALU.max).then_inc(mq_ok, 1)
                dve.wait_ge(mq_ok, NC * b + NC)
                wait(dve, r_ps, b)
                split_shift(dve, mq[:, :, :], mpart, mrest[:, :, :], (part_ok, rest_ok), b)

            def step(b, h, t):
                if h == 0 and exists(t + 1, TILES):
                    normed(t + 1)
                if exists(b, BATCHES):
                    matrix(b, h)
                    for c in range(NC):
                        dve.wait_ge(eq_ok, NC * b + c + 1)
                        dve.tensor_reduce(lq[:, c, :], heads(eq[c][:, :]), X, ALU.add).then_inc(lq_ok, 1)
                    dve.wait_ge(lq_ok, NC * b + NC)
                    wait(dve, qn_ok, NC * b)
                    dve.reciprocal(rq[:, :, :], lq[:, :, :]).then_inc(rq_ok, 1)
                if exists(b + 1, BATCHES):
                    queries_max(b + 1)
                if h == 0 and exists(t + 1, TILES):
                    low(b + 2, 0)
                    low(b + 3, 1)
                u = t - 1
                if h == 1 and exists(u, TILES):
                    result(u)

            def result(u):
                dve.wait_ge(inv_ok, u + 1)
                wait(dve, x_ok, u)
                dve.scalar_tensor_tensor(out=z[:, :], in0=inv[:, :], scalar=1e12, in1=y[:, :], op0=ALU.min,
                                         op1=ALU.mult).then_inc(z_ok, 1)
                dve.wait_ge(z_ok, u + 1)
                dve.scalar_tensor_tensor(out=k.x[:, u, :], in0=z[:, :], scalar=k.g8[:, :], in1=k.x[:, u, :],
                                         op0=ALU.mult, op1=ALU.add).then_inc(x_ok, 1)
                row_stats(dve, k, u, stats, x_ok, st_ok, ag_ok, mv_ok)

            def normed(t):
                wait(dve, lo_ok, 2 * t)
                wait(dve, hi_ok, 2 * t)
                dve.tensor_scalar(xn[:, :], k.x[:, t, :], k.mv[:, t, 0:1], k.rstd[:, bass.ds(t, 1)], ALU.subtract,
                                  ALU.mult).then_inc(xn_ok, 1)

            def matrix(b, h):
                wait(dve, o_ps, b - 1)
                dve.tensor_scalar(m_sb[h][:, :, :], k.M[:, b, :, :], 1.0, None, ALU.mult).then_inc(msb_ok, 1)

            dve.memset(mpart[:, :, :], 0.0).then_inc(init_ok, 1)
            dve.wait_ge(init_ok, 1)
            vec_x(dve)
            normed(0)
            low(0, 0)
            low(1, 1)
            queries_max(0)
            sweep(dve, step, BATCHES, 2)

        @block.gpsimd
        def _(pool):
            def step(b, h, t):
                for c in range(NC):
                    pool.wait_ge(rq_ok, b + 1)
                    wait(pool, x_ps, NC * (b - 1) + c + 1)
                    pool.tensor_tensor(heads(qn[c][:, :]), heads(eq[c][:, :]),
                                       rq[:, c, :].unsqueeze(2).broadcast_to([P, HEADS, D]), ALU.mult).then_inc(qn_ok, 1)

            sweep(pool, step, BATCHES, 0)

        @block.scalar
        def _(act):
            def high(b, h, t):
                act.wait_ge(xn_ok, t + 1)
                wait(act, q_ps, NC * (b - 1))
                act.activation(xs[h][HALF[h], :], xn[HALF[h], :], ACT.Copy).then_inc(hi_ok, 1)

            def shift(b):
                act.wait_ge(r_ps, b + 1)
                act.activation(mT[:, :], psR[0:96, 0:L], ACT.Copy).then_inc(mT_ok, 1)

            def transposed(b, c):
                act.wait_ge(x_ps, NC * b + c + 1)
                wait(act, o_ps, b)
                act.activation(qT[:, :, c * P:(c + 1) * P], psX[c % 2][:, :].rearrange("p (j n) -> p j n", j=NC),
                               ACT.Copy).then_inc(qT_ok, 1)

            def step(b, h, t):
                for c in range(NC):
                    if exists(b, BATCHES):
                        act.wait_ge(f_ps, NC * b + c + 1)
                        wait(act, qn_ok, NC * (b - 1) + c + 1)
                        act.activation(eq[c][:, :], psQ[c][:, :], ACT.Exp).then_inc(eq_ok, 1)
                    if exists(b - 1, BATCHES):
                        transposed(b - 1, c)
                if h == 0 and exists(t + 1, TILES):
                    high(b + 2, 0, t + 1)
                    high(b + 3, 1, t + 1)
                if exists(b + 1, BATCHES):
                    shift(b + 1)
                if h == 0 and exists(t - 1, TILES):
                    u = t - 1
                    act.wait_ge(o_ps, b)
                    wait(act, z_ok, u)
                    act.activation(y[:, :], psF[:, :], ACT.Identity, bias=k.bo1[:, :]).then_inc(y_ok, 1)
                    act.activation(sq[:, :], psF[:, :], ACT.Square, bias=k.bo1[:, :]).then_inc(sq_ok, 1)
                    act.wait_ge(ss_ps, u + 1)
                    act.activation(ln[:, :], psF[:, :], ACT.Ln, scale=2.0 ** LN_SCALE).then_inc(ln_ok, 1)
                    act.wait_ge(ln_ok, u + 1)
                    act.activation(inv[:, :], ln[:, :], ACT.Exp, scale=-0.5, bias=k.half_ln[:, :]).then_inc(inv_ok, 1)

            act_x(act)
            high(0, 0, 0)
            high(1, 1, 0)
            shift(0)
            sweep(act, step, BATCHES, 1)

        @block.tensor
        def _(pe):
            def queries(b, h):
                pe.wait_ge(lo_ok, b + 1)
                for c in range(NC):
                    wait(pe, eq_ok, NC * (b - 1) + c + 1)
                    pe.matmul(psQ[c][:, :], chunk(xs[h], c), k.wq_hi[:, :], start=True, stop=False)
                    pe.matmul(psQ[c][:, :], chunk(xs[h], c), k.wq_lo[:, :], start=False, stop=True).then_inc(q_ps, 1)

            def shift(b):
                pe.wait_ge(part_ok, 3 * b + 3)
                wait(pe, mT_ok, b)
                for c in range(NC):
                    mm = pe.transpose(psR[0:96, c * P:(c + 1) * P], mpart[:, c, :], k.ident16[:, :])
                mm.then_inc(r_ps, 1)

            def step(b, h, t):
                if exists(b, BATCHES):
                    pe.wait_ge(mT_ok, b + 1)
                    for c in range(NC):
                        pe.matmul(psQ[c][:, :], chunk(mT, c), k.ind[0:96, :], start=False, stop=True,
                                  skip_group_check=True).then_inc(f_ps, 1)
                if exists(b - 1, BATCHES):
                    for c in range(NC):
                        pe.wait_ge(qn_ok, NC * (b - 1) + c + 1)
                        wait(pe, qT_ok, NC * (b - 1) + c - 1)
                        for j in range(NC):
                            mm = pe.transpose(chunk(psX[c % 2], j), chunk(qn[c], j), k.ident[:, :])
                        mm.then_inc(x_ps, 1)
                if exists(b + 1, BATCHES):
                    queries(b + 1, 1 - h)
                if exists(b - 1, BATCHES):
                    pe.wait_ge(msb_ok, b)
                    pe.wait_ge(qT_ok, NC * b)
                    if h == 1:
                        wait(pe, ln_ok, t)
                    for j in range(NC):
                        mm = pe.matmul(psF[HALF[1 - h], :], m_sb[1 - h][:, j, :], qT[:, j, :], start=j == 0,
                                       stop=j == NC - 1)
                    mm.then_inc(o_ps, 1)
                if exists(b + 1, BATCHES):
                    shift(b + 1)
                if h == 0 and exists(t - 1, TILES):
                    pe.wait_ge(sq_ok, t)
                    pe.wait_ge(y_ok, t)
                    pe.matmul(psF[:, :], k.blk[:, :], sq[:, :], start=True, stop=True).then_inc(ss_ps, 1)

            queries(0, 0)
            shift(0)
            sweep(pe, step, BATCHES, 1)


def projection(nc, a, k):
    with ExitStack() as ctx:
        s = Scope(nc, ctx, "proj")
        x_s = [s.sb(f"x_s{p}", [P, L]) for p in range(2)]
        xT = [s.sb(f"xT{p}", [P, NC, P]) for p in range(2)]
        psT = [s.ps(f"psT{i}", [P, 512]) for i in range(2)]
        psH = [s.ps(f"psH{i}", [P, 512]) for i in range(2)]
        psZ = [s.ps(f"psZ{i}", [P, 512]) for i in range(2)]
        t_ps, xs_ok, xT_ok, z_ps, z_ok, h_ps, hs_ok, x_ok = (s.sem(n) for n in (
            "t_ps xs_ok xT_ok z_ps z_ok h_ps hs_ok x_ok").split())
        vec_x, act_x = row_rstd(k, 3, lambda e: None)
        block = s.block()

        @block.scalar
        def _(act):
            def step(i, p, j):
                act.wait_ge(t_ps, i + 1)
                act.activation(xT[p][:, :, :].rearrange("p a b -> p (a b)"), psT[p][:, :], ACT.Copy).then_inc(xT_ok, 1)
                act.wait_ge(z_ps, i + 1)
                act.activation(k.zT[:, i, :], psZ[p][:, 0:P], ACT.Copy).then_inc(z_ok, 1)

            act_x(act)
            sweep(act, step, TILES, 0)

        @block.vector
        def _(dve):
            def normed(i, p):
                wait(dve, t_ps, i - 1)
                dve.tensor_scalar(x_s[p][:, :], k.x[:, i, :], k.mv[:, i, 0:1], k.rstd[:, bass.ds(i, 1)], ALU.subtract,
                                  ALU.mult).then_inc(xs_ok, 1)

            def step(i, p, j):
                if exists(i + 2, TILES):
                    normed(i + 2, p)
                dve.wait_ge(h_ps, i + 1)
                dve.tensor_scalar(k.Hs[:, i, :], psH[p][:, 0:EXPERTS], 1.0, None, ALU.mult).then_inc(hs_ok, 1)
                dve.tensor_tensor(k.x[:, i, :], psH[p][:, :], k.x[:, i, :], ALU.add).then_inc(x_ok, 1)

            vec_x(dve)
            normed(0, 0)
            normed(1, 1)
            sweep(dve, step, TILES, 0)

        @block.tensor
        def _(pe):
            def up(i, p):
                pe.wait_ge(xs_ok, i + 1)
                wait(pe, xT_ok, i - 1)
                for c in range(NC):
                    mm = pe.transpose(chunk(psT[p], c), chunk(x_s[p], c), k.ident[:, :])
                mm.then_inc(t_ps, 1)

            def step(i, p, j):
                if exists(i + 1, TILES):
                    up(i + 1, 1 - p)
                pe.wait_ge(xT_ok, i + 1)
                wait(pe, z_ok, i - 1)
                for c in range(NC):
                    mm = pe.matmul(psZ[p][:, 0:P], k.A4[:, c, :], xT[p][:, c, :], start=c == 0, stop=c == NC - 1)
                mm.then_inc(z_ps, 1)
                wait(pe, hs_ok, i - 1)
                wait(pe, x_ok, i - 1)
                pe.matmul(psH[p][:, :], k.ones[:, :], k.bias_rows[2][:, :], start=True, stop=False)
                for c in range(NC):
                    mm = pe.matmul(psH[p][:, :], xT[p][:, c, :], k.WT[:, c, :], start=False, stop=c == NC - 1)
                mm.then_inc(h_ps, 1)

            up(0, 0)
            sweep(pe, step, TILES, 0)


def experts(nc, a, k):
    TE = [P, TILES, EXPERTS]
    with ExitStack() as ctx:
        s = Scope(nc, ctx, "exp")
        dl = s.sb("dl", TE)
        mx2 = s.sb("mx2", [P, 2])
        diag = s.sb("diag", [2, 3])
        ones2 = s.sb("ones2", [2, P])
        sc = s.sb("sc", [P, 2])
        lg, e, pr, w, u = (s.sb("d2" + n, TE) for n in "lepwu")
        r = s.sb("r", [P, TILES])
        top = s.sb("top", [P, TILES, 8])
        wf = s.sb("wf", [P, TILES, RANK])
        wT = s.sb("wT", [P, 4, P])
        zp = s.sb("zp", [P, TILES * P])
        zs = s.sb("zs", [P, TILES * P], F16)
        outb = [s.sb(f"outb{p}", [P, L]) for p in range(2)]
        psA = s.ps("psA", [P, 512])
        psB = s.ps("psB", [P, 512])
        psP = s.ps("psP", [P, 4, 512])
        psD = [psA, psB]
        a_ps, lnk, act_ok, p_ps, d_ps, o_ok, z_fin = (s.sem(n) for n in "a_ps lnk act_ok p_ps d_ps o_ok z_fin".split())
        wT_ps, wT_ok, done_v = (s.sem(n) for n in ("wT_ps", "wT_ok", "done_v"))
        store = [s.sem(f"store{p}") for p in range(2)]
        block = s.block()
        out = a["out"].rearrange("(t b) d l -> t (b d) l", b=2)

        def te(ap):
            return ap.unsqueeze(2).broadcast_to(TE)

        @block.vector
        def _(dve):
            n = [0]

            def link(ins):
                n[0] += 1
                ins.then_inc(lnk, 1)
                dve.wait_ge(lnk, n[0])

            link(dve.memset(ones2[:, :], 1.0))
            link(dve.memset(wf[:, :, :], 0.0))
            dve.wait_ge(a_ps, 1)
            link(dve.tensor_copy(dl[:, :, :], psA[:, 0:P].rearrange("p (t e) -> p t e", t=TILES)))
            for m, v in enumerate((k.Hs, dl)):
                link(dve.tensor_reduce(mx2[:, m:m + 1], v[:, :, :].rearrange("p a b -> p (a b)"), X, ALU.max,
                                       apply_absolute_value=True))
            link(dve.tensor_scalar(mx2[:, :], mx2[:, :], k.odd[:, :], None, ALU.mult))
            dve.sem_inc(done_v, 1)
            dve.wait_ge(a_ps, 2)
            link(dve.tensor_reduce(diag[:, 2:3], psB[0:2, 0:P], X, ALU.max))
            link(dve.tensor_scalar(diag[:, 2:3], diag[:, 2:3], 1e-6, None, ALU.max))
            link(dve.reciprocal(diag[:, 2:3], diag[:, 2:3]))
            link(dve.tensor_scalar(diag[:, 0:2], k.ident[0:2, 0:2], diag[:, 2:3], 0.5, ALU.mult, ALU.mult))
            dve.sem_inc(done_v, 1)
            dve.wait_ge(a_ps, 3)
            link(dve.tensor_copy(sc[:, :], psA[:, 256:258]))
            link(dve.tensor_scalar(lg[:, :, :], k.Hs[:, :, :], sc[:, 0:1], None, ALU.mult))
            link(dve.scalar_tensor_tensor(out=lg[:, :, :], in0=dl[:, :, :], scalar=sc[:, 1:2], in1=lg[:, :, :],
                                          op0=ALU.mult, op1=ALU.add))
            link(dve.tensor_reduce(r[:, :], lg[:, :, :], X, ALU.max))
            link(dve.tensor_tensor(lg[:, :, :], lg[:, :, :], te(r[:, :]), ALU.subtract))
            dve.sem_inc(done_v, 1)
            dve.wait_ge(act_ok, 1)
            link(dve.tensor_reduce(r[:, :], e[:, :, :], X, ALU.add))
            link(dve.reciprocal(r[:, :], r[:, :]))
            link(dve.tensor_tensor(pr[:, :, :], e[:, :, :], te(r[:, :]), ALU.mult))
            for t in range(TILES):
                dve.max(top[:, t, :], pr[:, t, :]).then_inc(lnk, 1)
            n[0] += TILES
            dve.wait_ge(lnk, n[0])
            link(dve.tensor_tensor(u[:, :, :], pr[:, :, :], top[:, :, 1:2].broadcast_to(TE), ALU.subtract))
            dve.sem_inc(done_v, 1)
            dve.wait_ge(act_ok, 2)
            link(dve.tensor_scalar(w[:, :, :], w[:, :, :], 1.0, None, ALU.add))
            link(dve.reciprocal(w[:, :, :], w[:, :, :]))
            link(dve.tensor_tensor(w[:, :, :], w[:, :, :], pr[:, :, :], ALU.mult))
            link(dve.tensor_reduce(r[:, :], w[:, :, :], X, ALU.add))
            link(dve.tensor_scalar(r[:, :], r[:, :], 1e-9, None, ALU.add))
            link(dve.reciprocal(r[:, :], r[:, :]))
            link(dve.tensor_tensor(wf[:, :, 0:EXPERTS], w[:, :, :], te(r[:, :]), ALU.mult))
            dve.sem_inc(done_v, 1)
            dve.wait_ge(wT_ps, 1)
            w4 = psB[:, :].rearrange("p (q n two) -> p q n two", q=4, two=2)[:, :, :, 1:2]
            for q in range(4):
                dve.tensor_copy(wT[:, q, :].rearrange("p (n two) -> p n two", two=2),
                                w4[:, q].broadcast_to([P, D, 2])).then_inc(wT_ok, 1)
            dve.wait_ge(p_ps, 1)
            for q in range(4):
                dve.tensor_tensor(zp[:, :].rearrange("p (g q n) -> p q g n", q=4, n=P)[:, q],
                                  psP[:, q, :].rearrange("p (g n) -> p g n", n=P),
                                  k.zT[:, q:TILES:4, :], ALU.mult).then_inc(lnk, 1)
            n[0] += 4
            dve.wait_ge(lnk, n[0])
            link(dve.tensor_copy(zs[:, :], zp[:, :]))
            for g in (1, 3):
                q = slice(g * RANK, (g + 1) * RANK)
                dve.tensor_tensor(zs[q, :], zp[q, :], zs[q, :], ALU.subtract).then_inc(z_fin, 1)

            def step(i, p, j):
                dve.wait_ge(d_ps, i + 1)
                wait(dve, store[p], 16 * j)
                dve.tensor_tensor(outb[p][:, :], psD[p][:, :], k.x[:, i, :], ALU.add).then_inc(o_ok, 1)

            sweep(dve, step, TILES, 0)

        @block.scalar
        def _(act):
            act.wait_ge(done_v, 3)
            act.activation(e[:, :, :], lg[:, :, :], ACT.Exp).then_inc(act_ok, 1)
            act.wait_ge(done_v, 4)
            act.activation(w[:, :, :], u[:, :, :], ACT.Exp, scale=-2.0).then_inc(act_ok, 1)

        @block.sync
        def _(sp):
            def step(i, p, j):
                sp.wait_ge(o_ok, i + 1)
                sp.dma_start(out[i], outb[p][:, :]).then_inc(store[p], 16)

            sweep(sp, step, TILES, 0)
            for p in range(2):
                sp.wait_ge(store[p], 16 * TILES // 2)

        @block.tensor
        def _(pe):
            for t in range(TILES):
                mm = pe.matmul(psA[:, t * EXPERTS:(t + 1) * EXPERTS], k.zT[0:RANK, t, :], k.limesT[:, :],
                               start=True, stop=True)
            mm.then_inc(a_ps, 1)
            pe.wait_ge(done_v, 1)
            pe.transpose(psB[0:2, 0:P], mx2[:, :], k.ident[:, :]).then_inc(a_ps, 1)
            pe.wait_ge(done_v, 2)
            pe.matmul(psA[:, 256:258], ones2[:, :], diag[:, 0:2], start=True, stop=True).then_inc(a_ps, 1)
            pe.wait_ge(done_v, 5)
            for q in range(4):
                mm = pe.transpose(chunk(psB, q), wf[:, 4 * q:4 * q + 4, :].rearrange("p a b -> p (a b)"), k.ident[:, :])
            mm.then_inc(wT_ps, 1)
            pe.wait_ge(wT_ok, 4)
            for t in range(TILES):
                r0 = RANK * (t % 4)
                mm = pe.matmul(psP[:, t % 4, (t // 4) * P:(t // 4 + 1) * P],
                               k.limes4[r0:r0 + EXPERTS, :, :].rearrange("p a b -> p (a b)"),
                               wT[r0:r0 + EXPERTS, t // 4, :], start=True, stop=True)
            mm.then_inc(p_ps, 1)
            pe.wait_ge(z_fin, 2)
            for t in range(TILES):
                if t >= 2:
                    pe.wait_ge(o_ok, t - 1)
                pe.matmul(psD[t % 2][:, :], chunk(zs, t), k.bm_parts[:, :], start=True, stop=True).then_inc(d_ps, 1)


def program(nc, a):
    with ExitStack() as ctx:
        s = Scope(nc, ctx, "all")
        k = Shared()
        k.x = s.sb("x_res", [P, TILES, L])
        k.mv = s.sb("mv", [P, TILES, 2])
        k.rstd = s.sb("rstd", [P, TILES])
        k.rs = Shared()
        k.rs.v, k.rs.ln, k.rs.y, k.rs.t = (s.sb("rs_" + n, [P, TILES]) for n in ("v", "ln", "y", "t"))
        k.rs.v_ok, k.rs.ln_ok, k.rs.y_ok, k.rs.t_ok, k.rs.rstd_ok = (
            s.sem("rs_" + n) for n in ("v_ok", "ln_ok", "y_ok", "t_ok", "rstd_ok"))
        k.passed = s.sem("passed")
        k.xabs = s.sb("xabs", [P, TILES])
        k.ident = s.sb("ident", [P, P])
        k.ident16 = s.sb("ident16", [P, P], BF16)
        k.ones = s.sb("ones", [P, P], BF16)
        k.ind = s.sb("ind", [P, L], BF16)
        k.blk = s.sb("blk", [P, P])
        k.odd = s.sb("odd", [P, 1])
        k.m_round = s.sb("m_round", [P, 1])
        k.m_minus = s.sb("m_minus", [P, 1])
        k.half_ln = s.sb("half_ln", [P, 1])
        k.bias_rows = [s.sb(f"bias_rows{i}", [P, L], BF16) for i in range(3)]
        k.bv2, k.bo2, k.bo1, k.g8 = (s.sb(n, [P, 1]) for n in ("bv2", "bo2", "bo1", "g8"))
        k.wT0 = s.sb("wT0", [P, 4, P])
        k.wq_hi, k.wq_lo, k.wk_hi, k.wk_lo = (s.sb(n, [P, L], F16) for n in ("wq_hi", "wq_lo", "wk_hi", "wk_lo"))
        k.wv_wo = s.sb("wv_wo", [D + 1, HEADS, D + 1])
        k.WT = s.sb("WT", [P, NC, L])
        k.A4 = s.sb("A4", [P, NC, P])
        k.bm_parts = s.sb("bm_parts", [P, L], F16)
        k.limes4 = s.sb("limes4", [P, 4, RANK])
        k.limesT = s.sb("limesT", [RANK, EXPERTS])
        k.ffs = s.sb("ffs", [P, 3])
        k.ffw = s.sb("ffw", [P, 3])
        k.s4, k.sg, k.su, k.su_abs, k.sd = (s.sb(n, [P, TILES]) for n in ("s4", "sg", "su", "su_abs", "sd"))
        setup(nc, a, k)
        with ExitStack() as ctx_ff:
            f = Scope(nc, ctx_ff, "all")
            k.wgT = f.sb("wgT", [P, NC, FF], BF16)
            k.wuT = f.sb("wuT", [P, NC, FF], BF16)
            k.wdT = f.sb("wdT", [P, FFC, L], BF16)
            with ExitStack() as ctx_raw:
                w = Scope(nc, ctx_raw, "all")
                raw = [w.sb("raw_g", [P, FFC, L]), w.sb("raw_u", [P, FFC, L]), w.sb("raw_d", [P, NC, FF])]
                raw_in = [w.sem(f"raw_in{n}") for n in range(3)]
                with nc.Block() as block:
                    @block.gpsimd
                    def _(pool):
                        full = (FFC - 1) * P
                        for n, src in enumerate((a["wg"], a["wu"])):
                            pool.dma_start(raw[n][:, 0:FFC - 1, :],
                                           src[0:full, :].rearrange("(c p) d -> p c d", p=P)).then_inc(raw_in[n], 16)
                            pool.dma_start(raw[n][0:FF - full, FFC - 1, :], src[full:FF, :]).then_inc(raw_in[n], 16)
                        pool.dma_start(raw[2][:, :, :], a["wd"].rearrange("(c p) d -> p c d", p=P)).then_inc(raw_in[2], 16)
                attention0(nc, a, k)
                ternary_weights(nc, a, k, raw, raw_in)
            feed_forward(nc, a, k)
        with ExitStack() as ctx_c:
            c = Scope(nc, ctx_c, "all")
            k.M = c.sb("M", [P, BATCHES, NC, D])
            key_side(nc, a, k)
            query_side(nc, a, k)
        k.zT = s.sb("zT", [P, TILES, P])
        k.Hs = s.sb("Hs", [P, TILES, EXPERTS])
        projection(nc, a, k)
        experts(nc, a, k)


_INS = dict(x="x", ctx_4096="ctx", L0_xattn_Wq="Wq0", L0_xattn_bq="bq0", L0_xattn_Wk="Wk0", L0_xattn_bk="bk0",
            L0_xattn_Wv="Wv0", L0_xattn_bv="bv0", L0_xattn_Wo="Wo0", L0_xattn_bo="bo0", L0_ffn_w_gate="wg",
            L0_ffn_w_up="wu", L0_ffn_w_down="wd", L0_ffn_s_gate="sg", L0_ffn_s_up="su", L0_ffn_s_down="sd",
            L1_xattn_Wq="Wq1", L1_xattn_Wk="Wk1", L1_xattn_Wv="Wv1", L1_xattn_Wo="Wo1", L1_xattn_bo="bo1",
            L1_xattn_g="g1", L1_ffn_W="W1", L1_ffn_b="b1", L1_ffn_A="A1", L1_ffn_Bmat="Bm1", L1_ffn_LiMEs="Li1")


def kernel(**inputs):
    import numpy as _np
    import concourse.bacc as _bacc
    from concourse import mybir as _mybir
    from concourse.bass_utils import run_bass_kernel_spmd as _run

    nc = _bacc.Bacc("TRN2", target_bir_lowering=False, num_devices=1)
    arrays, args = {}, {}
    for name, short in _INS.items():
        v = _np.ascontiguousarray(inputs[name])
        arrays[f"in_{name}_dram"] = v
        args[short] = nc.dram_tensor(f"in_{name}_dram", v.shape, _mybir.dt.from_np(v.dtype), kind="ExternalInput").ap()
    args["out"] = nc.dram_tensor("out_0_dram", (BATCHES, D, L), F32, kind="ExternalOutput").ap()
    program(nc, args)
    r = _run(nc, [arrays], core_ids=[0])
    return r.results[0]["out_0_dram"]
```

```python
import math
from contextlib import ExitStack

import concourse.bass as bass
from concourse import mybir
from concourse.alu_op_type import AluOpType as ALU

F32, F16, BF16 = mybir.dt.float32, mybir.dt.float16, mybir.dt.bfloat16
ACT = mybir.ActivationFunctionType
X = mybir.AxisListType.X

P = 128
D = 64
L = 512
HEADS = L // D
NC = L // P
BATCHES = 32
TILES = BATCHES * D // P
HALF = (slice(0, D), slice(D, P))
FF = 1376
FFC = (FF + P - 1) // P
FFB = [(a, min(a + 512, FF)) for a in range(0, FF, 512)]
RANK, EXPERTS = 32, 8
EPS = 1e-5
ROUND = 12582912.0
SQRT7 = math.sqrt(7.0)
LN_SCALE = 24


def chunk(ap, c, n=P):
    return ap[:, c * n:(c + 1) * n]


def exists(i, n):
    return not isinstance(i, int) or 0 <= i < n


def wait(eng, sem, value):
    if not isinstance(value, int) or value > 0:
        eng.wait_ge(sem, value)


def hold(eng, sem, value, passed):
    if not isinstance(value, int) or value > 0:
        eng.wait_ge(sem, value)
        eng.sem_inc(passed, 1)


def sweep(eng, step, n, tail, head=2):
    for i in range(head):
        step(i, i % 2, i // 2)
    with eng.Fori(head // 2, n // 2 - 1) as j:
        step(2 * j, 0, j)
        step(2 * j + 1, 1, j)
    for i in range(n - 2, n + tail):
        step(i, i % 2, i // 2)


class Shared:
    pass


class Scope:

    def __init__(self, nc, ctx, tag):
        self.nc, self.ctx, self.tag = nc, ctx, tag

    def sb(self, name, shape, dt=F32):
        return self.ctx.enter_context(self.nc.sbuf_tensor(f"{self.tag}_{name}", shape, dt))

    def ps(self, name, shape, dt=F32):
        return self.ctx.enter_context(self.nc.psum_tensor(f"{self.tag}_{name}", shape, dt))

    def sem(self, name):
        return self.ctx.enter_context(self.nc.semaphore(f"{self.tag}_{name}"))

    def block(self):
        return self.ctx.enter_context(self.nc.Block())


def row_stats(dve, k, t, stats, x_ok, st_ok, ag_ok, mv_ok):
    six, two = stats
    hold(dve, x_ok, t + 1, k.passed)
    dve.bn_stats(six[:, :], k.x[:, t, :]).then_inc(st_ok, 1)
    hold(dve, st_ok, t + 1, k.passed)
    hold(dve, mv_ok, t, k.passed)
    dve.bn_aggr(two[:, :], six[:, :]).then_inc(ag_ok, 1)
    hold(dve, ag_ok, t + 1, k.passed)
    dve.tensor_copy(k.mv[:, t, :], two[:, :]).then_inc(mv_ok, 1)


def row_rstd(k, n, start):
    r = k.rs

    def on_vector(dve):
        start(dve)
        dve.tensor_scalar(r.v[:, :], k.mv[:, :, 1], EPS, None, ALU.add).then_inc(r.v_ok, 1)
        dve.wait_ge(r.y_ok, n + 1)
        dve.tensor_tensor(r.t[:, :], r.y[:, :], r.y[:, :], ALU.mult).then_inc(r.t_ok, 1)
        dve.wait_ge(r.t_ok, 3 * n + 1)
        dve.tensor_tensor(r.t[:, :], r.t[:, :], r.v[:, :], ALU.mult).then_inc(r.t_ok, 1)
        dve.wait_ge(r.t_ok, 3 * n + 2)
        dve.tensor_scalar(r.t[:, :], r.t[:, :], -0.5, 1.5, ALU.mult, ALU.add).then_inc(r.t_ok, 1)
        dve.wait_ge(r.t_ok, 3 * n + 3)
        dve.tensor_tensor(k.rstd[:, :], r.y[:, :], r.t[:, :], ALU.mult).then_inc(r.rstd_ok, 1)
        dve.wait_ge(r.rstd_ok, n + 1)

    def on_scalar(act):
        act.wait_ge(r.v_ok, n + 1)
        act.activation(r.ln[:, :], r.v[:, :], ACT.Ln).then_inc(r.ln_ok, 1)
        act.wait_ge(r.ln_ok, n + 1)
        act.activation(r.y[:, :], r.ln[:, :], ACT.Exp, scale=-0.5).then_inc(r.y_ok, 1)

    return on_vector, on_scalar


def setup(nc, a, k):
    with ExitStack() as ctx:
        s = Scope(nc, ctx, "setup")
        wbd = s.sb("wbd", [P, 4, P])
        wdup = s.sb("wdup", [P, 2, NC, P])
        wo1 = s.sb("wo1", [D, L])
        wv1 = s.sb("wv1", [P, NC, D])
        wo1T = s.sb("wo1T", [P, NC, D])
        w_nat = s.sb("w_nat", [P, NC, L])
        brow = s.sb("brow", [1, 3, L])
        bsmall = s.sb("bsmall", [1, 2, D])
        part = s.sb("part", [1, 3, L], BF16)
        rest = s.sb("rest", [1, 3, L])
        bm = s.sb("bm", [P, L])
        stats = s.sb("stats", [P, TILES, 6])
        ps = [s.ps(f"ps{i}", [P, 512]) for i in range(8)]

        zero_ok = s.sem("zero_ok")
        ident_ok = s.sem("ident_ok")
        const_ok = s.sem("const_ok")
        x_in = [s.sem(f"x_in{i}") for i in range(4)]
        w_in = s.sem("w_in")
        stat_ok = s.sem("stat_ok")
        mv_ok = s.sem("mv_ok")
        tr = s.sem("tr")
        out0 = s.sem("out0")
        out1 = s.sem("out1")
        row_ok = s.sem("row_ok")
        vec_x, act_x = row_rstd(k, 0, lambda e: e.wait_ge(mv_ok, TILES))
        block = s.block()
        loads = []

        @block.sync
        def _(sp):
            xv = a["x"].rearrange("(t b) d l -> (b d) t l", b=2)
            g = TILES // 4
            for i in range(4):
                sp.dma_start(k.x[:, g * i:g * i + g, :], xv[:, g * i:g * i + g, :]).then_inc(x_in[i], 16)
            sp.wait_ge(zero_ok, 3)
            for n, w in enumerate((a["Wq0"], a["Wk0"], a["Wv0"], a["Wo0"])):
                for h in range(2):
                    sp.dma_start(wbd[HALF[h], n, h * D:(h + 1) * D], w).then_inc(w_in, 16)
                    loads.append(1)

        @block.scalar
        def _(act):
            act.preload_act_table_set("natural_log_exp_and_others")

            def load(dst, src):
                act.dma_start(dst, src).then_inc(w_in, 16)
                loads.append(1)

            load(bsmall[0:1, 0, :], a["bq0"].unsqueeze(0))
            load(bsmall[0:1, 1, :], a["bk0"].unsqueeze(0))
            load(brow[0:1, 2, :], a["b1"].unsqueeze(0))
            for h in range(2):
                load(k.bv2[HALF[h], :], a["bv0"].unsqueeze(1))
                load(k.bo2[HALF[h], :], a["bo0"].unsqueeze(1))
                load(k.bo1[HALF[h], :], a["bo1"].unsqueeze(1))
                load(k.g8[HALF[h], :], a["g1"].rearrange("a d b -> (a d) b"))
            for n, w in enumerate((a["Wq1"], a["Wk1"])):
                for h in range(2):
                    load(wdup[:, n, :, h * D:(h + 1) * D], w.rearrange("(c p) d -> p c d", p=P))
            load(wv1[:, :, :], a["Wv1"].rearrange("(c p) d -> p c d", p=P))
            load(wo1[:, :], a["Wo1"])
            load(w_nat[:, :, :], a["W1"].rearrange("(c p) d -> p c d", p=P))
            for q in range(4):
                load(k.A4[:, :, q * RANK:(q + 1) * RANK], a["A1"].rearrange("(c p) r -> p c r", p=P))
                load(bm[q * RANK:(q + 1) * RANK, :], a["Bm1"])
                load(k.limes4[q * RANK:q * RANK + EXPERTS, :, :],
                     a["Li1"].unsqueeze(1).broadcast_to([EXPERTS, 4, RANK]))
            with nc.allow_non_contiguous_dma(reason="256 numbers"):
                load(k.limesT[:, :], a["Li1"].rearrange("e r -> r e"))
            for n, w in enumerate((a["sg"], a["su"], a["sd"])):
                load(k.ffs[:, n:n + 1], w.unsqueeze(0).broadcast_to([P, 1]))
            n_in = 16 * (8 + len(loads))
            for n, w in enumerate((k.wq_hi, k.wk_hi)):
                act.wait_ge(tr, 3 + n)
                act.activation(w[:, :], ps[2 + n][:, :], ACT.Copy).then_inc(out1, 1)
            act_x(act)
            for i in range(NC):
                act.wait_ge(tr, 6 + i)
                act.activation(k.WT[:, i, :], ps[(5, 6, 7, 0)[i]][:, :], ACT.Copy).then_inc(out1, 1)

        n_in = 16 * (8 + 3 + 8 + 4 + 3 + 12 + 1 + 3)

        @block.gpsimd
        def _(pool):
            pool.memset(k.ident[:, :], 0.0).then_inc(zero_ok, 1)
            pool.memset(wbd[:, :, :], 0.0).then_inc(zero_ok, 1)
            pool.memset(k.ind[:, :], 0.0).then_inc(zero_ok, 1)
            pool.wait_ge(zero_ok, 3)
            pool.affine_select(out=k.ident[:, :], in_=k.ident[:, :], compare_op=ALU.not_equal, fill=1.0, base=0,
                               pattern=[[-1, P]], channel_multiplier=1).then_inc(ident_ok, 1)
            iv = k.ind[0:32, :].rearrange("p (h d) -> p h d", h=HEADS)
            pool.affine_select(out=iv, in_=iv, compare_op=ALU.not_equal, fill=1.0, base=0,
                               pattern=[[-1, HEADS], [0, D]], channel_multiplier=1).then_inc(ident_ok, 1)

        @block.vector
        def _(dve):
            for buf, value in ((k.ones, 1.0), (k.bias_rows[0], 0.0), (k.bias_rows[1], 0.0), (k.bias_rows[2], 0.0),
                               (k.blk, 0.0), (k.m_round, ROUND), (k.m_minus, -ROUND), (k.half_ln, 0.5 * LN_SCALE * math.log(2.0))):
                ap = buf[:, :] if len(buf.shape) == 2 else buf[:, :, :]
                dve.memset(ap, value).then_inc(const_ok, 1)
            dve.wait_ge(const_ok, 8)
            for h in range(2):
                dve.memset(k.blk[HALF[h], h * D:(h + 1) * D], 1.0).then_inc(const_ok, 1)
            dve.wait_ge(ident_ok, 2)
            dve.tensor_copy(k.ident16[:, :], k.ident[:, :]).then_inc(const_ok, 1)
            dve.tensor_copy(k.ident_h[:, :], k.ident[:, :]).then_inc(const_ok, 1)
            for g in (1, 2):
                dve.tensor_copy(k.ind[32 * g:32 * g + 32, :], k.ind[0:32, :]).then_inc(const_ok, 1)
            dve.tensor_reduce(k.odd[:, :], k.ident[:, :].rearrange("p (n two) -> p two n", two=2)[:, 1, :], X,
                              ALU.add).then_inc(const_ok, 1)
            for t in range(TILES):
                if t % 4 == 0:
                    dve.wait_ge(x_in[t // 4], 16)
                dve.bn_stats(stats[:, t, :], k.x[:, t, :]).then_inc(stat_ok, 1)
            for t in range(TILES):
                dve.wait_ge(stat_ok, t + 1)
                dve.bn_aggr(k.mv[:, t, :], stats[:, t, :]).then_inc(mv_ok, 1)
            vec_x(dve)
            dve.wait_ge(w_in, n_in)
            dve.tensor_scalar(k.g8[:, :], k.g8[:, :], math.sqrt(D), None, ALU.mult).then_inc(row_ok, 1)
            for n in range(2):
                dve.tensor_copy(brow[0:1, n, :].rearrange("p (c d) -> p c d", d=D),
                                bsmall[0:1, n, :].unsqueeze(1).broadcast_to([1, L // D, D])).then_inc(row_ok, 1)
            dve.wait_ge(row_ok, 3)
            dve.tensor_copy(part[:, :, :], brow[:, :, :]).then_inc(row_ok, 1)
            dve.wait_ge(row_ok, 4)
            dve.tensor_tensor(rest[:, :, :], brow[:, :, :], part[:, :, :], ALU.subtract).then_inc(row_ok, 1)
            for n in range(3):
                dve.tensor_copy(k.bias_rows[n][0:1, :], part[0:1, n, :]).then_inc(row_ok, 1)
            dve.wait_ge(row_ok, 8)
            dve.tensor_copy(part[:, :, :], rest[:, :, :]).then_inc(row_ok, 1)
            dve.wait_ge(row_ok, 9)
            for n in range(3):
                dve.tensor_copy(k.bias_rows[n][32:33, :], part[0:1, n, :]).then_inc(row_ok, 1)
                dve.tensor_tensor(k.bias_rows[n][64:65, :], rest[0:1, n, :], part[0:1, n, :],
                                  ALU.subtract).then_inc(row_ok, 1)
            dve.tensor_scalar(bm[:, :], bm[:, :], 16.0 / RANK, None, ALU.mult).then_inc(row_ok, 1)
            dve.wait_ge(row_ok, 16)
            dve.tensor_copy(k.bm_parts[:, :], bm[:, :]).then_inc(row_ok, 1)
            dve.wait_ge(row_ok, 17)
            dve.tensor_tensor(k.bm_parts[D:P, :], bm[D:P, :], k.bm_parts[D:P, :], ALU.subtract).then_inc(row_ok, 1)
            dve.wait_ge(tr, 1)
            dve.tensor_copy(k.wT0[:, :, :], ps[0][:, :].rearrange("p (n m) -> p n m", n=4)).then_inc(out0, 1)
            dve.wait_ge(tr, 2)
            dve.tensor_copy(wo1T[:, :, :], ps[1][:, 0:NC * D].rearrange("p (n m) -> p n m", n=NC)).then_inc(out0, 1)
            for n, (hi, lo) in enumerate(((k.wq_hi, k.wq_lo), (k.wk_hi, k.wk_lo))):
                dve.wait_ge(out1, n + 1)
                dve.tensor_tensor(lo[:, :], ps[2 + n][:, :], hi[:, :], ALU.subtract).then_inc(out0, 1)
            dve.wait_ge(tr, 5)
            for r in range(2):
                for rows in HALF:
                    dve.tensor_scalar(k.wv_wo[rows, r:HEADS:2, :],
                                      ps[(4, 1)[r]][0:D, :].rearrange("p (h m) -> p h m", h=HEADS)[:, r:HEADS:2, :],
                                      D ** -0.5, None, ALU.mult).then_inc(out0, 1)

        @block.tensor
        def _(pe):
            pe.wait_ge(ident_ok, 1)
            pe.wait_ge(w_in, n_in)
            for n in range(4):
                mm = pe.transpose(chunk(ps[0], n), wbd[:, n, :], k.ident[:, :])
            mm.then_inc(tr, 1)
            for c in range(NC):
                mm = pe.transpose(ps[1][:, c * D:(c + 1) * D], chunk(wo1, c), k.ident[0:D, 0:D])
            mm.then_inc(tr, 1)
            for n in range(2):
                for c in range(NC):
                    mm = pe.transpose(chunk(ps[2 + n], c), wdup[:, n, c, :], k.ident[:, :])
                mm.then_inc(tr, 1)
            pe.wait_ge(out0, 2)
            for h in range(HEADS):
                r = HALF[h % 2]
                mm = pe.matmul(ps[(4, 1)[h % 2]][0:D, h * D:(h + 1) * D], wv1[r, h // 2, :], wo1T[r, h // 2, :],
                               start=True, stop=True)
            mm.then_inc(tr, 1)
            for i in range(NC):
                if i == 3:
                    pe.wait_ge(out0, 1)
                for o in range(NC):
                    mm = pe.transpose(chunk(ps[(5, 6, 7, 0)[i]], o), w_nat[:, o, i * P:(i + 1) * P], k.ident[:, :])
                mm.then_inc(tr, 1)


def attention0(nc, a, k):
    with ExitStack() as ctx:
        s = Scope(nc, ctx, "att0")
        ctx_n = [s.sb(f"ctx_n{p}", [P, L]) for p in range(2)]
        ctx_h = [s.sb(f"ctx_h{p}", [P, 2, NC, D]) for p in range(2)]
        xn = [s.sb(f"xn{p}", [P, L]) for p in range(2)]
        q_t = s.sb("q_t", [P, L])
        k_t = s.sb("k_t", [P, 2, NC, 2, D])
        v_h = [s.sb(f"v_h{p}", [P, 2, NC, 2, D]) for p in range(2)]
        mx = s.sb("mx", [P, HEADS])
        sh = s.sb("sh", [P, L])
        ex = s.sb("ex", [P, L])
        sm = s.sb("sm", [P, HEADS])
        rs = s.sb("rs", [P, HEADS])
        pn = s.sb("pn", [P, L])
        wp = s.sb("wp", [P, L])
        dump = s.sb("dump", [P, L])
        stats = (s.sb("stats", [P, 6]), s.sb("mean_var", [P, 2]))
        ag_ok = s.sem("ag_ok")
        psQ, psK, psV, psS, psW, psO = (s.ps("ps" + n, [P, 512]) for n in "QKVSWO")
        (zero_ok, xn_ok, q_ps, k_ps, v_ps, s_ps, w_ps, o_ps, q_ok, k_ok, v_ok, mx_ok, sh_ok, ex_ok, sm_ok, rs_ok, pn_ok,
         wp_ok, x_ok, st_ok, mv_ok, ab_ok) = (s.sem(n) for n in (
             "zero_ok xn_ok q_ps k_ps v_ps s_ps w_ps o_ps q_ok k_ok v_ok mx_ok sh_ok ex_ok sm_ok rs_ok pn_ok "
             "wp_ok x_ok st_ok mv_ok ab_ok").split())
        ctx_in = [s.sem(f"ctx_in{p}") for p in range(2)]
        block = s.block()
        nat = a["ctx"].rearrange("(t b) d l -> t (b d) l", b=2)
        par = a["ctx"].rearrange("(t b) d (c r k) -> t r d b c k", b=2, r=2, k=D)

        @block.sync
        def _(sp):
            def step(i, p, j):
                wait(sp, v_ps, i - 1)
                sp.dma_start(ctx_n[p][:, :], nat[i]).then_inc(ctx_in[p], 16)
                for r in range(2):
                    for b in range(2):
                        sp.dma_start(ctx_h[p][HALF[r], b], par[i, r, :, b]).then_inc(ctx_in[p], 16)

            sweep(sp, step, TILES, 0)

        @block.gpsimd
        def _(pool):
            for buf in (k_t, v_h[0], v_h[1]):
                pool.memset(buf[:, :, :, :, :], 0.0).then_inc(zero_ok, 1)

            def step(i, p, j):
                pool.wait_ge(rs_ok, i + 1)
                pool.tensor_tensor(pn[:, :].rearrange("p (h e) -> p h e", h=HEADS),
                                   ex[:, :].rearrange("p (h e) -> p h e", h=HEADS),
                                   rs[:, :].unsqueeze(2).broadcast_to([P, HEADS, D]), ALU.mult).then_inc(pn_ok, 1)

            sweep(pool, step, TILES, 0)

        @block.vector
        def _(dve):
            def normed(i, p):
                dve.tensor_scalar(xn[p][:, :], k.x[:, i, :], k.mv[:, i, 0:1], k.rstd[:, bass.ds(i, 1)], ALU.subtract,
                                  ALU.mult).then_inc(xn_ok, 1)

            def step(i, p, j):
                t = i - 1
                if exists(t, TILES):
                    dve.wait_ge(s_ps, t + 1)
                    s3 = psS[:, :].rearrange("p (h e) -> p h e", h=HEADS)
                    dve.tensor_reduce(mx[:, :], s3, X, ALU.max).then_inc(mx_ok, 1)
                    dve.wait_ge(mx_ok, t + 1)
                    dve.tensor_tensor(sh[:, :].rearrange("p (h e) -> p h e", h=HEADS), s3,
                                      mx[:, :].unsqueeze(2).broadcast_to([P, HEADS, D]), ALU.subtract).then_inc(sh_ok, 1)
                if exists(i, TILES):
                    dve.wait_ge(k_ps, i + 1)
                    wait(dve, k_ok, 2 * i)
                    dve.wait_ge(zero_ok, 3)
                    for r in range(2):
                        dve.tensor_copy(k_t[HALF[r], :, :, r, :],
                                        psK[HALF[r], :].rearrange("p (c b e) -> p b c e", b=2, e=D)).then_inc(k_ok, 1)
                if exists(t, TILES):
                    dve.wait_ge(ex_ok, t + 1)
                    dve.tensor_reduce(sm[:, :], ex[:, :].rearrange("p (h e) -> p h e", h=HEADS), X,
                                      ALU.add).then_inc(sm_ok, 1)
                    dve.wait_ge(sm_ok, t + 1)
                    dve.reciprocal(rs[:, :], sm[:, :]).then_inc(rs_ok, 1)
                if exists(i + 1, TILES):
                    normed(i + 1, 1 - p)
                if exists(t, TILES):
                    dve.wait_ge(o_ps, t + 1)
                    dve.scalar_tensor_tensor(out=k.x[:, t, :], in0=psO[:, :], scalar=k.bo2[:, :], in1=k.x[:, t, :],
                                             op0=ALU.add, op1=ALU.add).then_inc(x_ok, 1)
                    row_stats(dve, k, t, stats, x_ok, st_ok, ag_ok, mv_ok)

            normed(0, 0)
            sweep(dve, step, TILES, 1)

        @block.scalar
        def _(act):
            def step(i, p, j):
                t = i - 1
                if exists(t, TILES):
                    act.wait_ge(sh_ok, t + 1)
                    wait(act, pn_ok, t)
                    act.activation(ex[:, :], sh[:, :], ACT.Exp, scale=D ** -0.5).then_inc(ex_ok, 1)
                if exists(i, TILES):
                    act.wait_ge(q_ps, i + 1)
                    act.activation(q_t[:, :], psQ[:, :], ACT.Copy).then_inc(q_ok, 1)
                    act.wait_ge(v_ps, i + 1)
                    act.wait_ge(zero_ok, 3)
                    for r in range(2):
                        act.activation(v_h[p][HALF[r], :, :, r, :],
                                       psV[HALF[r], :].rearrange("p (b c e) -> p b c e", b=2, e=D), ACT.Identity,
                                       bias=k.bv2[HALF[r], :]).then_inc(v_ok, 1)
                if exists(t, TILES):
                    act.wait_ge(w_ps, t + 1)
                    act.activation(wp[:, :], psW[:, :], ACT.Copy).then_inc(wp_ok, 1)
                    act.wait_ge(mv_ok, t + 1)
                    hold(act, ab_ok, t, k.passed)
                    act.activation(dump[:, :], k.x[:, t, :], ACT.Abs, scale=-1.0, bias=k.mv[:, t, 0:1],
                                   accum_out=k.xabs[:, bass.ds(t, 1)]).then_inc(ab_ok, 1)

            sweep(act, step, TILES, 1)

        @block.tensor
        def _(pe):
            def step(i, p, j):
                t = i - 1
                if exists(i, TILES):
                    pe.wait_ge(xn_ok, i + 1)
                    wait(pe, q_ok, i)
                    pe.matmul(psQ[:, :], k.ones[:, :], k.bias_rows[0][:, :], start=True, stop=True)
                    for c in range(NC):
                        mm = pe.matmul(chunk(psQ, c), chunk(xn[p], c), k.wT0[:, 0, :], start=False, stop=True,
                                       skip_group_check=True)
                    mm.then_inc(q_ps, 1)
                    pe.wait_ge(ctx_in[p], 80 * j + 80)
                    wait(pe, k_ok, 2 * i)
                    pe.matmul(psK[:, :], k.ones[:, :], k.bias_rows[1][:, :], start=True, stop=True)
                    for c in range(NC):
                        mm = pe.matmul(chunk(psK, c), chunk(ctx_n[p], c), k.wT0[:, 1, :], start=False,
                                       stop=True, skip_group_check=True)
                    mm.then_inc(k_ps, 1)
                    wait(pe, v_ok, 2 * i)
                    pe.matmul(psV[:, :], k.wT0[:, 2, :], ctx_h[p][:, :, :, :].rearrange("p b c k -> p (b c k)"),
                              start=True, stop=True).then_inc(v_ps, 1)
                if exists(t, TILES):
                    pe.wait_ge(pn_ok, t + 1)
                    for c in range(NC):
                        mm = pe.matmul(chunk(psW, c), chunk(pn, c), k.wT0[:, 3, :], start=True, stop=True)
                    mm.then_inc(w_ps, 1)
                if exists(i, TILES):
                    pe.wait_ge(q_ok, i + 1)
                    pe.wait_ge(k_ok, 2 * i + 2)
                    wait(pe, sh_ok, i)
                    for c in range(NC):
                        for b in range(2):
                            mm = pe.matmul(psS[HALF[b], c * P:(c + 1) * P], q_t[:, c * P + b * D:c * P + b * D + D],
                                           k_t[:, b, c, :, :], start=True, stop=True)
                    mm.then_inc(s_ps, 1)
                if exists(t, TILES):
                    pe.wait_ge(wp_ok, t + 1)
                    pe.wait_ge(v_ok, 2 * t + 2)
                    wait(pe, x_ok, t)
                    for c in range(NC):
                        for b in range(2):
                            mm = pe.matmul(psO[HALF[b], c * P:(c + 1) * P], wp[:, c * P + b * D:c * P + b * D + D],
                                           v_h[1 - p][:, b, c, :, :], start=True, stop=True)
                    mm.then_inc(o_ps, 1)

            sweep(pe, step, TILES, 1)


def ternary_weights(nc, a, k, raw, raw_in):
    with ExitStack() as ctx:
        s = Scope(nc, ctx, "tern")
        dump = s.sb("dumpw", [P, FFC * L], BF16)
        asum = s.sb("asum", [P, 3])
        mean = s.sb("mean", [P, 3])
        den = s.sb("den", [P, 3])
        inv = s.sb("inv", [P, 3])
        t0 = s.sb("t0", [P, TILES])
        beta = s.sb("beta", [P, TILES])
        ones32 = s.sb("ones32", [P, P])
        psM = s.ps("psM", [P, 512])
        psT = [s.ps(f"psT{i}", [P, 512]) for i in range(6)]
        (abs_ok, pad_ok, sum_ps, mean_ok, den_ok, inv_ok, q1_ok, q2_ok, t_ps, ev_v, ev_a, sc_ok) = (s.sem(n) for n in (
            "abs_ok pad_ok sum_ps mean_ok den_ok inv_ok q1_ok q2_ok t_ps ev_v ev_a sc_ok").split())
        vec_x, act_x = row_rstd(k, 1, lambda e: None)
        block = s.block()
        flat = [raw[0][:, :, :].rearrange("p a b -> p (a b)"), raw[1][:, :, :].rearrange("p a b -> p (a b)"),
                raw[2][:, :, :].rearrange("p a b -> p (a b)")]
        groups = []
        for n, dst in ((0, k.wgT), (1, k.wuT)):
            for c in range(NC):
                for f in range(0, FFC, 4):
                    js = range(f, min(f + 4, FFC))
                    blocks = [(raw[n][0:min(P, FF - j * P), j, c * P:(c + 1) * P], (j - f) * P, min(P, FF - j * P))
                              for j in js]
                    width = min(FF, (f + 4) * P) - f * P
                    groups.append((n, blocks, P, dst[:, c, f * P:f * P + width], width))
        for j in range(FFC):
            rows = min(P, FF - j * P)
            blocks = [(raw[2][:, c, j * P:j * P + rows], c * P, P) for c in range(NC)]
            groups.append((2, blocks, rows, k.wdT[0:rows, j, :], L))

        @block.gpsimd
        def _(pool):
            for n in range(3):
                pool.wait_ge(inv_ok, 1)
                pool.tensor_scalar(flat[n], flat[n], inv[:, n:n + 1], ROUND, ALU.mult, ALU.add).then_inc(q1_ok, 1)

        @block.scalar
        def _(act):
            act.wait_ge(pad_ok, 2)
            for n in range(3):
                act.wait_ge(raw_in[n], 32 if n < 2 else 16)
                wait(act, abs_ok, n)
                act.activation(dump[:, 0:flat[n].shape[1]], flat[n], ACT.Abs, accum_out=asum[:, n:n + 1]).then_inc(abs_ok, 1)
            act_x(act)
            for g, (n, blocks, rows, dst, width) in enumerate(groups):
                if g % 2:
                    act.wait_ge(t_ps, g + 1)
                    act.activation(dst, psT[g % 6][0:rows, 0:width], ACT.Identity,
                                   bias=k.m_minus[0:rows, :]).then_inc(ev_a, 1)

        @block.tensor
        def _(pe):
            pe.wait_ge(abs_ok, 3)
            pe.wait_ge(pad_ok, 3)
            pe.matmul(psM[:, 0:3], ones32[:, :], asum[:, :], start=True, stop=True).then_inc(sum_ps, 1)
            for g, (n, blocks, rows, dst, width) in enumerate(groups):
                pe.wait_ge(q2_ok, n + 1)
                if g >= 6:
                    pe.wait_ge(ev_a if g % 2 else ev_v, (g - 6) // 2 + 1)
                for src, at, wide in blocks:
                    mm = pe.transpose(psT[g % 6][0:rows, at:at + wide], src, k.ident[0:src.shape[0], 0:src.shape[0]])
                mm.then_inc(t_ps, 1)

        @block.vector
        def _(dve):
            for n in range(2):
                dve.memset(raw[n][FF - (FFC - 1) * P:P, FFC - 1, :], 0.0).then_inc(pad_ok, 1)
            dve.memset(ones32[:, :], 1.0).then_inc(pad_ok, 1)
            vec_x(dve)
            dve.wait_ge(sum_ps, 1)
            dve.tensor_scalar(mean[:, :], psM[:, 0:3], 1.0 / (FF * L), None, ALU.mult).then_inc(mean_ok, 1)
            dve.wait_ge(mean_ok, 1)
            dve.tensor_scalar(den[:, :], mean[:, :], EPS, None, ALU.add).then_inc(den_ok, 1)
            dve.wait_ge(den_ok, 1)
            dve.reciprocal(inv[:, :], den[:, :]).then_inc(inv_ok, 1)
            n = [0]

            def link(ins):
                n[0] += 1
                ins.then_inc(sc_ok, 1)
                dve.wait_ge(sc_ok, n[0])

            w = k.ffw
            link(dve.tensor_tensor(w[:, :], mean[:, :], k.ffs[:, :], ALU.mult))
            link(dve.tensor_tensor(t0[:, :], k.xabs[:, :], k.rstd[:, :], ALU.mult))
            link(dve.tensor_scalar(beta[:, :], t0[:, :], 1.0 / L, None, ALU.mult))
            link(dve.tensor_scalar(t0[:, :], beta[:, :], EPS, None, ALU.add))
            link(dve.reciprocal(k.s4[:, :], t0[:, :]))
            link(dve.scalar_tensor_tensor(out=k.s4[:, :], in0=k.s4[:, :], scalar=SQRT7, in1=k.rstd[:, :], op0=ALU.mult,
                                          op1=ALU.mult))
            link(dve.tensor_scalar(k.sg[:, :], beta[:, :], w[:, 0:1], None, ALU.mult))
            link(dve.tensor_scalar(k.su[:, :], beta[:, :], w[:, 1:2], None, ALU.mult))
            link(dve.tensor_scalar(t0[:, :], k.su[:, :], -1.0, None, ALU.mult))
            link(dve.tensor_tensor(k.su_abs[:, :], k.su[:, :], t0[:, :], ALU.max))
            link(dve.tensor_scalar(k.sd[:, :], k.su_abs[:, :], w[:, 2:3], 1.0 / 127.0, ALU.mult, ALU.mult))
            link(dve.tensor_scalar(k.su[:, :], k.su[:, :], 127.0, None, ALU.mult))
            for m in range(3):
                dve.wait_ge(q1_ok, m + 1)
                dve.tensor_scalar(flat[m], flat[m], ROUND + 1.0, ROUND - 1.0, ALU.min, ALU.max).then_inc(q2_ok, 1)
            for g, (m, blocks, rows, dst, width) in enumerate(groups):
                if g % 2 == 0:
                    dve.wait_ge(t_ps, g + 1)
                    dve.tensor_scalar(dst, psT[g % 6][0:rows, 0:width], ROUND, None, ALU.subtract).then_inc(ev_v, 1)


def feed_forward(nc, a, k):
    with ExitStack() as ctx:
        s = Scope(nc, ctx, "ff")
        y = s.sb("y", [P, L])
        yr = [s.sb(f"yr{p}", [P, L]) for p in range(2)]
        xq = [s.sb(f"xq{p}", [P, L], BF16) for p in range(2)]
        r1 = [s.sb(f"r1_{p}", [P, 512]) for p in range(2)]
        r2 = [s.sb(f"r2_{p}", [P, 512]) for p in range(2)]
        h = s.sb("h", [P, FF])
        hr = s.sb("hr", [P, FF])
        hq = s.sb("hq", [P, FFC, P], BF16)
        gm = s.sb("gm", [P, 1])
        gd = s.sb("gd", [P, 1])
        gi = s.sb("gi", [P, 1])
        qs = s.sb("qs", [P, 1])
        os_ = [s.sb(f"os{p}", [P, 1]) for p in range(2)]
        stats = (s.sb("stats", [P, 6]), s.sb("mean_var", [P, 2]))
        ag_ok = s.sem("ag_ok")
        psX = s.ps("psX", [P, 512])
        psG = [s.ps(f"psG{i}", [P, 512]) for i in range(2)]
        psU = [s.ps(f"psU{i}", [P, 512]) for i in range(2)]
        psT = [s.ps(f"psT{i}", [P, 512]) for i in range(2)]
        psD = s.ps("psD", [P, 512])
        (y_ok, yr_ok, x_ps, xq_ok, g_ps, u_ps, r1_ok, r2_ok, h_ok, gm_ok, gd_ok, gi_ok, qs_ok, os_ok, hr_ok, t_ps, hq_a,
         hq_v, d_ps, x_ok, st_ok, mv_ok) = (s.sem(n) for n in (
             "y_ok yr_ok x_ps xq_ok g_ps u_ps r1_ok r2_ok h_ok gm_ok gd_ok gi_ok qs_ok os_ok hr_ok t_ps hq_a "
             "hq_v d_ps x_ok st_ok mv_ok").split())
        block = s.block()
        NB = len(FFB)
        TG = [range(f, min(f + 4, FFC)) for f in range(0, FFC, 4)]
        NG = len(TG)

        @block.vector
        def _(dve):
            def quantise(i, p):
                wait(dve, yr_ok, i)
                dve.tensor_scalar(y[:, :], k.x[:, i, :], k.mv[:, i, 0:1], k.s4[:, bass.ds(i, 1)], ALU.subtract,
                                  ALU.mult).then_inc(y_ok, 1)
                dve.wait_ge(y_ok, i + 1)
                wait(dve, x_ps, i - 1)
                dve.tensor_scalar(yr[p][:, :], y[:, :], ROUND, ROUND + 7.0, ALU.add, ALU.min).then_inc(yr_ok, 1)

            def take_x(i, p):
                dve.wait_ge(x_ps, i + 1)
                dve.tensor_scalar(xq[p][:, :], psX[:, :], ROUND, -8.0, ALU.subtract, ALU.max).then_inc(xq_ok, 1)

            def step(i, p, j):
                t = i - 1
                if exists(i, TILES):
                    for n, (f0, f1) in enumerate(FFB):
                        dve.wait_ge(r2_ok, NB * i + n + 1)
                        dve.wait_ge(u_ps, NB * i + n + 1)
                        if n == 0:
                            wait(dve, hr_ok, i)
                        q = (NB * p + n) % 2
                        dve.tensor_tensor(h[:, f0:f1], psU[q][:, 0:f1 - f0], r2[q][:, 0:f1 - f0],
                                          ALU.mult).then_inc(h_ok, 1)
                if exists(i + 1, TILES):
                    take_x(i + 1, 1 - p)
                if exists(t, TILES):
                    for n in (1, 2):
                        js = TG[n]
                        w = P * len(js)
                        dve.wait_ge(t_ps, NG * t + n + 1)
                        if n == 1:
                            dve.tensor_scalar(hq[:, js[0]:js[0] + 4, :].rearrange("p a b -> p (a b)"),
                                              psT[(NG * (1 - p) + n) % 2][:, 0:w], ROUND, None, ALU.subtract).then_inc(hq_v, 1)
                        else:
                            q = psT[(NG * (1 - p) + n) % 2]
                            dve.tensor_scalar(hq[:, js[0]:js[0] + 2, :].rearrange("p a b -> p (a b)"), q[:, 0:2 * P],
                                              ROUND, None, ALU.subtract).then_inc(hq_v, 1)
                            last = FF - (FFC - 1) * P
                            dve.tensor_scalar(hq[0:last, FFC - 1, :], q[0:last, 2 * P:3 * P], ROUND, None,
                                              ALU.subtract).then_inc(hq_v, 1)
                if exists(i, TILES):
                    dve.wait_ge(h_ok, NB * i + NB)
                    dve.tensor_reduce(gm[:, :], h[:, :], X, ALU.max, apply_absolute_value=True).then_inc(gm_ok, 1)
                    dve.wait_ge(gm_ok, i + 1)
                    dve.tensor_scalar(gd[:, :], gm[:, :], k.su_abs[:, bass.ds(i, 1)], EPS, ALU.mult, ALU.add).then_inc(gd_ok, 1)
                    wait(dve, x_ok, i - 1)
                    dve.tensor_scalar(os_[p][:, :], gm[:, :], k.sd[:, bass.ds(i, 1)], None, ALU.mult).then_inc(os_ok, 1)
                    dve.wait_ge(gd_ok, i + 1)
                    dve.reciprocal(gi[:, :], gd[:, :]).then_inc(gi_ok, 1)
                    dve.wait_ge(gi_ok, i + 1)
                    dve.tensor_scalar(qs[:, :], gi[:, :], k.su[:, bass.ds(i, 1)], None, ALU.mult).then_inc(qs_ok, 1)
                if exists(i + 2, TILES):
                    quantise(i + 2, p)
                if exists(t, TILES):
                    dve.wait_ge(d_ps, t + 1)
                    dve.wait_ge(os_ok, t + 1)
                    dve.scalar_tensor_tensor(out=k.x[:, t, :], in0=psD[:, :], scalar=os_[1 - p][:, :],
                                             in1=k.x[:, t, :], op0=ALU.mult, op1=ALU.add).then_inc(x_ok, 1)
                    row_stats(dve, k, t, stats, x_ok, st_ok, ag_ok, mv_ok)

            quantise(0, 0)
            quantise(1, 1)
            take_x(0, 0)
            sweep(dve, step, TILES, 1)

        @block.scalar
        def _(act):
            def step(i, p, j):
                t = i - 1
                if exists(i, TILES):
                    for n, (f0, f1) in enumerate(FFB):
                        q = (NB * p + n) % 2
                        hold(act, g_ps, NB * i + n + 1, k.passed)
                        act.activation(r1[q][:, 0:f1 - f0], psG[q][:, 0:f1 - f0], ACT.Relu,
                                       scale=k.sg[:, bass.ds(i, 1)]).then_inc(r1_ok, 1)
                        act.wait_ge(r1_ok, NB * i + n + 1)
                        wait(act, h_ok, NB * i + n - 1)
                        act.activation(r2[q][:, 0:f1 - f0], r1[q][:, 0:f1 - f0], ACT.Square).then_inc(r2_ok, 1)
                if exists(t, TILES):
                    act.wait_ge(t_ps, NG * t + 1)
                    act.activation(hq[:, 0:4, :].rearrange("p a b -> p (a b)"), psT[(NG * (1 - p)) % 2][:, :],
                                   ACT.Identity, bias=k.m_minus[:, :]).then_inc(hq_a, 1)
                if exists(i, TILES):
                    act.wait_ge(qs_ok, i + 1)
                    wait(act, t_ps, NG * i)
                    act.activation(hr[:, :], h[:, :], ACT.Identity, scale=qs[:, :],
                                   bias=k.m_round[:, :]).then_inc(hr_ok, 1)

            sweep(act, step, TILES, 1)

        @block.tensor
        def _(pe):
            def x_up(i, p):
                pe.wait_ge(yr_ok, i + 1)
                wait(pe, xq_ok, i)
                for c in range(NC):
                    mm = pe.transpose(chunk(psX, c), chunk(yr[p], c), k.ident[:, :])
                mm.then_inc(x_ps, 1)

            def step(i, p, j):
                t = i - 1
                if exists(i, TILES):
                    pe.wait_ge(xq_ok, i + 1)
                    for n, (f0, f1) in enumerate(FFB):
                        q = (NB * p + n) % 2
                        wait(pe, r1_ok, NB * i + n - 1)
                        for c in range(NC):
                            mm = pe.matmul(psG[q][:, 0:f1 - f0], chunk(xq[p], c), k.wgT[:, c, f0:f1], start=c == 0,
                                           stop=c == NC - 1)
                        mm.then_inc(g_ps, 1)
                        wait(pe, h_ok, NB * i + n - 1)
                        for c in range(NC):
                            mm = pe.matmul(psU[q][:, 0:f1 - f0], chunk(xq[p], c), k.wuT[:, c, f0:f1], start=c == 0,
                                           stop=c == NC - 1)
                        mm.then_inc(u_ps, 1)
                if exists(i + 1, TILES):
                    x_up(i + 1, 1 - p)
                if exists(t, TILES):
                    pe.wait_ge(hr_ok, t + 1)
                    for n, js in enumerate(TG):
                        if n == 0:
                            wait(pe, hq_v, 3 * t - 2)
                        elif n == 1:
                            wait(pe, hq_v, 3 * t)
                        else:
                            pe.wait_ge(hq_a, t + 1)
                        for m in js:
                            w = min(P, FF - m * P)
                            mm = pe.transpose(psT[(NG * (1 - p) + n) % 2][0:w, (m - js[0]) * P:(m - js[0] + 1) * P],
                                              hr[:, m * P:m * P + w], k.ident[:, :])
                        mm.then_inc(t_ps, 1)
                    wait(pe, x_ok, t)
                    pe.wait_ge(hq_a, t + 1)
                    pe.wait_ge(hq_v, 3 * t + 3)
                    for m in range(FFC):
                        w = min(P, FF - m * P)
                        mm = pe.matmul(psD[:, :], hq[0:w, m, :], k.wdT[0:w, m, :], start=m == 0, stop=m == FFC - 1)
                    mm.then_inc(d_ps, 1)

            x_up(0, 0)
            sweep(pe, step, TILES, 1)


def split_shift(dve, m, part, rest, sems, n):
    p_ok, r_ok = sems
    w = m.shape[2]
    dve.tensor_scalar(part[:, :, 0:w], m, -1.0, None, ALU.mult).then_inc(p_ok, 1)
    dve.wait_ge(p_ok, 3 * n + 1)
    dve.scalar_tensor_tensor(out=rest, in0=m, scalar=-1.0, in1=part[:, :, 0:w], op0=ALU.mult,
                             op1=ALU.subtract).then_inc(r_ok, 1)
    dve.wait_ge(r_ok, n + 1)
    dve.tensor_copy(part[:, :, 32:32 + w], rest).then_inc(p_ok, 1)
    dve.wait_ge(p_ok, 3 * n + 2)
    dve.tensor_tensor(part[:, :, 64:64 + w], rest, part[:, :, 32:32 + w], ALU.subtract).then_inc(p_ok, 1)


def key_side(nc, a, k):
    with ExitStack() as ctx:
        s = Scope(nc, ctx, "keys")
        cf = s.sb("cf", [P, L])
        cs = [s.sb(f"cs{h}", [P, L], F16) for h in range(2)]
        cT = [s.sb(f"cT{h}", [P, NC, P], F16) for h in range(2)]
        mk = s.sb("mk", [P, NC])
        ek = [s.sb(f"ek{h}", [P, NC, L]) for h in range(2)]
        le = [s.sb(f"le{h}", [P, NC]) for h in range(2)]
        e_hi = s.sb("e_hi", [P, NC, L], F16)
        e_lo = s.sb("e_lo", [P, NC, L], F16)
        gT = s.sb("gT", [P, L])
        rl = [s.sb(f"rl{h}", [P, NC]) for h in range(2)]
        psC = s.ps("psC", [P, NC, P], F16)
        psK = [s.ps(f"psK{i}", [P, 512]) for i in range(2)]
        psT = [s.ps(f"psT{i}", [P, 512]) for i in range(2)]
        psG = s.ps("psG", [P, 512])
        psM = s.ps("psM", [P, NC, D])
        (c_in, hi_ok, lo_ok, c_ps, cT_ok, k_ps, mk_ok, ek_ok, t_ps, ehi_ok, elo_ok, g_ps, gT_ok, m_ps, rl_ok,
         M_ok) = (s.sem(n) for n in (
             "c_in hi_ok lo_ok c_ps cT_ok k_ps mk_ok ek_ok t_ps ehi_ok elo_ok g_ps gT_ok m_ps rl_ok M_ok").split())
        block = s.block()
        nat = a["ctx"].rearrange("(t b) d l -> t (b d) l", b=2)

        @block.sync
        def _(sp):
            def step(t, p, j):
                wait(sp, lo_ok, 2 * t)
                sp.dma_start(cf[:, :], nat[t]).then_inc(c_in, 16)

            sweep(sp, step, TILES, 0)

        @block.gpsimd
        def _(pool):
            def step(b, h, t):
                hold(pool, c_in, 16 * t + 16, k.passed)
                r = HALF[h]
                hold(pool, k_ps, NC * (b - 1), k.passed)
                hold(pool, c_ps, b - 1, k.passed)
                pool.tensor_scalar(cs[h][r, :], cf[r, :], 1.0, 0.0, ALU.mult, ALU.add).then_inc(hi_ok, 1)

            sweep(pool, step, BATCHES, 0)

        @block.vector
        def _(dve):
            def low(b, h):
                dve.wait_ge(hi_ok, b + 1)
                dve.tensor_tensor(cs[h][HALF[1 - h], :], cf[HALF[h], :], cs[h][HALF[h], :],
                                  ALU.subtract).then_inc(lo_ok, 1)

            def keys_max(b, c):
                dve.wait_ge(k_ps, NC * b + c + 1)
                wait(dve, ek_ok, NC * (b - 1) + c + 1)
                dve.tensor_reduce(mk[:, c:c + 1], psK[c % 2][:, :], X, ALU.max, negate=True).then_inc(mk_ok, 1)

            def exp_low(b, j):
                dve.wait_ge(ehi_ok, NC * b + j + 1)
                wait(dve, g_ps, NC * (b - 1) + j + 1)
                dve.tensor_tensor(e_lo[:, j, :], psT[j % 2][:, :], e_hi[:, j, :], ALU.subtract).then_inc(elo_ok, 1)

            def sums(b, h):
                dve.wait_ge(ek_ok, NC * b + NC)
                wait(dve, M_ok, b - 1)
                dve.reciprocal(rl[h][:, :], le[h][:, :]).then_inc(rl_ok, 1)

            def matrix(b, h):
                dve.wait_ge(rl_ok, b + 1)
                dve.wait_ge(m_ps, b + 1)
                dve.tensor_tensor(k.M[:, b, :, :], psM[:, :, :], rl[h][:, :].unsqueeze(2).broadcast_to([P, NC, D]),
                                  ALU.mult).then_inc(M_ok, 1)

            def step(b, h, t):
                for c in range(NC):
                    if exists(b + 1 + (c + 1) // NC, BATCHES):
                        keys_max(b + 1 + (c + 1) // NC, (c + 1) % NC)
                    if exists(b, BATCHES):
                        exp_low(b, c)
                    if c == 0 and exists(b, BATCHES):
                        sums(b, h)
                    if c == 1 and exists(b + 2, BATCHES):
                        low(b + 2, h)
                    if c == 2 and exists(b - 1, BATCHES):
                        matrix(b - 1, 1 - h)

            low(0, 0)
            low(1, 1)
            for c in range(NC + 1):
                keys_max(c // NC, c % NC)
            sweep(dve, step, BATCHES, 1)

        @block.scalar
        def _(act):
            def transposed(b, h):
                act.wait_ge(c_ps, b + 1)
                wait(act, g_ps, NC * (b - 1))
                act.activation(cT[h][:, :, :], psC[:, :, :], ACT.Copy).then_inc(cT_ok, 1)

            def exponentials(b, h, c):
                act.wait_ge(mk_ok, NC * b + c + 1)
                wait(act, t_ps, NC * (b - 1))
                wait(act, rl_ok, b - 1)
                act.activation(ek[h][:, c, :], psK[c % 2][:, :], ACT.Exp, bias=mk[:, c:c + 1],
                               accum_out=le[h][:, c:c + 1]).then_inc(ek_ok, 1)

            def step(b, h, t):
                for c in range(NC):
                    if exists(b, BATCHES):
                        act.wait_ge(t_ps, NC * b + c + 1)
                        wait(act, g_ps, NC * (b - 1) + c + 1)
                        act.activation(e_hi[:, c, :], psT[c % 2][:, :], ACT.Copy).then_inc(ehi_ok, 1)
                    if exists(b + 1 + (c + 1) // NC, BATCHES):
                        exponentials(b + 1 + (c + 1) // NC, (h + 1 + (c + 1) // NC) % 2, (c + 1) % NC)
                    if c == 0 and exists(b - 1, BATCHES):
                        act.wait_ge(g_ps, NC * b)
                        wait(act, m_ps, b - 1)
                        act.activation(gT[:, :], psG[:, :], ACT.Copy).then_inc(gT_ok, 1)
                    if c == 1 and exists(b + 1, BATCHES):
                        transposed(b + 1, 1 - h)

            for c in range(NC + 1):
                exponentials(c // NC, c // NC, c % NC)
                if c == 2:
                    transposed(0, 0)
            sweep(act, step, BATCHES, 1)

        @block.tensor
        def _(pe):
            def context(b, h):
                pe.wait_ge(lo_ok, b + 1)
                wait(pe, cT_ok, b)
                for c in range(NC):
                    mm = pe.transpose(psC[:, c, :], chunk(cs[h], c), k.ident_h[:, :])
                mm.then_inc(c_ps, 1)

            def keys(b, h, c):
                pe.wait_ge(lo_ok, b + 1)
                wait(pe, ek_ok, NC * b + c - 1)
                pe.matmul(psK[c % 2][:, :], chunk(k.wk_hi, c), cs[h][:, :], start=True, stop=False)
                pe.matmul(psK[c % 2][:, :], chunk(k.wk_lo, c), cs[h][:, :], start=False, stop=True).then_inc(k_ps, 1)

            def turn(b, h, j):
                pe.wait_ge(ek_ok, NC * b + NC)
                wait(pe, elo_ok, NC * b + j - 1)
                for c in range(NC):
                    mm = pe.transpose(chunk(psT[j % 2], c), chunk(ek[h][:, c, :], j), k.ident[:, :])
                mm.then_inc(t_ps, 1)

            def gather(b, h, j):
                if j == 0:
                    pe.wait_ge(cT_ok, b + 1)
                    wait(pe, gT_ok, b)
                pe.wait_ge(elo_ok, NC * b + j + 1)
                pe.matmul(psG[:, :], cT[h][:, j, :], e_hi[:, j, :], start=j == 0, stop=True, skip_group_check=True)
                mm = pe.matmul(psG[HALF[h], :], cT[h][:, j, h * D:(h + 1) * D], e_lo[:, j, :], start=False, stop=True,
                               skip_group_check=True)
                mm.then_inc(g_ps, 1)

            def matrix(b):
                pe.wait_ge(gT_ok, b + 1)
                wait(pe, M_ok, b)
                for n in range(HEADS):
                    mm = pe.matmul(psM[HALF[n % 2], n // 2, :], gT[:, n * D:(n + 1) * D], k.wv_wo[:, n, :],
                                   start=True, stop=True)
                mm.then_inc(m_ps, 1)

            def step(b, h, t):
                for c in range(NC):
                    if exists(b, BATCHES):
                        turn(b, h, c)
                    if exists(b + 1 + (c + 1) // NC, BATCHES):
                        keys(b + 1 + (c + 1) // NC, (h + 1 + (c + 1) // NC) % 2, (c + 1) % NC)
                    if c > 0 and exists(b, BATCHES):
                        gather(b, h, c - 1)
                    if c == 0 and exists(b - 1, BATCHES):
                        gather(b - 1, 1 - h, NC - 1)
                    if c == 1 and exists(b + 1, BATCHES):
                        context(b + 1, 1 - h)
                    if c == 2 and exists(b - 1, BATCHES):
                        matrix(b - 1)

            for c in range(NC + 1):
                keys(c // NC, c // NC, c % NC)
                if c == 0:
                    context(0, 0)
            sweep(pe, step, BATCHES, 1)


def query_side(nc, a, k):
    with ExitStack() as ctx:
        s = Scope(nc, ctx, "query")
        gbo = s.sb("gbo", [P, 1])
        xn = s.sb("xn", [P, L])
        xs = [s.sb(f"xs{h}", [P, L], F16) for h in range(2)]
        mq = s.sb("mq", [P, NC, HEADS])
        mpart = s.sb("mpart", [P, NC, 96], BF16)
        mrest = s.sb("mrest", [P, NC, HEADS])
        mT = s.sb("mT", [96, L], BF16)
        eq = [s.sb(f"eq{h}", [P, NC, L]) for h in range(2)]
        qn = [s.sb(f"qn{i}", [P, L]) for i in range(NC)]
        lq = s.sb("lq", [P, NC, HEADS])
        rq = s.sb("rq", [P, NC, HEADS])
        qT = s.sb("qT", [P, NC, L])
        m_sb = [s.sb(f"m_sb{h}", [P, NC, D]) for h in range(2)]
        y = s.sb("y", [P, L])
        sq = s.sb("sq", [P, L])
        ln = s.sb("ln", [P, L])
        inv = s.sb("inv", [P, L])
        z = s.sb("z", [P, L])
        stats = (s.sb("stats", [P, 6]), s.sb("mean_var", [P, 2]))
        ag_ok = s.sem("ag_ok")
        psQ = [s.ps(f"psQ{i}", [P, 512]) for i in range(NC)]
        psR = s.ps("psR", [P, 1024], BF16)
        psX = [s.ps(f"psX{i}", [P, 512]) for i in range(2)]
        psF = s.ps("psF", [P, 512])
        (init_ok, xn_ok, hi_ok, lo_ok, q_ps, mq_ok, part_ok, rest_ok, r_ps, mT_ok, f_ps, eq_ok, lq_ok, rq_ok, qn_ok,
         x_ps, qT_ok, msb_ok, o_ps, y_ok, sq_ok, ss_ps, ln_ok, inv_ok, z_ok, x_ok, st_ok, mv_ok) = (s.sem(n) for n in (
             "init_ok xn_ok hi_ok lo_ok q_ps mq_ok part_ok rest_ok r_ps mT_ok f_ps eq_ok lq_ok rq_ok qn_ok "
             "x_ps qT_ok msb_ok o_ps y_ok sq_ok ss_ps ln_ok inv_ok z_ok x_ok st_ok mv_ok").split())
        vec_x, act_x = row_rstd(k, 2, lambda e: None)
        block = s.block()

        def heads(ap):
            return ap.rearrange("p (h d) -> p h d", h=HEADS)

        @block.vector
        def _(dve):
            def low(b, h):
                dve.wait_ge(hi_ok, b + 1)
                dve.tensor_tensor(xs[h][HALF[1 - h], :], xn[HALF[h], :], xs[h][HALF[h], :],
                                  ALU.subtract).then_inc(lo_ok, 1)

            def queries_max(b):
                for c in range(NC):
                    dve.wait_ge(q_ps, NC * b + c + 1)
                    dve.tensor_reduce(mq[:, c, :], heads(psQ[c][:, :]), X, ALU.max).then_inc(mq_ok, 1)
                dve.wait_ge(mq_ok, NC * b + NC)
                wait(dve, r_ps, b)
                split_shift(dve, mq[:, :, :], mpart, mrest[:, :, :], (part_ok, rest_ok), b)

            def step(b, h, t):
                if h == 0 and exists(t + 1, TILES):
                    normed(t + 1)
                if exists(b + 1, BATCHES):
                    queries_max(b + 1)
                if exists(b, BATCHES):
                    for c in range(NC):
                        dve.wait_ge(eq_ok, NC * b + c + 1)
                        dve.tensor_reduce(lq[:, c, :], heads(eq[h][:, c, :]), X, ALU.add).then_inc(lq_ok, 1)
                    dve.wait_ge(lq_ok, NC * b + NC)
                    wait(dve, qn_ok, NC * b)
                    dve.reciprocal(rq[:, :, :], lq[:, :, :]).then_inc(rq_ok, 1)
                    matrix(b, h)
                if h == 0 and exists(t + 1, TILES):
                    low(b + 2, 0)
                    low(b + 3, 1)
                if h == 0 and exists(t - 2, TILES):
                    row_stats(dve, k, t - 2, stats, x_ok, st_ok, ag_ok, mv_ok)
                if h == 1 and exists(t - 1, TILES):
                    u = t - 1
                    dve.wait_ge(inv_ok, u + 1)
                    wait(dve, x_ok, u)
                    dve.scalar_tensor_tensor(out=z[:, :], in0=inv[:, :], scalar=1e12, in1=y[:, :], op0=ALU.min,
                                             op1=ALU.mult).then_inc(z_ok, 1)

            def normed(t):
                wait(dve, lo_ok, 2 * t)
                wait(dve, hi_ok, 2 * t)
                dve.tensor_scalar(xn[:, :], k.x[:, t, :], k.mv[:, t, 0:1], k.rstd[:, bass.ds(t, 1)], ALU.subtract,
                                  ALU.mult).then_inc(xn_ok, 1)

            def matrix(b, h):
                wait(dve, o_ps, b - 1)
                dve.tensor_scalar(m_sb[h][:, :, :], k.M[:, b, :, :], 1.0, None, ALU.mult).then_inc(msb_ok, 1)

            dve.memset(mpart[:, :, :], 0.0).then_inc(init_ok, 1)
            dve.tensor_tensor(gbo[:, :], k.g8[:, :], k.bo1[:, :], ALU.mult).then_inc(init_ok, 1)
            dve.wait_ge(init_ok, 2)
            vec_x(dve)
            normed(0)
            low(0, 0)
            low(1, 1)
            queries_max(0)
            sweep(dve, step, BATCHES, 3, head=4)

        @block.gpsimd
        def _(pool):
            def step(b, h, t):
                if exists(b, BATCHES):
                    for c in range(NC):
                        pool.wait_ge(rq_ok, b + 1)
                        wait(pool, x_ps, NC * (b - 1) + c + 1)
                        pool.tensor_tensor(heads(qn[c][:, :]), heads(eq[h][:, c, :]),
                                           rq[:, c, :].unsqueeze(2).broadcast_to([P, HEADS, D]),
                                           ALU.mult).then_inc(qn_ok, 1)
                if h == 1 and exists(t - 1, TILES):
                    hold(pool, z_ok, t, k.passed)
                    pool.tensor_tensor(k.x[:, t - 1, :], k.x[:, t - 1, :], z[:, :], ALU.add).then_inc(x_ok, 1)

            sweep(pool, step, BATCHES, 2)

        @block.scalar
        def _(act):
            def high(b, h, t):
                act.wait_ge(xn_ok, t + 1)
                wait(act, q_ps, NC * (b - 1))
                act.activation(xs[h][HALF[h], :], xn[HALF[h], :], ACT.Copy).then_inc(hi_ok, 1)

            def shift(b):
                act.wait_ge(r_ps, b + 1)
                act.activation(mT[:, :], psR[0:96, 0:L], ACT.Copy).then_inc(mT_ok, 1)

            def transposed(b, c):
                act.wait_ge(x_ps, NC * b + c + 1)
                wait(act, o_ps, b)
                act.activation(qT[:, :, c * P:(c + 1) * P], psX[c % 2][:, :].rearrange("p (j n) -> p j n", j=NC),
                               ACT.Copy).then_inc(qT_ok, 1)

            def exponentials(b, h):
                for c in range(NC):
                    act.wait_ge(f_ps, NC * b + c + 1)
                    wait(act, qn_ok, NC * (b - 2) + c + 1)
                    act.activation(eq[h][:, c, :], psQ[c][:, :], ACT.Exp).then_inc(eq_ok, 1)

            def step(b, h, t):
                for c in range(NC):
                    if exists(b - 1, BATCHES):
                        transposed(b - 1, c)
                    if c in (1, 3) and h == 0 and exists(t + 1, TILES):
                        high(b + 2 + c // 2, c // 2, t + 1)
                    if c == 2 and h == 1 and exists(t - 1, TILES):
                        act.wait_ge(ss_ps, t)
                        wait(act, z_ok, t - 1)
                        act.activation(ln[:, :], psF[:, :], ACT.Ln, scale=2.0 ** LN_SCALE).then_inc(ln_ok, 1)
                if h == 1 and exists(t - 1, TILES):
                    act.wait_ge(ln_ok, t)
                    act.activation(inv[:, :], ln[:, :], ACT.Exp, scale=-0.5, bias=k.half_ln[:, :]).then_inc(inv_ok, 1)
                if exists(b + 1, BATCHES):
                    shift(b + 1)
                    exponentials(b + 1, 1 - h)
                if h == 0 and exists(t - 1, TILES):
                    act.wait_ge(o_ps, b)
                    wait(act, z_ok, t - 1)
                    act.activation(y[:, :], psF[:, :], ACT.Identity, scale=k.g8[:, :], bias=gbo[:, :]).then_inc(y_ok, 1)
                    act.activation(sq[:, :], psF[:, :], ACT.Square, bias=k.bo1[:, :]).then_inc(sq_ok, 1)

            act.wait_ge(init_ok, 2)
            act_x(act)
            high(0, 0, 0)
            high(1, 1, 0)
            shift(0)
            exponentials(0, 0)
            sweep(act, step, BATCHES, 2)

        @block.tensor
        def _(pe):
            def queries(b, h, c):
                pe.wait_ge(lo_ok, b + 1)
                wait(pe, eq_ok, NC * (b - 1) + c + 1)
                pe.matmul(psQ[c][:, :], chunk(xs[h], c), k.wq_hi[:, :], start=True, stop=False)
                pe.matmul(psQ[c][:, :], chunk(xs[h], c), k.wq_lo[:, :], start=False, stop=True).then_inc(q_ps, 1)

            def shift(b):
                pe.wait_ge(part_ok, 3 * b + 3)
                wait(pe, mT_ok, b)
                for c in range(NC):
                    mm = pe.transpose(psR[0:96, c * P:(c + 1) * P], mpart[:, c, :], k.ident16[:, :])
                mm.then_inc(r_ps, 1)

            def fold(b):
                pe.wait_ge(mT_ok, b + 1)
                for c in range(NC):
                    pe.matmul(psQ[c][:, :], chunk(mT, c), k.ind[0:96, :], start=False, stop=True,
                              skip_group_check=True).then_inc(f_ps, 1)

            def turn(b, c):
                pe.wait_ge(qn_ok, NC * b + c + 1)
                wait(pe, qT_ok, NC * b + c - 1)
                for j in range(NC):
                    mm = pe.transpose(chunk(psX[c % 2], j), chunk(qn[c], j), k.ident[:, :])
                mm.then_inc(x_ps, 1)

            def out(b, h, j):
                if j == 0:
                    pe.wait_ge(msb_ok, b + 1)
                    pe.wait_ge(qT_ok, NC * b + NC)
                mm = pe.matmul(psF[HALF[h], :], m_sb[h][:, j, :], qT[:, j, :], start=j == 0, stop=j == NC - 1)
                if j == NC - 1:
                    mm.then_inc(o_ps, 1)

            def step(b, h, t):
                for c in range(NC):
                    if exists(b + 1, BATCHES):
                        queries(b + 1, 1 - h, c)
                    if exists(b - 1, BATCHES):
                        turn(b - 1, c)
                    if c == 1 and h == 1 and exists(t - 1, TILES):
                        pe.wait_ge(sq_ok, t)
                        pe.wait_ge(y_ok, t)
                        pe.matmul(psF[:, :], k.blk[:, :], sq[:, :], start=True, stop=True).then_inc(ss_ps, 1)
                if exists(b - 1, BATCHES):
                    if h == 1:
                        wait(pe, ln_ok, t)
                    out(b - 1, 1 - h, 0)
                    out(b - 1, 1 - h, 1)
                if exists(b + 1, BATCHES):
                    shift(b + 1)
                if exists(b - 1, BATCHES):
                    out(b - 1, 1 - h, 2)
                    out(b - 1, 1 - h, 3)
                if exists(b + 1, BATCHES):
                    fold(b + 1)

            for c in range(NC):
                queries(0, 0, c)
            shift(0)
            fold(0)
            sweep(pe, step, BATCHES, 2)


def projection(nc, a, k):
    with ExitStack() as ctx:
        s = Scope(nc, ctx, "proj")
        x_s = [s.sb(f"x_s{p}", [P, L]) for p in range(2)]
        xT = [s.sb(f"xT{p}", [P, NC, P]) for p in range(2)]
        psT = [s.ps(f"psT{i}", [P, 512]) for i in range(2)]
        psH = [s.ps(f"psH{i}", [P, 512]) for i in range(2)]
        psZ = [s.ps(f"psZ{i}", [P, 512]) for i in range(2)]
        t_ps, xs_ok, xT_ok, z_ps, z_ok, h_ps, hs_ok, x_ok = (s.sem(n) for n in (
            "t_ps xs_ok xT_ok z_ps z_ok h_ps hs_ok x_ok").split())
        vec_x, act_x = row_rstd(k, 3, lambda e: None)
        block = s.block()

        @block.scalar
        def _(act):
            def step(i, p, j):
                act.wait_ge(t_ps, i + 1)
                act.activation(xT[p][:, :, :].rearrange("p a b -> p (a b)"), psT[p][:, :], ACT.Copy).then_inc(xT_ok, 1)
                act.wait_ge(z_ps, i + 1)
                act.activation(k.zT[:, i, :], psZ[p][:, 0:P], ACT.Copy).then_inc(z_ok, 1)

            act_x(act)
            sweep(act, step, TILES, 0)

        @block.vector
        def _(dve):
            def normed(i, p):
                wait(dve, t_ps, i - 1)
                dve.tensor_scalar(x_s[p][:, :], k.x[:, i, :], k.mv[:, i, 0:1], k.rstd[:, bass.ds(i, 1)], ALU.subtract,
                                  ALU.mult).then_inc(xs_ok, 1)

            def step(i, p, j):
                if exists(i + 2, TILES):
                    normed(i + 2, p)
                dve.wait_ge(h_ps, i + 1)
                dve.tensor_scalar(k.Hs[:, i, :], psH[p][:, 0:EXPERTS], 1.0, None, ALU.mult).then_inc(hs_ok, 1)
                dve.tensor_tensor(k.x[:, i, :], psH[p][:, :], k.x[:, i, :], ALU.add).then_inc(x_ok, 1)

            vec_x(dve)
            normed(0, 0)
            normed(1, 1)
            sweep(dve, step, TILES, 0)

        @block.tensor
        def _(pe):
            def up(i, p):
                pe.wait_ge(xs_ok, i + 1)
                wait(pe, xT_ok, i - 1)
                for c in range(NC):
                    mm = pe.transpose(chunk(psT[p], c), chunk(x_s[p], c), k.ident[:, :])
                mm.then_inc(t_ps, 1)

            def step(i, p, j):
                if exists(i + 1, TILES):
                    up(i + 1, 1 - p)
                pe.wait_ge(xT_ok, i + 1)
                wait(pe, z_ok, i - 1)
                for c in range(NC):
                    mm = pe.matmul(psZ[p][:, 0:P], k.A4[:, c, :], xT[p][:, c, :], start=c == 0, stop=c == NC - 1)
                mm.then_inc(z_ps, 1)
                wait(pe, hs_ok, i - 1)
                wait(pe, x_ok, i - 1)
                pe.matmul(psH[p][:, :], k.ones[:, :], k.bias_rows[2][:, :], start=True, stop=False)
                for c in range(NC):
                    mm = pe.matmul(psH[p][:, :], xT[p][:, c, :], k.WT[:, c, :], start=False, stop=c == NC - 1)
                mm.then_inc(h_ps, 1)

            up(0, 0)
            sweep(pe, step, TILES, 0)


def experts(nc, a, k):
    TE = [P, TILES, EXPERTS]
    with ExitStack() as ctx:
        s = Scope(nc, ctx, "exp")
        dl = s.sb("dl", TE)
        mx2 = s.sb("mx2", [P, 2])
        diag = s.sb("diag", [2, 3])
        ones2 = s.sb("ones2", [2, P])
        sc = s.sb("sc", [P, 2])
        lg, e, pr, w, u = (s.sb("d2" + n, TE) for n in "lepwu")
        r = s.sb("r", [P, TILES])
        top = s.sb("top", [P, TILES, 8])
        wf = s.sb("wf", [P, TILES, RANK])
        wT = s.sb("wT", [P, 4, P])
        zp = s.sb("zp", [P, TILES * P])
        zs = s.sb("zs", [P, TILES * P], F16)
        outb = [s.sb(f"outb{p}", [P, L]) for p in range(2)]
        psA = s.ps("psA", [P, 512])
        psB = s.ps("psB", [P, 512])
        psP = s.ps("psP", [P, 4, 512])
        psD = [psA, psB]
        a_ps, lnk, act_ok, p_ps, d_ps, o_ok, z_fin = (s.sem(n) for n in "a_ps lnk act_ok p_ps d_ps o_ok z_fin".split())
        wT_ps, wT_ok, done_v = (s.sem(n) for n in ("wT_ps", "wT_ok", "done_v"))
        store = [s.sem(f"store{p}") for p in range(2)]
        block = s.block()
        out = a["out"].rearrange("(t b) d l -> t (b d) l", b=2)

        def te(ap):
            return ap.unsqueeze(2).broadcast_to(TE)

        @block.vector
        def _(dve):
            n = [0]

            def link(ins):
                n[0] += 1
                ins.then_inc(lnk, 1)
                dve.wait_ge(lnk, n[0])

            link(dve.memset(ones2[:, :], 1.0))
            link(dve.memset(wf[:, :, :], 0.0))
            dve.wait_ge(a_ps, 1)
            link(dve.tensor_copy(dl[:, :, :], psA[:, 0:P].rearrange("p (t e) -> p t e", t=TILES)))
            for m, v in enumerate((k.Hs, dl)):
                link(dve.tensor_reduce(mx2[:, m:m + 1], v[:, :, :].rearrange("p a b -> p (a b)"), X, ALU.max,
                                       apply_absolute_value=True))
            link(dve.tensor_scalar(mx2[:, :], mx2[:, :], k.odd[:, :], None, ALU.mult))
            dve.sem_inc(done_v, 1)
            dve.wait_ge(a_ps, 2)
            link(dve.tensor_reduce(diag[:, 2:3], psB[0:2, 0:P], X, ALU.max))
            link(dve.tensor_scalar(diag[:, 2:3], diag[:, 2:3], 1e-6, None, ALU.max))
            link(dve.reciprocal(diag[:, 2:3], diag[:, 2:3]))
            link(dve.tensor_scalar(diag[:, 0:2], k.ident[0:2, 0:2], diag[:, 2:3], 0.5, ALU.mult, ALU.mult))
            dve.sem_inc(done_v, 1)
            dve.wait_ge(a_ps, 3)
            link(dve.tensor_copy(sc[:, :], psA[:, 256:258]))
            link(dve.tensor_scalar(lg[:, :, :], k.Hs[:, :, :], sc[:, 0:1], None, ALU.mult))
            link(dve.scalar_tensor_tensor(out=lg[:, :, :], in0=dl[:, :, :], scalar=sc[:, 1:2], in1=lg[:, :, :],
                                          op0=ALU.mult, op1=ALU.add))
            link(dve.tensor_reduce(r[:, :], lg[:, :, :], X, ALU.max))
            link(dve.tensor_tensor(lg[:, :, :], lg[:, :, :], te(r[:, :]), ALU.subtract))
            dve.sem_inc(done_v, 1)
            dve.wait_ge(act_ok, 1)
            link(dve.tensor_reduce(r[:, :], e[:, :, :], X, ALU.add))
            link(dve.reciprocal(r[:, :], r[:, :]))
            link(dve.tensor_tensor(pr[:, :, :], e[:, :, :], te(r[:, :]), ALU.mult))
            for t in range(TILES):
                dve.max(top[:, t, :], pr[:, t, :]).then_inc(lnk, 1)
            n[0] += TILES
            dve.wait_ge(lnk, n[0])
            link(dve.tensor_tensor(u[:, :, :], pr[:, :, :], top[:, :, 1:2].broadcast_to(TE), ALU.subtract))
            dve.sem_inc(done_v, 1)
            dve.wait_ge(act_ok, 2)
            link(dve.tensor_scalar(w[:, :, :], w[:, :, :], 1.0, None, ALU.add))
            link(dve.reciprocal(w[:, :, :], w[:, :, :]))
            link(dve.tensor_tensor(w[:, :, :], w[:, :, :], pr[:, :, :], ALU.mult))
            link(dve.tensor_reduce(r[:, :], w[:, :, :], X, ALU.add))
            link(dve.tensor_scalar(r[:, :], r[:, :], 1e-9, None, ALU.add))
            link(dve.reciprocal(r[:, :], r[:, :]))
            link(dve.tensor_tensor(wf[:, :, 0:EXPERTS], w[:, :, :], te(r[:, :]), ALU.mult))
            dve.sem_inc(done_v, 1)
            dve.wait_ge(wT_ps, 1)
            w4 = psB[:, :].rearrange("p (q n two) -> p q n two", q=4, two=2)[:, :, :, 1:2]
            for q in range(4):
                dve.tensor_copy(wT[:, q, :].rearrange("p (n two) -> p n two", two=2),
                                w4[:, q].broadcast_to([P, D, 2])).then_inc(wT_ok, 1)
            dve.wait_ge(p_ps, 1)
            for q in range(4):
                dve.tensor_tensor(zp[:, :].rearrange("p (g q n) -> p q g n", q=4, n=P)[:, q],
                                  psP[:, q, :].rearrange("p (g n) -> p g n", n=P),
                                  k.zT[:, q:TILES:4, :], ALU.mult).then_inc(lnk, 1)
            n[0] += 4
            dve.wait_ge(lnk, n[0])
            link(dve.tensor_copy(zs[:, :], zp[:, :]))
            for g in (1, 3):
                q = slice(g * RANK, (g + 1) * RANK)
                dve.tensor_tensor(zs[q, :], zp[q, :], zs[q, :], ALU.subtract).then_inc(z_fin, 1)

            def step(i, p, j):
                dve.wait_ge(d_ps, i + 1)
                wait(dve, store[p], 16 * j)
                dve.tensor_tensor(outb[p][:, :], psD[p][:, :], k.x[:, i, :], ALU.add).then_inc(o_ok, 1)

            sweep(dve, step, TILES, 0)

        @block.scalar
        def _(act):
            act.wait_ge(done_v, 3)
            act.activation(e[:, :, :], lg[:, :, :], ACT.Exp).then_inc(act_ok, 1)
            act.wait_ge(done_v, 4)
            act.activation(w[:, :, :], u[:, :, :], ACT.Exp, scale=-2.0).then_inc(act_ok, 1)

        @block.sync
        def _(sp):
            def step(i, p, j):
                sp.wait_ge(o_ok, i + 1)
                sp.dma_start(out[i], outb[p][:, :]).then_inc(store[p], 16)

            sweep(sp, step, TILES, 0)
            for p in range(2):
                sp.wait_ge(store[p], 16 * TILES // 2)

        @block.tensor
        def _(pe):
            for t in range(TILES):
                mm = pe.matmul(psA[:, t * EXPERTS:(t + 1) * EXPERTS], k.zT[0:RANK, t, :], k.limesT[:, :],
                               start=True, stop=True)
            mm.then_inc(a_ps, 1)
            pe.wait_ge(done_v, 1)
            pe.transpose(psB[0:2, 0:P], mx2[:, :], k.ident[:, :]).then_inc(a_ps, 1)
            pe.wait_ge(done_v, 2)
            pe.matmul(psA[:, 256:258], ones2[:, :], diag[:, 0:2], start=True, stop=True).then_inc(a_ps, 1)
            pe.wait_ge(done_v, 5)
            for q in range(4):
                mm = pe.transpose(chunk(psB, q), wf[:, 4 * q:4 * q + 4, :].rearrange("p a b -> p (a b)"), k.ident[:, :])
            mm.then_inc(wT_ps, 1)
            pe.wait_ge(wT_ok, 4)
            for t in range(TILES):
                r0 = RANK * (t % 4)
                mm = pe.matmul(psP[:, t % 4, (t // 4) * P:(t // 4 + 1) * P],
                               k.limes4[r0:r0 + EXPERTS, :, :].rearrange("p a b -> p (a b)"),
                               wT[r0:r0 + EXPERTS, t // 4, :], start=True, stop=True)
            mm.then_inc(p_ps, 1)
            pe.wait_ge(z_fin, 2)
            for t in range(TILES):
                if t >= 2:
                    pe.wait_ge(o_ok, t - 1)
                pe.matmul(psD[t % 2][:, :], chunk(zs, t), k.bm_parts[:, :], start=True, stop=True).then_inc(d_ps, 1)


def program(nc, a):
    with ExitStack() as ctx:
        s = Scope(nc, ctx, "all")
        k = Shared()
        k.x = s.sb("x_res", [P, TILES, L])
        k.mv = s.sb("mv", [P, TILES, 2])
        k.rstd = s.sb("rstd", [P, TILES])
        k.rs = Shared()
        k.rs.v, k.rs.ln, k.rs.y, k.rs.t = (s.sb("rs_" + n, [P, TILES]) for n in ("v", "ln", "y", "t"))
        k.rs.v_ok, k.rs.ln_ok, k.rs.y_ok, k.rs.t_ok, k.rs.rstd_ok = (
            s.sem("rs_" + n) for n in ("v_ok", "ln_ok", "y_ok", "t_ok", "rstd_ok"))
        k.passed = s.sem("passed")
        k.xabs = s.sb("xabs", [P, TILES])
        k.ident = s.sb("ident", [P, P])
        k.ident16 = s.sb("ident16", [P, P], BF16)
        k.ident_h = s.sb("ident_h", [P, P], F16)
        k.ones = s.sb("ones", [P, P], BF16)
        k.ind = s.sb("ind", [P, L], BF16)
        k.blk = s.sb("blk", [P, P])
        k.odd = s.sb("odd", [P, 1])
        k.m_round = s.sb("m_round", [P, 1])
        k.m_minus = s.sb("m_minus", [P, 1])
        k.half_ln = s.sb("half_ln", [P, 1])
        k.bias_rows = [s.sb(f"bias_rows{i}", [P, L], BF16) for i in range(3)]
        k.bv2, k.bo2, k.bo1, k.g8 = (s.sb(n, [P, 1]) for n in ("bv2", "bo2", "bo1", "g8"))
        k.wT0 = s.sb("wT0", [P, 4, P])
        k.wq_hi, k.wq_lo, k.wk_hi, k.wk_lo = (s.sb(n, [P, L], F16) for n in ("wq_hi", "wq_lo", "wk_hi", "wk_lo"))
        k.wv_wo = s.sb("wv_wo", [P, HEADS, D])
        k.WT = s.sb("WT", [P, NC, L])
        k.A4 = s.sb("A4", [P, NC, P])
        k.bm_parts = s.sb("bm_parts", [P, L], F16)
        k.limes4 = s.sb("limes4", [P, 4, RANK])
        k.limesT = s.sb("limesT", [RANK, EXPERTS])
        k.ffs = s.sb("ffs", [P, 3])
        k.ffw = s.sb("ffw", [P, 3])
        k.s4, k.sg, k.su, k.su_abs, k.sd = (s.sb(n, [P, TILES]) for n in ("s4", "sg", "su", "su_abs", "sd"))
        setup(nc, a, k)
        with ExitStack() as ctx_ff:
            f = Scope(nc, ctx_ff, "all")
            k.wgT = f.sb("wgT", [P, NC, FF], BF16)
            k.wuT = f.sb("wuT", [P, NC, FF], BF16)
            k.wdT = f.sb("wdT", [P, FFC, L], BF16)
            with ExitStack() as ctx_raw:
                w = Scope(nc, ctx_raw, "all")
                raw = [w.sb("raw_g", [P, FFC, L]), w.sb("raw_u", [P, FFC, L]), w.sb("raw_d", [P, NC, FF])]
                raw_in = [w.sem(f"raw_in{n}") for n in range(3)]
                with nc.Block() as block:
                    @block.gpsimd
                    def _(pool):
                        full = (FFC - 1) * P
                        for n, src in enumerate((a["wg"], a["wu"])):
                            pool.dma_start(raw[n][:, 0:FFC - 1, :],
                                           src[0:full, :].rearrange("(c p) d -> p c d", p=P)).then_inc(raw_in[n], 16)
                            pool.dma_start(raw[n][0:FF - full, FFC - 1, :], src[full:FF, :]).then_inc(raw_in[n], 16)
                        pool.dma_start(raw[2][:, :, :], a["wd"].rearrange("(c p) d -> p c d", p=P)).then_inc(raw_in[2], 16)
                attention0(nc, a, k)
                ternary_weights(nc, a, k, raw, raw_in)
            feed_forward(nc, a, k)
        with ExitStack() as ctx_c:
            c = Scope(nc, ctx_c, "all")
            k.M = c.sb("M", [P, BATCHES, NC, D])
            key_side(nc, a, k)
            query_side(nc, a, k)
        k.zT = s.sb("zT", [P, TILES, P])
        k.Hs = s.sb("Hs", [P, TILES, EXPERTS])
        projection(nc, a, k)
        experts(nc, a, k)


_INS = dict(x="x", ctx_4096="ctx", L0_xattn_Wq="Wq0", L0_xattn_bq="bq0", L0_xattn_Wk="Wk0", L0_xattn_bk="bk0",
            L0_xattn_Wv="Wv0", L0_xattn_bv="bv0", L0_xattn_Wo="Wo0", L0_xattn_bo="bo0", L0_ffn_w_gate="wg",
            L0_ffn_w_up="wu", L0_ffn_w_down="wd", L0_ffn_s_gate="sg", L0_ffn_s_up="su", L0_ffn_s_down="sd",
            L1_xattn_Wq="Wq1", L1_xattn_Wk="Wk1", L1_xattn_Wv="Wv1", L1_xattn_Wo="Wo1", L1_xattn_bo="bo1",
            L1_xattn_g="g1", L1_ffn_W="W1", L1_ffn_b="b1", L1_ffn_A="A1", L1_ffn_Bmat="Bm1", L1_ffn_LiMEs="Li1")


def kernel(**inputs):
    import numpy as _np
    import concourse.bacc as _bacc
    from concourse import mybir as _mybir
    from concourse.bass_utils import run_bass_kernel_spmd as _run

    nc = _bacc.Bacc("TRN2", target_bir_lowering=False, num_devices=1)
    arrays, args = {}, {}
    for name, short in _INS.items():
        v = _np.ascontiguousarray(inputs[name])
        arrays[f"in_{name}_dram"] = v
        args[short] = nc.dram_tensor(f"in_{name}_dram", v.shape, _mybir.dt.from_np(v.dtype), kind="ExternalInput").ap()
    args["out"] = nc.dram_tensor("out_0_dram", (BATCHES, D, L), F32, kind="ExternalOutput").ap()
    program(nc, args)
    r = _run(nc, [arrays], core_ids=[0])
    return r.results[0]["out_0_dram"]
```

```python
import math
from contextlib import ExitStack

import concourse.bass as bass
from concourse import mybir
from concourse.alu_op_type import AluOpType as ALU

F32, F16, BF16 = mybir.dt.float32, mybir.dt.float16, mybir.dt.bfloat16
ACT = mybir.ActivationFunctionType
X = mybir.AxisListType.X

P = 128
D = 64
L = 512
HEADS = L // D
NC = L // P
BATCHES = 32
TILES = BATCHES * D // P
HALF = (slice(0, D), slice(D, P))
FF = 1376
FFC = (FF + P - 1) // P
FFB = [(a, min(a + 512, FF)) for a in range(0, FF, 512)]
RANK, EXPERTS = 32, 8
EPS = 1e-5
ROUND = 12582912.0
SQRT7 = math.sqrt(7.0)
W_SCALE = 64.0
LN_SCALE = 24


def chunk(ap, c, n=P):
    return ap[:, c * n:(c + 1) * n]


def exists(i, n):
    return not isinstance(i, int) or 0 <= i < n


def wait(eng, sem, value):
    if not isinstance(value, int) or value > 0:
        eng.wait_ge(sem, value)


def hold(eng, sem, value, passed):
    if not isinstance(value, int) or value > 0:
        eng.wait_ge(sem, value)
        eng.sem_inc(passed, 1)


def sweep(eng, step, n, tail, head=2, between=None, unroll=2):
    head += (n - 2 - head) % unroll
    for i in range(head):
        step(i, i % 2, i // 2)
    pairs = unroll // 2
    with eng.Fori(0, (n - 2 - head) // unroll) as j:
        for m in range(pairs):
            half = pairs * j + (head // 2 + m)
            step(2 * half, 0, half)
            step(2 * half + 1, 1, half)
    if between:
        between(eng)
    for i in range(n - 2, n + tail):
        step(i, i % 2, i // 2)


class Shared:
    pass


class Scope:

    def __init__(self, nc, ctx, tag):
        self.nc, self.ctx, self.tag = nc, ctx, tag

    def sb(self, name, shape, dt=F32):
        return self.ctx.enter_context(self.nc.sbuf_tensor(f"{self.tag}_{name}", shape, dt))

    def ps(self, name, shape, dt=F32):
        return self.ctx.enter_context(self.nc.psum_tensor(f"{self.tag}_{name}", shape, dt))

    def sem(self, name):
        return self.ctx.enter_context(self.nc.semaphore(f"{self.tag}_{name}"))

    def block(self):
        return self.ctx.enter_context(self.nc.Block())


def row_stats(dve, k, t, stats, x_ok, st_ok, ag_ok, mv_ok):
    six, two = stats
    hold(dve, x_ok, t + 1, k.passed)
    dve.bn_stats(six[:, :], k.x[:, t, :]).then_inc(st_ok, 1)
    hold(dve, st_ok, t + 1, k.passed)
    hold(dve, mv_ok, t + 1, k.passed)
    dve.bn_aggr(two[:, :], six[:, :]).then_inc(ag_ok, 1)
    hold(dve, ag_ok, t + 1, k.passed)
    dve.tensor_copy(k.mv[:, t, :], two[:, :]).then_inc(mv_ok, 1)


def row_rstd(k, n, start):
    r = k.rs

    def on_vector(dve):
        start(dve)
        dve.tensor_scalar(r.v[:, :], k.mv[:, :, 1], EPS, None, ALU.add).then_inc(r.v_ok, 1)
        dve.wait_ge(r.y_ok, n + 1)
        dve.tensor_tensor(r.t[:, :], r.y[:, :], r.y[:, :], ALU.mult).then_inc(r.t_ok, 1)
        dve.wait_ge(r.t_ok, 3 * n + 1)
        dve.tensor_tensor(r.t[:, :], r.t[:, :], r.v[:, :], ALU.mult).then_inc(r.t_ok, 1)
        dve.wait_ge(r.t_ok, 3 * n + 2)
        dve.tensor_scalar(r.t[:, :], r.t[:, :], -0.5, 1.5, ALU.mult, ALU.add).then_inc(r.t_ok, 1)
        dve.wait_ge(r.t_ok, 3 * n + 3)
        dve.tensor_tensor(k.rstd[:, :], r.y[:, :], r.t[:, :], ALU.mult).then_inc(r.rstd_ok, 1)
        dve.wait_ge(r.rstd_ok, n + 1)

    def on_scalar(act):
        act.wait_ge(r.v_ok, n + 1)
        act.activation(r.ln[:, :], r.v[:, :], ACT.Ln).then_inc(r.ln_ok, 1)
        act.wait_ge(r.ln_ok, n + 1)
        act.activation(r.y[:, :], r.ln[:, :], ACT.Exp, scale=-0.5).then_inc(r.y_ok, 1)

    return on_vector, on_scalar


def setup(nc, a, k):
    with ExitStack() as ctx:
        s = Scope(nc, ctx, "setup")
        w_two = s.sb("w_two", [P, 4, D])
        brow = s.sb("brow", [1, 2, D])
        part = s.sb("part", [1, 2, D], BF16)
        rest = s.sb("rest", [1, 2, D])
        stats = s.sb("stats", [P, TILES, 6])
        psW = s.ps("psW", [P, 512])

        zero_ok = s.sem("zero_ok")
        ident_ok = s.sem("ident_ok")
        const_ok = s.sem("const_ok")
        x_in = [s.sem(f"x_in{i}") for i in range(4)]
        w_in = s.sem("w_in")
        b_in = s.sem("b_in")
        stat_ok = s.sem("stat_ok")
        mv_ok = s.sem("mv_ok")
        w_ps = s.sem("w_ps")
        wT_ok = s.sem("wT_ok")
        row_ok = s.sem("row_ok")
        vec_x, act_x = row_rstd(k, 0, lambda e: e.wait_ge(mv_ok, TILES))
        block = s.block()

        @block.sync
        def _(sp):
            xv = a["x"].rearrange("(t b) d l -> (b d) t l", b=2)
            g = TILES // 4
            for i in range(4):
                sp.dma_start(k.x[:, g * i:g * i + g, :], xv[:, g * i:g * i + g, :]).then_inc(x_in[i], 16)
            load_context0(sp, a, k, 0, 0)
            load_context0(sp, a, k, 1, 1)

        @block.scalar
        def _(act):
            act.dma_start(brow[0:1, 0, :], a["bq0"].unsqueeze(0)).then_inc(b_in, 16)
            act.dma_start(brow[0:1, 1, :], a["bk0"].unsqueeze(0)).then_inc(b_in, 16)
            for n, w in enumerate((a["Wq0"], a["Wk0"], a["Wv0"], a["Wo0"])):
                for h in range(2):
                    act.dma_start(w_two[HALF[h], n, :], w).then_inc(w_in, 16)
            for h in range(2):
                act.dma_start(k.bv2[HALF[h], :], a["bv0"].unsqueeze(1)).then_inc(w_in, 16)
                act.dma_start(k.bo2[HALF[h], :], a["bo0"].unsqueeze(1)).then_inc(w_in, 16)
            act.preload_act_table_set("natural_log_exp_and_others")
            act.wait_ge(w_ps, 1)
            act.wait_ge(zero_ok, 3)
            for h in range(2):
                act.activation(k.wT0[HALF[h], :, h * D:(h + 1) * D],
                               psW[0:D, :].rearrange("p (n m) -> p n m", n=4)[:, :, h * D:(h + 1) * D],
                               ACT.Copy).then_inc(wT_ok, 1)
            act_x(act)
            act.wait_ge(w_in, 16 * 12)

        @block.gpsimd
        def _(pool):
            pool.memset(k.ident[:, :], 0.0).then_inc(zero_ok, 1)
            pool.memset(k.wT0[:, :, :], 0.0).then_inc(zero_ok, 1)
            pool.memset(k.ind[:, :], 0.0).then_inc(zero_ok, 1)
            pool.wait_ge(zero_ok, 3)
            pool.affine_select(out=k.ident[:, :], in_=k.ident[:, :], compare_op=ALU.not_equal, fill=1.0, base=0,
                               pattern=[[-1, P]], channel_multiplier=1).then_inc(ident_ok, 1)
            iv = k.ind[0:32, :].rearrange("p (h d) -> p h d", h=HEADS)
            pool.affine_select(out=iv, in_=iv, compare_op=ALU.not_equal, fill=1.0, base=0,
                               pattern=[[-1, HEADS], [0, D]], channel_multiplier=1).then_inc(ident_ok, 1)

        @block.vector
        def _(dve):
            consts = ((k.ones, 1.0), (k.ones32, 1.0), (k.bias_rows[0], 0.0), (k.bias_rows[1], 0.0),
                      (k.bias_rows[2], 0.0), (k.blk, 0.0), (k.m_round, ROUND), (k.m_minus, -ROUND),
                      (k.half_ln, 0.5 * LN_SCALE * math.log(2.0)))
            for buf, value in consts:
                dve.memset(buf[:, :], value).then_inc(const_ok, 1)
            dve.wait_ge(const_ok, len(consts))
            for h in range(2):
                dve.memset(k.blk[HALF[h], h * D:(h + 1) * D], 1.0).then_inc(const_ok, 1)
            dve.wait_ge(ident_ok, 2)
            dve.tensor_copy(k.ident16[:, :], k.ident[:, :]).then_inc(const_ok, 1)
            dve.tensor_copy(k.ident_h[:, :], k.ident[:, :]).then_inc(const_ok, 1)
            for g in (1, 2):
                dve.tensor_copy(k.ind[32 * g:32 * g + 32, :], k.ind[0:32, :]).then_inc(const_ok, 1)
            dve.tensor_reduce(k.odd[:, :], k.ident[:, :].rearrange("p (n two) -> p two n", two=2)[:, 1, :], X,
                              ALU.add).then_inc(const_ok, 1)
            def biases():
                dve.wait_ge(b_in, 16 * 2)
                dve.tensor_copy(part[:, :, :], brow[:, :, :]).then_inc(row_ok, 1)
                dve.wait_ge(row_ok, 1)
                dve.tensor_tensor(rest[:, :, :], brow[:, :, :], part[:, :, :], ALU.subtract).then_inc(row_ok, 1)

                def spread(partition, src):
                    for n in range(2):
                        dve.tensor_copy(k.bias_rows[n][partition:partition + 1, :].rearrange("p (c d) -> p c d", d=D),
                                        src[0:1, n, :].unsqueeze(1).broadcast_to([1, L // D, D])).then_inc(row_ok, 1)

                spread(0, part)
                dve.wait_ge(row_ok, 4)
                dve.tensor_copy(part[:, :, :], rest[:, :, :]).then_inc(row_ok, 1)
                dve.wait_ge(row_ok, 5)
                dve.tensor_tensor(rest[:, :, :], rest[:, :, :], part[:, :, :], ALU.subtract).then_inc(row_ok, 1)
                spread(32, part)
                dve.wait_ge(row_ok, 6)
                spread(64, rest)

            for t in range(TILES):
                if t == 3 * TILES // 4:
                    biases()
                if t % 4 == 0:
                    dve.wait_ge(x_in[t // 4], 16)
                dve.bn_stats(stats[:, t, :], k.x[:, t, :]).then_inc(stat_ok, 1)
            for t in range(TILES):
                dve.wait_ge(stat_ok, t + 1)
                dve.bn_aggr(k.mv[:, t, :], stats[:, t, :]).then_inc(mv_ok, 1)
            vec_x(dve)

        @block.tensor
        def _(pe):
            pe.wait_ge(ident_ok, 1)
            pe.wait_ge(w_in, 16 * 12)
            for n in range(4):
                mm = pe.transpose(chunk(psW, n)[0:D, :], w_two[:, n, :], k.ident[:, :])
            mm.then_inc(w_ps, 1)


def later_loads(nc, a, k, act):
    n = [0]

    def load(dst, src):
        act.dma_start(dst, src).then_inc(k.late_in, 16)
        n[0] += 1

    late = k.late
    load(late.brow[0:1, :], a["b1"].unsqueeze(0))
    for h in range(2):
        load(k.bo1[HALF[h], :], a["bo1"].unsqueeze(1))
        load(k.g8[HALF[h], :], a["g1"].rearrange("a d b -> (a d) b"))
    for m, w in enumerate((a["Wq1"], a["Wk1"])):
        for h in range(2):
            load(late.wdup[:, m, :, h * D:(h + 1) * D], w.rearrange("(c p) d -> p c d", p=P))
    load(late.wv1[:, :, :], a["Wv1"].rearrange("(c p) d -> p c d", p=P))
    load(late.wo1[:, :], a["Wo1"])
    load(late.w_nat[:, :, :], a["W1"].rearrange("(c p) d -> p c d", p=P))
    for q in range(4):
        load(late.A4[:, :, q * RANK:(q + 1) * RANK], a["A1"].rearrange("(c p) r -> p c r", p=P))
        load(late.bm[q * RANK:(q + 1) * RANK, :], a["Bm1"])
        load(k.limes4[q * RANK:q * RANK + EXPERTS, :, :], a["Li1"].unsqueeze(1).broadcast_to([EXPERTS, 4, RANK]))
    with nc.allow_non_contiguous_dma(reason="256 numbers"):
        load(k.limesT[:, :], a["Li1"].rearrange("e r -> r e"))
    for m, w in enumerate((a["sg"], a["su"], a["sd"])):
        load(k.ffs[:, m:m + 1], w.unsqueeze(0).broadcast_to([P, 1]))
    assert n[0] == k.n_late


def later_rows(dve, k, row_ok):
    late = k.late
    dve.wait_ge(k.late_in, 16 * k.n_late)
    dve.tensor_scalar(k.g8[:, :], k.g8[:, :], math.sqrt(D), None, ALU.mult).then_inc(row_ok, 1)
    dve.tensor_scalar(late.brow[:, :], late.brow[:, :], W_SCALE, None, ALU.mult).then_inc(row_ok, 1)
    dve.wait_ge(row_ok, 2)
    row = k.bias_rows[2]
    dve.tensor_copy(row[0:1, :], late.brow[:, :]).then_inc(row_ok, 1)
    dve.wait_ge(row_ok, 3)
    dve.tensor_tensor(late.brow[:, :], late.brow[:, :], row[0:1, :], ALU.subtract).then_inc(row_ok, 1)
    dve.wait_ge(row_ok, 4)
    dve.tensor_copy(late.part[:, :], late.brow[:, :]).then_inc(row_ok, 1)
    dve.wait_ge(row_ok, 5)
    dve.tensor_copy(row[32:33, :], late.part[:, :]).then_inc(row_ok, 1)
    dve.tensor_tensor(row[64:65, :], late.brow[:, :], late.part[:, :], ALU.subtract).then_inc(row_ok, 1)
    bm = late.bm
    dve.tensor_scalar(bm[:, :], bm[:, :], 16.0 / RANK * W_SCALE, None, ALU.mult).then_inc(row_ok, 1)
    dve.wait_ge(row_ok, 8)
    dve.tensor_copy(k.bm_parts[:, :], bm[:, :]).then_inc(row_ok, 1)
    dve.wait_ge(row_ok, 9)
    for g in (1, 3):
        r = slice(g * RANK, (g + 1) * RANK)
        dve.tensor_tensor(k.bm_parts[r, :], bm[r, :], k.bm_parts[r, :], ALU.subtract).then_inc(row_ok, 1)


def later_weights(s, k, ps):
    late = k.late
    tr = s.sem("tr")
    out0 = s.sem("out0")
    out1 = s.sem("out1")
    WT_BANK = (4, 5, 6, 0)

    def on_scalar(act):
        for n, w in enumerate((k.wq_hi, k.wk_hi)):
            act.wait_ge(tr, 2 + n)
            act.activation(w[:, :], ps[n][:, :], ACT.Copy).then_inc(out1, 1)
        act.activation(k.A_hi[:, :, :], late.A4[:, :, :], ACT.Copy, scale=W_SCALE).then_inc(out1, 1)
        for i in range(NC):
            act.wait_ge(tr, 5 + i)
            act.activation(k.WT_hi[:, i, :], ps[WT_BANK[i]][:, :], ACT.Copy, scale=W_SCALE).then_inc(out1, 1)

    def on_vector(dve):
        dve.wait_ge(tr, 1)
        dve.tensor_copy(late.wo1T[:, :, :], ps[6][:, 0:NC * D].rearrange("p (n m) -> p n m", n=NC)).then_inc(out0, 1)
        for n, (hi, lo) in enumerate(((k.wq_hi, k.wq_lo), (k.wk_hi, k.wk_lo))):
            dve.wait_ge(out1, n + 1)
            dve.tensor_tensor(lo[:, :], ps[n][:, :], hi[:, :], ALU.subtract).then_inc(out0, 1)
        dve.wait_ge(tr, 4)
        for r in range(2):
            for rows in HALF:
                dve.tensor_scalar(k.wv_wo[rows, r:HEADS:2, :],
                                  ps[2 + r][0:D, :].rearrange("p (h m) -> p h m", h=HEADS)[:, r:HEADS:2, :],
                                  D ** -0.5, None, ALU.mult).then_inc(out0, 1)
        dve.wait_ge(out1, 3)
        dve.scalar_tensor_tensor(out=k.A_lo[:, :, :], in0=late.A4[:, :, :], scalar=W_SCALE, in1=k.A_hi[:, :, :],
                                 op0=ALU.mult, op1=ALU.subtract).then_inc(out0, 1)
        for i in range(NC):
            dve.wait_ge(out1, 4 + i)
            dve.scalar_tensor_tensor(out=k.WT_lo[:, i, :], in0=ps[WT_BANK[i]][:, :], scalar=W_SCALE,
                                     in1=k.WT_hi[:, i, :], op0=ALU.mult, op1=ALU.subtract).then_inc(out0, 1)

    def on_tensor(pe):
        for c in range(NC):
            mm = pe.transpose(ps[6][:, c * D:(c + 1) * D], chunk(late.wo1, c), k.ident[0:D, 0:D])
        mm.then_inc(tr, 1)
        for n in range(2):
            for c in range(NC):
                mm = pe.transpose(chunk(ps[n], c), late.wdup[:, n, c, :], k.ident[:, :])
            mm.then_inc(tr, 1)
        pe.wait_ge(out0, 1)
        for h in range(HEADS):
            r = HALF[h % 2]
            mm = pe.matmul(ps[2 + h % 2][0:D, h * D:(h + 1) * D], late.wv1[r, h // 2, :], late.wo1T[r, h // 2, :],
                           start=True, stop=True)
        mm.then_inc(tr, 1)
        for i in range(NC):
            if i == 3:
                pe.wait_ge(out0, 2)
            for o in range(NC):
                mm = pe.transpose(chunk(ps[WT_BANK[i]], o), late.w_nat[:, o, i * P:(i + 1) * P], k.ident[:, :])
            mm.then_inc(tr, 1)

    return on_vector, on_scalar, on_tensor, out0, out1


def load_context0(sp, a, k, i, p):
    nat = a["ctx"].rearrange("(t b) d l -> t (b d) l", b=2)
    par = a["ctx"].rearrange("(t b) d (c r k) -> t r d b c k", b=2, r=2, k=D)
    sp.dma_start(k.ctx_n[p][:, :], nat[i]).then_inc(k.ctx_in[p], 16)
    for r in range(2):
        for b in range(2):
            sp.dma_start(k.ctx_h[p][HALF[r], b], par[i, r, :, b]).then_inc(k.ctx_in[p], 16)


def attention0(nc, a, k):
    with ExitStack() as ctx:
        s = Scope(nc, ctx, "att0")
        ctx_n, ctx_h, ctx_in = k.ctx_n, k.ctx_h, k.ctx_in
        xn = [s.sb(f"xn{p}", [P, L]) for p in range(2)]
        q_t = s.sb("q_t", [P, L])
        k_t = s.sb("k_t", [P, 2, NC, 2, D])
        v_h = [s.sb(f"v_h{p}", [P, 2, NC, 2, D]) for p in range(2)]
        mx = s.sb("mx", [P, HEADS])
        sh = s.sb("sh", [P, L])
        ex = s.sb("ex", [P, L])
        sm = s.sb("sm", [P, HEADS])
        rs = s.sb("rs", [P, HEADS])
        pn = s.sb("pn", [P, L])
        wp = s.sb("wp", [P, L])
        dump = s.sb("dump", [P, L])
        wdump = s.sb("wdump", [P, FFC * L // 8], BF16)
        wa_ok = s.sem("wa_ok")
        pad_ok = s.sem("pad_ok")
        row_ok = s.sem("row_ok")
        stats = (s.sb("stats", [P, 6]), s.sb("mean_var", [P, 2]))
        ag_ok = s.sem("ag_ok")
        psQ, psK, psV, psS, psW, psO = (s.ps("ps" + n, [P, 512]) for n in "QKVSWO")
        (zero_ok, xn_ok, q_ps, k_ps, v_ps, s_ps, w_ps, o_ps, q_ok, k_ok, v_ok, mx_ok, sh_ok, ex_ok, sm_ok, rs_ok, pn_ok,
         wp_ok, x_ok, st_ok, mv_ok, ab_ok) = (s.sem(n) for n in (
             "zero_ok xn_ok q_ps k_ps v_ps s_ps w_ps o_ps q_ok k_ok v_ok mx_ok sh_ok ex_ok sm_ok rs_ok pn_ok "
             "wp_ok x_ok st_ok mv_ok ab_ok").split())
        raw_in = [s.sem(f"raw_in{n}") for n in range(3)]
        RAW_STEPS = 6
        RAW_IN = (6 * 16, 6 * 16, NC * 16)
        flat = [w[:, :, :].rearrange("p a b -> p (a b)").rearrange("p (t f) -> p t f", t=TILES // 2) for w in k.raw]
        block = s.block()

        @block.sync
        def _(sp):
            def step(i, p, j):
                if not isinstance(i, int) or i >= 2:
                    sp.wait_ge(v_ps, i - 1)
                    load_context0(sp, a, k, i, p)

            sweep(sp, step, TILES, 0)

        @block.gpsimd
        def _(pool):
            for buf in (k_t, v_h[0], v_h[1]):
                pool.memset(buf[:, :, :, :, :], 0.0).then_inc(zero_ok, 1)
            full = FFC - 1
            loads = []
            for n, src in enumerate((a["wg"], a["wu"])):
                for c in range(0, full, 2):
                    loads.append((n, k.raw[n][:, c:c + 2, :], src[c * P:(c + 2) * P, :].rearrange("(c p) d -> p c d", p=P)))
                loads.append((n, k.raw[n][0:FF - full * P, full, :], src[full * P:FF, :]))
            for c in range(NC):
                loads.append((2, k.raw[2][:, c, :], a["wd"][c * P:(c + 1) * P, :]))
            each = -(-len(loads) // RAW_STEPS)

            def step(i, p, j):
                pool.wait_ge(rs_ok, i + 1)
                pool.tensor_tensor(pn[:, :].rearrange("p (h e) -> p h e", h=HEADS),
                                   ex[:, :].rearrange("p (h e) -> p h e", h=HEADS),
                                   rs[:, :].unsqueeze(2).broadcast_to([P, HEADS, D]), ALU.mult).then_inc(pn_ok, 1)
                if isinstance(i, int) and i < RAW_STEPS:
                    for n, dst, src in loads[i * each:(i + 1) * each]:
                        pool.dma_start(dst, src).then_inc(raw_in[n], 16)

            sweep(pool, step, TILES, 0, head=RAW_STEPS)

        @block.vector
        def _(dve):
            def normed(i, p):
                dve.tensor_scalar(xn[p][:, :], k.x[:, i, :], k.mv[:, i, 0:1], k.rstd[:, bass.ds(i, 1)], ALU.subtract,
                                  ALU.mult).then_inc(xn_ok, 1)

            def step(i, p, j):
                t, u = i - 1, i - 2
                if exists(t, TILES):
                    dve.wait_ge(s_ps, t + 1)
                    s3 = psS[:, :].rearrange("p (h e) -> p h e", h=HEADS)
                    dve.tensor_reduce(mx[:, :], s3, X, ALU.max).then_inc(mx_ok, 1)
                    dve.wait_ge(mx_ok, t + 1)
                    dve.tensor_tensor(sh[:, :].rearrange("p (h e) -> p h e", h=HEADS), s3,
                                      mx[:, :].unsqueeze(2).broadcast_to([P, HEADS, D]), ALU.subtract).then_inc(sh_ok, 1)
                if exists(u, TILES):
                    dve.wait_ge(o_ps, u + 1)
                    dve.scalar_tensor_tensor(out=k.x[:, u, :], in0=psO[:, :], scalar=k.bo2[:, :], in1=k.x[:, u, :],
                                             op0=ALU.add, op1=ALU.add).then_inc(x_ok, 1)
                if exists(t, TILES):
                    dve.wait_ge(ex_ok, t + 1)
                    dve.tensor_reduce(sm[:, :], ex[:, :].rearrange("p (h e) -> p h e", h=HEADS), X,
                                      ALU.add).then_inc(sm_ok, 1)
                    dve.wait_ge(sm_ok, t + 1)
                    dve.reciprocal(rs[:, :], sm[:, :]).then_inc(rs_ok, 1)
                if exists(i, TILES):
                    dve.wait_ge(k_ps, i + 1)
                    wait(dve, k_ok, 2 * i)
                    dve.wait_ge(zero_ok, 3)
                    for r in range(2):
                        dve.tensor_copy(k_t[HALF[r], :, :, r, :],
                                        psK[HALF[r], :].rearrange("p (c b e) -> p b c e", b=2, e=D)).then_inc(k_ok, 1)
                if exists(i + 1, TILES):
                    normed(i + 1, 1 - p)
                if exists(u, TILES):
                    row_stats(dve, k, u, stats, x_ok, st_ok, ag_ok, mv_ok)

            dve.sem_inc(mv_ok, 1)
            normed(0, 0)
            for n in range(2):
                dve.memset(k.raw[n][FF - (FFC - 1) * P:P, FFC - 1, :], 0.0).then_inc(pad_ok, 1)
            sweep(dve, step, TILES, 2, between=lambda e: later_rows(e, k, row_ok))

        @block.scalar
        def _(act):
            def weight_sum(i, n, weights):
                w = i - TILES // 2
                if weights and exists(w, TILES // 2):
                    hold(act, wa_ok, 3 * w + n, k.passed)
                    act.wait_ge(raw_in[n], RAW_IN[n])
                    act.activation(wdump[:, 0:flat[n].shape[2]], flat[n][:, w, :], ACT.Abs,
                                   accum_out=k.wabs[:, n, bass.ds(w, 1)]).then_inc(wa_ok, 1)

            def step(i, p, j, weights=False):
                t, u = i - 1, i - 2
                if exists(t, TILES):
                    act.wait_ge(sh_ok, t + 1)
                    wait(act, pn_ok, t)
                    act.activation(ex[:, :], sh[:, :], ACT.Exp, scale=D ** -0.5).then_inc(ex_ok, 1)
                weight_sum(i, 0, weights)
                if exists(i, TILES):
                    act.wait_ge(q_ps, i + 1)
                    act.activation(q_t[:, :], psQ[:, :], ACT.Copy).then_inc(q_ok, 1)
                    act.wait_ge(v_ps, i + 1)
                    act.wait_ge(zero_ok, 3)
                    for r in range(2):
                        act.activation(v_h[p][HALF[r], :, :, r, :],
                                       psV[HALF[r], :].rearrange("p (b c e) -> p b c e", b=2, e=D), ACT.Identity,
                                       bias=k.bv2[HALF[r], :]).then_inc(v_ok, 1)
                weight_sum(i, 1, weights)
                if exists(t, TILES):
                    act.wait_ge(w_ps, t + 1)
                    act.activation(wp[:, :], psW[:, :], ACT.Copy).then_inc(wp_ok, 1)
                weight_sum(i, 2, weights)
                if exists(u, TILES):
                    act.wait_ge(mv_ok, u + 2)
                    hold(act, ab_ok, u, k.passed)
                    act.activation(dump[:, :], k.x[:, u, :], ACT.Abs, scale=-1.0, bias=k.mv[:, u, 0:1],
                                   accum_out=k.xabs[:, bass.ds(u, 1)]).then_inc(ab_ok, 1)

            step(0, 0, 0)
            step(1, 1, 0)
            later_loads(nc, a, k, act)
            with act.Fori(1, TILES // 4) as j:
                step(2 * j, 0, j)
                step(2 * j + 1, 1, j)
            act.wait_ge(pad_ok, 2)
            with act.Fori(TILES // 4, TILES // 2 - 1) as j:
                step(2 * j, 0, j, weights=True)
                step(2 * j + 1, 1, j, weights=True)
            for i in range(TILES - 2, TILES + 2):
                step(i, i % 2, i // 2, weights=True)
            act.wait_ge(k.late_in, 16 * k.n_late)

        @block.tensor
        def _(pe):
            def step(i, p, j):
                t = i - 1
                if exists(i, TILES):
                    pe.wait_ge(xn_ok, i + 1)
                    wait(pe, q_ok, i)
                    pe.matmul(psQ[:, :], k.ones[:, :], k.bias_rows[0][:, :], start=True, stop=True)
                    for c in range(NC):
                        mm = pe.matmul(chunk(psQ, c), chunk(xn[p], c), k.wT0[:, 0, :], start=False, stop=True,
                                       skip_group_check=True)
                    mm.then_inc(q_ps, 1)
                    pe.wait_ge(ctx_in[p], 80 * j + 80)
                    wait(pe, k_ok, 2 * i)
                    pe.matmul(psK[:, :], k.ones[:, :], k.bias_rows[1][:, :], start=True, stop=True)
                    for c in range(NC):
                        mm = pe.matmul(chunk(psK, c), chunk(ctx_n[p], c), k.wT0[:, 1, :], start=False,
                                       stop=True, skip_group_check=True)
                    mm.then_inc(k_ps, 1)
                    wait(pe, v_ok, 2 * i)
                    pe.matmul(psV[:, :], k.wT0[:, 2, :], ctx_h[p][:, :, :, :].rearrange("p b c k -> p (b c k)"),
                              start=True, stop=True).then_inc(v_ps, 1)
                if exists(t, TILES):
                    pe.wait_ge(pn_ok, t + 1)
                    for c in range(NC):
                        mm = pe.matmul(chunk(psW, c), chunk(pn, c), k.wT0[:, 3, :], start=True, stop=True)
                    mm.then_inc(w_ps, 1)
                if exists(i, TILES):
                    pe.wait_ge(q_ok, i + 1)
                    pe.wait_ge(k_ok, 2 * i + 2)
                    wait(pe, sh_ok, i)
                    for c in range(NC):
                        for b in range(2):
                            mm = pe.matmul(psS[HALF[b], c * P:(c + 1) * P], q_t[:, c * P + b * D:c * P + b * D + D],
                                           k_t[:, b, c, :, :], start=True, stop=True)
                    mm.then_inc(s_ps, 1)
                if exists(t, TILES):
                    pe.wait_ge(wp_ok, t + 1)
                    pe.wait_ge(v_ok, 2 * t + 2)
                    wait(pe, x_ok, t)
                    for c in range(NC):
                        for b in range(2):
                            mm = pe.matmul(psO[HALF[b], c * P:(c + 1) * P], wp[:, c * P + b * D:c * P + b * D + D],
                                           v_h[1 - p][:, b, c, :, :], start=True, stop=True)
                    mm.then_inc(o_ps, 1)

            sweep(pe, step, TILES, 1)


def ternary_weights(nc, a, k):
    with ExitStack() as ctx:
        s = Scope(nc, ctx, "tern")
        asum = s.sb("asum", [P, 3])
        mean = s.sb("mean", [P, 3])
        den = s.sb("den", [P, 3])
        inv = s.sb("inv", [P, 3])
        t0 = s.sb("t0", [P, TILES])
        beta = s.sb("beta", [P, TILES])
        ps = [s.ps(f"ps{i}", [P, 512]) for i in range(8)]
        psT, psM = ps[0:6], ps[7]
        (abs_ok, sum_ps, mean_ok, den_ok, inv_ok, q1_ok, q1_act, q2_ok, t_ps, ev_v, ev_a, sc_ok) = (s.sem(n) for n in (
            "abs_ok sum_ps mean_ok den_ok inv_ok q1_ok q1_act q2_ok t_ps ev_v ev_a sc_ok").split())
        vec_x, act_x = row_rstd(k, 1, lambda e: None)
        vec_w, act_w, pe_w, out0, out1 = later_weights(s, k, ps)
        block = s.block()
        raw = k.raw
        pieces, groups = [], []
        for n, dst in ((0, k.wgT), (1, k.wuT)):
            for f in range(0, FFC, 4):
                js = range(f, min(f + 4, FFC))
                width = min(FF, (f + 4) * P) - f * P
                for c in range(NC):
                    blocks = [(raw[n][0:min(P, FF - j * P), j, c * P:(c + 1) * P], (j - f) * P, min(P, FF - j * P))
                              for j in js]
                    groups.append((len(pieces), blocks, P, dst[:, c, f * P:f * P + width], width))
                pieces.append((n, raw[n][:, f:f + len(js), :]))
        for f in range(0, FFC, 4):
            js = range(f, min(f + 4, FFC))
            for j in js:
                rows = min(P, FF - j * P)
                blocks = [(raw[2][:, c, j * P:j * P + rows], c * P, P) for c in range(NC)]
                groups.append((len(pieces), blocks, rows, k.wdT[0:rows, j, :], L))
            pieces.append((2, raw[2][:, :, f * P:min(FF, (f + 4) * P)]))
        ON_ACT = (3,)

        def on_vector(g):
            return g % 3 == 0

        @block.gpsimd
        def _(pool):
            pool.wait_ge(inv_ok, 1)
            for m, (n, w) in enumerate(pieces):
                if m not in ON_ACT:
                    pool.tensor_scalar(w, w, inv[:, n:n + 1], ROUND, ALU.mult, ALU.add).then_inc(q1_ok, 1)

        @block.scalar
        def _(act):
            act_x(act)
            act_w(act)
            act.wait_ge(inv_ok, 1)
            for m in ON_ACT:
                n, w = pieces[m]
                act.activation(w, w, ACT.Identity, scale=inv[:, n:n + 1], bias=k.m_round[:, :]).then_inc(q1_act, 1)
            for g, (m, blocks, rows, dst, width) in enumerate(groups):
                if not on_vector(g):
                    act.wait_ge(t_ps, g + 1)
                    act.activation(dst, psT[g % 6][0:rows, 0:width], ACT.Identity,
                                   bias=k.m_minus[0:rows, :]).then_inc(ev_a, 1)

        @block.tensor
        def _(pe):
            pe.wait_ge(abs_ok, 1)
            pe.matmul(psM[:, 0:3], k.ones32[:, :], asum[:, :], start=True, stop=True).then_inc(sum_ps, 1)
            pe_w(pe)
            pe.wait_ge(out0, 12)
            pe.wait_ge(out1, 7)
            for g, (m, blocks, rows, dst, width) in enumerate(groups):
                pe.wait_ge(q2_ok, m + 1)
                if g >= 6:
                    u = g - 6
                    if on_vector(g):
                        pe.wait_ge(ev_v, u // 3 + 1)
                    else:
                        pe.wait_ge(ev_a, u // 3 * 2 + u % 3)
                for src, at, wide in blocks:
                    mm = pe.transpose(psT[g % 6][0:rows, at:at + wide], src, k.ident[0:src.shape[0], 0:src.shape[0]])
                mm.then_inc(t_ps, 1)

        @block.vector
        def _(dve):
            dve.tensor_reduce(asum[:, :], k.wabs[:, :, :], X, ALU.add).then_inc(abs_ok, 1)
            dve.wait_ge(sum_ps, 1)
            dve.tensor_scalar(mean[:, :], psM[:, 0:3], 1.0 / (FF * L), None, ALU.mult).then_inc(mean_ok, 1)
            dve.wait_ge(mean_ok, 1)
            dve.tensor_scalar(den[:, :], mean[:, :], EPS, None, ALU.add).then_inc(den_ok, 1)
            dve.wait_ge(den_ok, 1)
            dve.reciprocal(inv[:, :], den[:, :]).then_inc(inv_ok, 1)
            vec_x(dve)
            vec_w(dve)
            taken = [0]

            def take(m_before):
                while taken[0] < len(groups) and groups[taken[0]][0] < m_before:
                    g = taken[0]
                    m, blocks, rows, dst, width = groups[g]
                    if on_vector(g):
                        dve.wait_ge(t_ps, g + 1)
                        dve.tensor_scalar(dst, psT[g % 6][0:rows, 0:width], ROUND, None, ALU.subtract).then_inc(ev_v, 1)
                    taken[0] += 1

            for m, (n, w) in enumerate(pieces):
                if m in ON_ACT:
                    dve.wait_ge(q1_act, ON_ACT.index(m) + 1)
                else:
                    dve.wait_ge(q1_ok, m + 1 - sum(1 for q in ON_ACT if q < m))
                dve.tensor_scalar(w, w, ROUND + 1.0, ROUND - 1.0, ALU.min, ALU.max).then_inc(q2_ok, 1)
                take(m)
            n = [0]

            def link(ins):
                n[0] += 1
                ins.then_inc(sc_ok, 1)
                dve.wait_ge(sc_ok, n[0])

            w = k.ffw
            link(dve.tensor_tensor(w[:, :], mean[:, :], k.ffs[:, :], ALU.mult))
            link(dve.tensor_tensor(t0[:, :], k.xabs[:, :], k.rstd[:, :], ALU.mult))
            link(dve.tensor_scalar(beta[:, :], t0[:, :], 1.0 / L, None, ALU.mult))
            link(dve.tensor_scalar(t0[:, :], beta[:, :], EPS, None, ALU.add))
            link(dve.reciprocal(k.s4[:, :], t0[:, :]))
            link(dve.scalar_tensor_tensor(out=k.s4[:, :], in0=k.s4[:, :], scalar=SQRT7, in1=k.rstd[:, :], op0=ALU.mult,
                                          op1=ALU.mult))
            link(dve.tensor_scalar(k.sg[:, :], beta[:, :], w[:, 0:1], None, ALU.mult))
            link(dve.tensor_scalar(k.su[:, :], beta[:, :], w[:, 1:2], None, ALU.mult))
            link(dve.tensor_scalar(t0[:, :], k.su[:, :], -1.0, None, ALU.mult))
            link(dve.tensor_tensor(k.su_abs[:, :], k.su[:, :], t0[:, :], ALU.max))
            link(dve.tensor_scalar(k.sd[:, :], k.su_abs[:, :], w[:, 2:3], 1.0 / 127.0, ALU.mult, ALU.mult))
            link(dve.tensor_scalar(k.su[:, :], k.su[:, :], 127.0, None, ALU.mult))
            take(len(pieces))


def feed_forward(nc, a, k):
    with ExitStack() as ctx:
        s = Scope(nc, ctx, "ff")
        room = [w[:, :, :].rearrange("p a b -> p (a b)") for w in k.raw]
        y = room[0][:, 0:L]
        yr = [room[0][:, (p + 1) * L:(p + 2) * L] for p in range(2)]
        xq = [s.sb(f"xq{p}", [P, L], BF16) for p in range(2)]
        r1 = [room[0][:, (p + 3) * L:(p + 4) * L] for p in range(2)]
        r2 = [room[0][:, (p + 5) * L:(p + 6) * L] for p in range(2)]
        h = [room[1][:, p * FF:(p + 1) * FF] for p in range(2)]
        hr = room[2][:, 0:FF]
        hq = s.sb("hq", [P, FFC, P], BF16)
        gm = s.sb("gm", [P, 1])
        gd = s.sb("gd", [P, 1])
        gi = s.sb("gi", [P, 1])
        qs = s.sb("qs", [P, 1])
        os_ = [s.sb(f"os{p}", [P, 1]) for p in range(2)]
        stats = (s.sb("stats", [P, 6]), s.sb("mean_var", [P, 2]))
        ag_ok = s.sem("ag_ok")
        psX = s.ps("psX", [P, 512])
        psG = [s.ps(f"psG{i}", [P, 512]) for i in range(2)]
        psU = [s.ps(f"psU{i}", [P, 512]) for i in range(2)]
        psT = [s.ps(f"psT{i}", [P, 512]) for i in range(2)]
        psD = s.ps("psD", [P, 512])
        (y_ok, yr_ok, x_ps, xq_ok, g_ps, u_ps, r1_ok, r2_ok, h_ok, gm_ok, gd_ok, gi_ok, qs_ok, os_ok, hr_ok, t_ps, hq_a,
         hq_v, d_ps, x_ok, st_ok, mv_ok) = (s.sem(n) for n in (
             "y_ok yr_ok x_ps xq_ok g_ps u_ps r1_ok r2_ok h_ok gm_ok gd_ok gi_ok qs_ok os_ok hr_ok t_ps hq_a "
             "hq_v d_ps x_ok st_ok mv_ok").split())
        block = s.block()
        NB = len(FFB)
        TG = [range(f, min(f + 4, FFC)) for f in range(0, FFC, 4)]
        NG = len(TG)

        @block.sync
        def _(sp):
            sp.dma_start(k.cf[:, :], a["ctx"].rearrange("(t b) d l -> t (b d) l", b=2)[0]).then_inc(k.c_in, 16)

        @block.gpsimd
        def _(pool):
            def step(i, p, j):
                hold(pool, qs_ok, i + 1, k.passed)
                hold(pool, t_ps, NG * i, k.passed)
                pool.tensor_scalar(hr, h[p], qs[:, :], ROUND, ALU.mult, ALU.add).then_inc(hr_ok, 1)

            sweep(pool, step, TILES, 0)

        @block.vector
        def _(dve):
            def quantise(i, p):
                wait(dve, yr_ok, i)
                dve.tensor_scalar(y[:, :], k.x[:, i, :], k.mv[:, i, 0:1], k.s4[:, bass.ds(i, 1)], ALU.subtract,
                                  ALU.mult).then_inc(y_ok, 1)
                dve.wait_ge(y_ok, i + 1)
                wait(dve, x_ps, i - 1)
                dve.tensor_scalar(yr[p][:, :], y[:, :], ROUND, ROUND + 7.0, ALU.add, ALU.min).then_inc(yr_ok, 1)

            def take_x(i, p):
                dve.wait_ge(x_ps, i + 1)
                dve.tensor_scalar(xq[p][:, :], psX[:, :], ROUND, -8.0, ALU.subtract, ALU.max).then_inc(xq_ok, 1)

            def result(u, p):
                dve.wait_ge(d_ps, u + 1)
                dve.wait_ge(os_ok, u + 1)
                dve.scalar_tensor_tensor(out=k.x[:, u, :], in0=psD[:, :], scalar=os_[p][:, :], in1=k.x[:, u, :],
                                         op0=ALU.mult, op1=ALU.add).then_inc(x_ok, 1)

            def step(i, p, j):
                t, u = i - 1, i - 2
                if not exists(i, TILES):
                    result(u, p)
                    row_stats(dve, k, u, stats, x_ok, st_ok, ag_ok, mv_ok)
                if exists(i, TILES):
                    for n, (f0, f1) in enumerate(FFB):
                        if n == 1 and exists(u, TILES):
                            result(u, p)
                        if n == 2 and exists(u, TILES):
                            row_stats(dve, k, u, stats, x_ok, st_ok, ag_ok, mv_ok)
                        dve.wait_ge(r2_ok, NB * i + n + 1)
                        dve.wait_ge(u_ps, NB * i + n + 1)
                        if n == 0:
                            wait(dve, hr_ok, i - 1)
                        q = (NB * p + n) % 2
                        dve.tensor_tensor(h[p][:, f0:f1], psU[q][:, 0:f1 - f0], r2[q][:, 0:f1 - f0],
                                          ALU.mult).then_inc(h_ok, 1)
                if not exists(t, TILES) and exists(i + 1, TILES):
                    take_x(i + 1, 1 - p)
                if exists(t, TILES):
                    for n in (1, 2):
                        if n == 2 and exists(i + 1, TILES):
                            take_x(i + 1, 1 - p)
                        js = TG[n]
                        w = P * len(js)
                        dve.wait_ge(t_ps, NG * t + n + 1)
                        if n == 1:
                            dve.tensor_scalar(hq[:, js[0]:js[0] + 4, :].rearrange("p a b -> p (a b)"),
                                              psT[(NG * (1 - p) + n) % 2][:, 0:w], ROUND, None, ALU.subtract).then_inc(hq_v, 1)
                        else:
                            q = psT[(NG * (1 - p) + n) % 2]
                            dve.tensor_scalar(hq[:, js[0]:js[0] + 2, :].rearrange("p a b -> p (a b)"), q[:, 0:2 * P],
                                              ROUND, None, ALU.subtract).then_inc(hq_v, 1)
                            last = FF - (FFC - 1) * P
                            dve.tensor_scalar(hq[0:last, FFC - 1, :], q[0:last, 2 * P:3 * P], ROUND, None,
                                              ALU.subtract).then_inc(hq_v, 1)
                if exists(i, TILES):
                    dve.wait_ge(h_ok, NB * i + NB)
                    dve.tensor_reduce(gm[:, :], h[p][:, :], X, ALU.max, apply_absolute_value=True).then_inc(gm_ok, 1)
                    dve.wait_ge(gm_ok, i + 1)
                    dve.tensor_scalar(gd[:, :], gm[:, :], k.su_abs[:, bass.ds(i, 1)], EPS, ALU.mult, ALU.add).then_inc(gd_ok, 1)
                    wait(dve, x_ok, i - 1)
                    dve.tensor_scalar(os_[p][:, :], gm[:, :], k.sd[:, bass.ds(i, 1)], None, ALU.mult).then_inc(os_ok, 1)
                    dve.wait_ge(gd_ok, i + 1)
                    dve.reciprocal(gi[:, :], gd[:, :]).then_inc(gi_ok, 1)
                    dve.wait_ge(gi_ok, i + 1)
                    wait(dve, hr_ok, i)
                    dve.tensor_scalar(qs[:, :], gi[:, :], k.su[:, bass.ds(i, 1)], None, ALU.mult).then_inc(qs_ok, 1)
                if exists(i + 2, TILES):
                    quantise(i + 2, p)

            dve.sem_inc(mv_ok, 1)
            quantise(0, 0)
            quantise(1, 1)
            take_x(0, 0)
            sweep(dve, step, TILES, 2)

        @block.scalar
        def _(act):
            def gate(i, p, n):
                q = (NB * p + n) % 2
                w = FFB[n][1] - FFB[n][0]
                hold(act, g_ps, NB * i + n + 1, k.passed)
                act.activation(r1[q][:, 0:w], psG[q][:, 0:w], ACT.Relu,
                               scale=k.sg[:, bass.ds(i, 1)]).then_inc(r1_ok, 1)
                act.wait_ge(r1_ok, NB * i + n + 1)
                wait(act, h_ok, NB * i + n - 1)
                act.activation(r2[q][:, 0:w], r1[q][:, 0:w], ACT.Square).then_inc(r2_ok, 1)

            def step(i, p, j):
                t = i - 1
                if exists(i, TILES):
                    gate(i, p, 0)
                    gate(i, p, 1)
                    gate(i, p, 2)
                if exists(t, TILES):
                    act.wait_ge(t_ps, NG * t + 1)
                    act.activation(hq[:, 0:4, :].rearrange("p a b -> p (a b)"), psT[(NG * (1 - p)) % 2][:, :],
                                   ACT.Identity, bias=k.m_minus[:, :]).then_inc(hq_a, 1)

            sweep(act, step, TILES, 1)

        @block.tensor
        def _(pe):
            def x_up(i, p):
                pe.wait_ge(yr_ok, i + 1)
                wait(pe, xq_ok, i)
                for c in range(NC):
                    mm = pe.transpose(chunk(psX, c), chunk(yr[p], c), k.ident[:, :])
                mm.then_inc(x_ps, 1)

            def step(i, p, j):
                t = i - 1
                if exists(i, TILES):
                    pe.wait_ge(xq_ok, i + 1)
                    for n, (f0, f1) in enumerate(FFB):
                        q = (NB * p + n) % 2
                        wait(pe, r1_ok, NB * i + n - 1)
                        for c in range(NC):
                            mm = pe.matmul(psG[q][:, 0:f1 - f0], chunk(xq[p], c), k.wgT[:, c, f0:f1], start=c == 0,
                                           stop=c == NC - 1)
                        mm.then_inc(g_ps, 1)
                        wait(pe, h_ok, NB * i + n - 1)
                        for c in range(NC):
                            mm = pe.matmul(psU[q][:, 0:f1 - f0], chunk(xq[p], c), k.wuT[:, c, f0:f1], start=c == 0,
                                           stop=c == NC - 1)
                        mm.then_inc(u_ps, 1)
                if not exists(t, TILES):
                    x_up(i + 1, 1 - p)
                if exists(t, TILES):
                    pe.wait_ge(hr_ok, t + 1)
                    for n, js in enumerate(TG):
                        if n == NG - 1 and exists(i + 1, TILES):
                            x_up(i + 1, 1 - p)
                        if n == 0:
                            wait(pe, hq_v, 3 * t - 2)
                        elif n == 1:
                            wait(pe, hq_v, 3 * t)
                        else:
                            pe.wait_ge(hq_a, t + 1)
                        for m in js:
                            w = min(P, FF - m * P)
                            mm = pe.transpose(psT[(NG * (1 - p) + n) % 2][0:w, (m - js[0]) * P:(m - js[0] + 1) * P],
                                              hr[:, m * P:m * P + w], k.ident[:, :])
                        mm.then_inc(t_ps, 1)
                    wait(pe, x_ok, t)
                    pe.wait_ge(hq_a, t + 1)
                    for m in range(FFC):
                        if m == 4:
                            pe.wait_ge(hq_v, 3 * t + 1)
                        elif m == 8:
                            pe.wait_ge(hq_v, 3 * t + 3)
                        w = min(P, FF - m * P)
                        mm = pe.matmul(psD[:, :], hq[0:w, m, :], k.wdT[0:w, m, :], start=m == 0, stop=m == FFC - 1)
                    mm.then_inc(d_ps, 1)

            x_up(0, 0)
            sweep(pe, step, TILES, 1)


def split_shift(dve, m, part, rest, sems, n):
    p_ok, r_ok = sems
    w = m.shape[2]
    dve.tensor_scalar(part[:, :, 0:w], m, -1.0, None, ALU.mult).then_inc(p_ok, 1)
    dve.wait_ge(p_ok, 3 * n + 1)
    dve.scalar_tensor_tensor(out=rest, in0=m, scalar=-1.0, in1=part[:, :, 0:w], op0=ALU.mult,
                             op1=ALU.subtract).then_inc(r_ok, 1)
    dve.wait_ge(r_ok, n + 1)
    dve.tensor_copy(part[:, :, 32:32 + w], rest).then_inc(p_ok, 1)
    dve.wait_ge(p_ok, 3 * n + 2)
    dve.tensor_tensor(part[:, :, 64:64 + w], rest, part[:, :, 32:32 + w], ALU.subtract).then_inc(p_ok, 1)


def key_side(nc, a, k):
    with ExitStack() as ctx:
        s = Scope(nc, ctx, "keys")
        cf, c_in = k.cf, k.c_in
        cs = [s.sb(f"cs{h}", [P, L], F16) for h in range(2)]
        cT = [s.sb(f"cT{h}", [P, NC, P], F16) for h in range(2)]
        mk = s.sb("mk", [P, NC])
        ek = [s.sb(f"ek{h}", [P, NC, L]) for h in range(2)]
        le = [s.sb(f"le{h}", [P, NC]) for h in range(2)]
        e_hi = s.sb("e_hi", [P, NC, L], F16)
        e_lo = s.sb("e_lo", [P, NC, L], F16)
        gT = s.sb("gT", [P, L])
        rl = [s.sb(f"rl{h}", [P, NC]) for h in range(2)]
        psC = s.ps("psC", [P, NC, P], F16)
        psK = [s.ps(f"psK{i}", [P, 512]) for i in range(2)]
        psT = [s.ps(f"psT{i}", [P, 512]) for i in range(2)]
        psG = s.ps("psG", [P, 512])
        psM = s.ps("psM", [P, NC, D])
        (hi_ok, lo_ok, c_ps, cT_ok, k_ps, mk_ok, ek_ok, t_ps, ehi_ok, elo_ok, g_ps, gT_ok, m_ps, rl_ok,
         M_ok) = (s.sem(n) for n in (
             "hi_ok lo_ok c_ps cT_ok k_ps mk_ok ek_ok t_ps ehi_ok elo_ok g_ps gT_ok m_ps rl_ok M_ok").split())
        block = s.block()
        nat = a["ctx"].rearrange("(t b) d l -> t (b d) l", b=2)

        @block.sync
        def _(sp):
            def step(t, p, j):
                if not isinstance(t, int) or t > 0:
                    sp.wait_ge(lo_ok, 2 * t)
                    sp.dma_start(cf[:, :], nat[t]).then_inc(c_in, 16)

            sweep(sp, step, TILES, 0)

        @block.gpsimd
        def _(pool):
            def step(b, h, t):
                hold(pool, c_in, 16 * t + 16, k.passed)
                r = HALF[h]
                hold(pool, k_ps, NC * (b - 1), k.passed)
                hold(pool, c_ps, b - 1, k.passed)
                pool.tensor_scalar(cs[h][r, :], cf[r, :], 1.0, 0.0, ALU.mult, ALU.add).then_inc(hi_ok, 1)

            sweep(pool, step, BATCHES, 0, unroll=4)

        @block.vector
        def _(dve):
            def low(b, h):
                dve.wait_ge(hi_ok, b + 1)
                dve.tensor_tensor(cs[h][HALF[1 - h], :], cf[HALF[h], :], cs[h][HALF[h], :],
                                  ALU.subtract).then_inc(lo_ok, 1)

            def keys_max(b, c):
                dve.wait_ge(k_ps, NC * b + c + 1)
                wait(dve, ek_ok, NC * (b - 1) + c + 1)
                dve.tensor_reduce(mk[:, c:c + 1], psK[c % 2][:, :], X, ALU.max, negate=True).then_inc(mk_ok, 1)

            def exp_low(b, j):
                dve.wait_ge(ehi_ok, NC * b + j + 1)
                wait(dve, g_ps, NC * (b - 1) + j + 1)
                dve.tensor_tensor(e_lo[:, j, :], psT[j % 2][:, :], e_hi[:, j, :], ALU.subtract).then_inc(elo_ok, 1)

            def sums(b, h):
                dve.wait_ge(ek_ok, NC * b + NC)
                wait(dve, M_ok, b - 1)
                dve.reciprocal(rl[h][:, :], le[h][:, :]).then_inc(rl_ok, 1)

            def matrix(b, h):
                dve.wait_ge(rl_ok, b + 1)
                dve.wait_ge(m_ps, b + 1)
                dve.tensor_tensor(k.M[:, b, :, :], psM[:, :, :], rl[h][:, :].unsqueeze(2).broadcast_to([P, NC, D]),
                                  ALU.mult).then_inc(M_ok, 1)

            def step(b, h, t):
                for c in range(NC):
                    if exists(b + 1 + (c + 1) // NC, BATCHES):
                        keys_max(b + 1 + (c + 1) // NC, (c + 1) % NC)
                    if exists(b, BATCHES):
                        exp_low(b, c)
                    if c == 0 and exists(b, BATCHES):
                        sums(b, h)
                    if c == 1 and exists(b + 2, BATCHES):
                        low(b + 2, h)
                    if c == 2 and exists(b - 1, BATCHES):
                        matrix(b - 1, 1 - h)

            low(0, 0)
            low(1, 1)
            for c in range(NC + 1):
                keys_max(c // NC, c % NC)
            sweep(dve, step, BATCHES, 1, unroll=4)

        @block.scalar
        def _(act):
            def transposed(b, h):
                act.wait_ge(c_ps, b + 1)
                wait(act, g_ps, NC * (b - 1))
                act.activation(cT[h][:, :, :], psC[:, :, :], ACT.Copy).then_inc(cT_ok, 1)

            def exponentials(b, h, c):
                act.wait_ge(mk_ok, NC * b + c + 1)
                wait(act, t_ps, NC * (b - 1))
                wait(act, rl_ok, b - 1)
                act.activation(ek[h][:, c, :], psK[c % 2][:, :], ACT.Exp, bias=mk[:, c:c + 1],
                               accum_out=le[h][:, c:c + 1]).then_inc(ek_ok, 1)

            def step(b, h, t):
                for c in range(NC):
                    if exists(b, BATCHES):
                        act.wait_ge(t_ps, NC * b + c + 1)
                        wait(act, g_ps, NC * (b - 1) + c + 1)
                        act.activation(e_hi[:, c, :], psT[c % 2][:, :], ACT.Copy).then_inc(ehi_ok, 1)
                    if exists(b + 1 + (c + 1) // NC, BATCHES):
                        exponentials(b + 1 + (c + 1) // NC, (h + 1 + (c + 1) // NC) % 2, (c + 1) % NC)
                    if c == 0 and exists(b - 1, BATCHES):
                        act.wait_ge(g_ps, NC * b)
                        wait(act, m_ps, b - 1)
                        act.activation(gT[:, :], psG[:, :], ACT.Copy).then_inc(gT_ok, 1)
                    if c == 1 and exists(b + 1, BATCHES):
                        transposed(b + 1, 1 - h)

            for c in range(NC + 1):
                exponentials(c // NC, c // NC, c % NC)
                if c == 2:
                    transposed(0, 0)
            sweep(act, step, BATCHES, 1, unroll=4)

        @block.tensor
        def _(pe):
            def context(b, h):
                pe.wait_ge(lo_ok, b + 1)
                wait(pe, cT_ok, b)
                for c in range(NC):
                    mm = pe.transpose(psC[:, c, :], chunk(cs[h], c), k.ident_h[:, :])
                mm.then_inc(c_ps, 1)

            def keys(b, h, c):
                pe.wait_ge(lo_ok, b + 1)
                wait(pe, ek_ok, NC * b + c - 1)
                pe.matmul(psK[c % 2][:, :], chunk(k.wk_hi, c), cs[h][:, :], start=True, stop=False)
                pe.matmul(psK[c % 2][:, :], chunk(k.wk_lo, c), cs[h][:, :], start=False, stop=True).then_inc(k_ps, 1)

            def turn(b, h, j):
                pe.wait_ge(ek_ok, NC * b + NC)
                wait(pe, elo_ok, NC * b + j - 1)
                for c in range(NC):
                    mm = pe.transpose(chunk(psT[j % 2], c), chunk(ek[h][:, c, :], j), k.ident[:, :])
                mm.then_inc(t_ps, 1)

            def gather(b, h, j):
                if j == 0:
                    pe.wait_ge(cT_ok, b + 1)
                    wait(pe, gT_ok, b)
                pe.wait_ge(elo_ok, NC * b + j + 1)
                pe.matmul(psG[:, :], cT[h][:, j, :], e_hi[:, j, :], start=j == 0, stop=True, skip_group_check=True)
                mm = pe.matmul(psG[HALF[h], :], cT[h][:, j, h * D:(h + 1) * D], e_lo[:, j, :], start=False, stop=True,
                               skip_group_check=True)
                mm.then_inc(g_ps, 1)

            def matrix(b):
                pe.wait_ge(gT_ok, b + 1)
                wait(pe, M_ok, b)
                for n in range(HEADS):
                    mm = pe.matmul(psM[HALF[n % 2], n // 2, :], gT[:, n * D:(n + 1) * D], k.wv_wo[:, n, :],
                                   start=True, stop=True)
                mm.then_inc(m_ps, 1)

            def step(b, h, t):
                for c in range(NC):
                    if exists(b, BATCHES):
                        turn(b, h, c)
                    if exists(b + 1 + (c + 1) // NC, BATCHES):
                        keys(b + 1 + (c + 1) // NC, (h + 1 + (c + 1) // NC) % 2, (c + 1) % NC)
                    if c > 0 and exists(b, BATCHES):
                        gather(b, h, c - 1)
                    if c == 0 and exists(b - 1, BATCHES):
                        gather(b - 1, 1 - h, NC - 1)
                    if c == 1 and exists(b + 1, BATCHES):
                        context(b + 1, 1 - h)
                    if c == 2 and exists(b - 1, BATCHES):
                        matrix(b - 1)

            for c in range(NC + 1):
                keys(c // NC, c // NC, c % NC)
                if c == 0:
                    context(0, 0)
            sweep(pe, step, BATCHES, 1, unroll=4)


def query_side(nc, a, k):
    with ExitStack() as ctx:
        s = Scope(nc, ctx, "query")
        gbo = s.sb("gbo", [P, 1])
        xn = s.sb("xn", [P, L])
        xs = [s.sb(f"xs{h}", [P, L], F16) for h in range(2)]
        mq = s.sb("mq", [P, NC, HEADS])
        mpart = s.sb("mpart", [P, NC, 96], BF16)
        mrest = s.sb("mrest", [P, NC, HEADS])
        mT = s.sb("mT", [96, L], BF16)
        eq = [s.sb(f"eq{h}", [P, NC, L]) for h in range(2)]
        qn = [s.sb(f"qn{h}", [P, NC, L]) for h in range(2)]
        lq = s.sb("lq", [P, NC, HEADS])
        rq = s.sb("rq", [P, NC, HEADS])
        qT = [s.sb(f"qT{h}", [P, NC, L]) for h in range(2)]
        m_sb = [s.sb(f"m_sb{h}", [P, NC, D]) for h in range(2)]
        y = s.sb("y", [P, L])
        sq = s.sb("sq", [P, L])
        ln = s.sb("ln", [P, L])
        inv = s.sb("inv", [P, L])
        z = s.sb("z", [P, L])
        stats = (s.sb("stats", [P, 6]), s.sb("mean_var", [P, 2]))
        ag_ok = s.sem("ag_ok")
        psQ = [s.ps(f"psQ{i}", [P, 512]) for i in range(NC)]
        psR = s.ps("psR", [P, 1024], BF16)
        psX = [s.ps(f"psX{i}", [P, 512]) for i in range(2)]
        psF = s.ps("psF", [P, 512])
        (init_ok, xn_ok, hi_ok, lo_ok, q_ps, mq_ok, part_ok, rest_ok, r_ps, mT_ok, f_ps, eq_ok, lq_ok, rq_ok, qn_ok,
         x_ps, qT_ok, msb_ok, o_ps, y_ok, sq_ok, ss_ps, ln_ok, inv_ok, z_ok, x_ok, st_ok, mv_ok) = (s.sem(n) for n in (
             "init_ok xn_ok hi_ok lo_ok q_ps mq_ok part_ok rest_ok r_ps mT_ok f_ps eq_ok lq_ok rq_ok qn_ok "
             "x_ps qT_ok msb_ok o_ps y_ok sq_ok ss_ps ln_ok inv_ok z_ok x_ok st_ok mv_ok").split())
        vec_x, act_x = row_rstd(k, 2, lambda e: None)
        block = s.block()

        def heads(ap):
            return ap.rearrange("p (h d) -> p h d", h=HEADS)

        @block.vector
        def _(dve):
            def low(b, h):
                dve.wait_ge(hi_ok, b + 1)
                dve.tensor_tensor(xs[h][HALF[1 - h], :], xn[HALF[h], :], xs[h][HALF[h], :],
                                  ALU.subtract).then_inc(lo_ok, 1)

            def queries_max(b):
                for c in range(NC):
                    dve.wait_ge(q_ps, NC * b + c + 1)
                    dve.tensor_reduce(mq[:, c, :], heads(psQ[c][:, :]), X, ALU.max).then_inc(mq_ok, 1)
                dve.wait_ge(mq_ok, NC * b + NC)
                wait(dve, r_ps, b)
                split_shift(dve, mq[:, :, :], mpart, mrest[:, :, :], (part_ok, rest_ok), b)

            def step(b, h, t):
                if h == 0 and exists(t + 1, TILES):
                    normed(t + 1)
                if exists(b + 1, BATCHES):
                    queries_max(b + 1)
                if h == 0 and exists(t + 1, TILES):
                    low(b + 2, 0)
                if exists(b, BATCHES):
                    wait(dve, rq_ok, b)
                    for c in range(NC):
                        dve.wait_ge(eq_ok, NC * b + c + 1)
                        dve.tensor_reduce(lq[:, c, :], heads(eq[h][:, c, :]), X, ALU.add).then_inc(lq_ok, 1)
                    dve.wait_ge(lq_ok, NC * b + NC)
                    wait(dve, qn_ok, NC * b)
                    dve.reciprocal(rq[:, :, :], lq[:, :, :]).then_inc(rq_ok, 1)
                if exists(b - 1, BATCHES):
                    matrix(b - 1, 1 - h)
                if h == 0 and exists(t + 1, TILES):
                    low(b + 3, 1)
                if h == 1 and exists(t - 2, TILES):
                    row_stats(dve, k, t - 2, stats, x_ok, st_ok, ag_ok, mv_ok)
                if h == 0 and exists(t - 2, TILES):
                    u = t - 2
                    dve.wait_ge(inv_ok, u + 1)
                    wait(dve, x_ok, u)
                    dve.scalar_tensor_tensor(out=z[:, :], in0=inv[:, :], scalar=1e12, in1=y[:, :], op0=ALU.min,
                                             op1=ALU.mult).then_inc(z_ok, 1)

            def normed(t):
                wait(dve, lo_ok, 2 * t)
                wait(dve, hi_ok, 2 * t)
                dve.tensor_scalar(xn[:, :], k.x[:, t, :], k.mv[:, t, 0:1], k.rstd[:, bass.ds(t, 1)], ALU.subtract,
                                  ALU.mult).then_inc(xn_ok, 1)

            def matrix(b, h):
                wait(dve, o_ps, b - 1)
                dve.tensor_scalar(m_sb[h][:, :, :], k.M[:, b, :, :], 1.0, None, ALU.mult).then_inc(msb_ok, 1)

            dve.sem_inc(mv_ok, 1)
            dve.memset(mpart[:, :, :], 0.0).then_inc(init_ok, 1)
            dve.tensor_tensor(gbo[:, :], k.g8[:, :], k.bo1[:, :], ALU.mult).then_inc(init_ok, 1)
            dve.wait_ge(init_ok, 2)
            vec_x(dve)
            normed(0)
            low(0, 0)
            low(1, 1)
            queries_max(0)
            sweep(dve, step, BATCHES, 4, head=4, unroll=4)

        @block.gpsimd
        def _(pool):
            def step(b, h, t):
                if exists(b, BATCHES):
                    for c in range(NC):
                        pool.wait_ge(rq_ok, b + 1)
                        wait(pool, x_ps, NC * (b - 2) + c + 1)
                        pool.tensor_tensor(heads(qn[h][:, c, :]), heads(eq[h][:, c, :]),
                                           rq[:, c, :].unsqueeze(2).broadcast_to([P, HEADS, D]),
                                           ALU.mult).then_inc(qn_ok, 1)
                if h == 0 and exists(t - 2, TILES):
                    hold(pool, z_ok, t - 1, k.passed)
                    pool.tensor_tensor(k.x[:, t - 2, :], k.x[:, t - 2, :], z[:, :], ALU.add).then_inc(x_ok, 1)

            sweep(pool, step, BATCHES, 3, head=4, unroll=4)

        @block.scalar
        def _(act):
            def high(b, h, t):
                act.wait_ge(xn_ok, t + 1)
                wait(act, q_ps, NC * (b - 1))
                act.activation(xs[h][HALF[h], :], xn[HALF[h], :], ACT.Copy).then_inc(hi_ok, 1)

            def shift(b):
                act.wait_ge(r_ps, b + 1)
                act.activation(mT[:, :], psR[0:96, 0:L], ACT.Copy).then_inc(mT_ok, 1)

            def transposed(b, h, c):
                act.wait_ge(x_ps, NC * b + c + 1)
                wait(act, o_ps, b - 1)
                act.activation(qT[h][:, :, c * P:(c + 1) * P], psX[c % 2][:, :].rearrange("p (j n) -> p j n", j=NC),
                               ACT.Copy).then_inc(qT_ok, 1)

            def exponentials(b, h):
                for c in range(NC):
                    act.wait_ge(f_ps, NC * b + c + 1)
                    wait(act, qn_ok, NC * (b - 2) + c + 1)
                    act.activation(eq[h][:, c, :], psQ[c][:, :], ACT.Exp).then_inc(eq_ok, 1)

            def step(b, h, t):
                for c in range(NC):
                    if exists(b - 2, BATCHES):
                        transposed(b - 2, h, c)
                    if c == 1 and h == 0 and exists(t - 2, TILES):
                        act.wait_ge(ss_ps, t - 1)
                        wait(act, z_ok, t - 2)
                        act.activation(ln[:, :], psF[:, :], ACT.Ln, scale=2.0 ** LN_SCALE).then_inc(ln_ok, 1)
                    if c in (1, 3) and h == 0 and exists(t + 1, TILES):
                        high(b + 2 + c // 2, c // 2, t + 1)
                if h == 0 and exists(t - 2, TILES):
                    act.wait_ge(ln_ok, t - 1)
                    act.activation(inv[:, :], ln[:, :], ACT.Exp, scale=-0.5, bias=k.half_ln[:, :]).then_inc(inv_ok, 1)
                if exists(b + 1, BATCHES):
                    shift(b + 1)
                    exponentials(b + 1, 1 - h)
                if h == 1 and exists(t - 1, TILES):
                    act.wait_ge(o_ps, 2 * t)
                    wait(act, z_ok, t - 1)
                    act.activation(y[:, :], psF[:, :], ACT.Identity, scale=k.g8[:, :], bias=gbo[:, :]).then_inc(y_ok, 1)
                    act.activation(sq[:, :], psF[:, :], ACT.Square, bias=k.bo1[:, :]).then_inc(sq_ok, 1)

            act.wait_ge(init_ok, 2)
            act_x(act)
            high(0, 0, 0)
            high(1, 1, 0)
            shift(0)
            exponentials(0, 0)
            sweep(act, step, BATCHES, 3, head=4, unroll=4)

        @block.tensor
        def _(pe):
            def queries(b, h, c):
                pe.wait_ge(lo_ok, b + 1)
                wait(pe, eq_ok, NC * (b - 1) + c + 1)
                pe.matmul(psQ[c][:, :], chunk(xs[h], c), k.wq_hi[:, :], start=True, stop=False)
                pe.matmul(psQ[c][:, :], chunk(xs[h], c), k.wq_lo[:, :], start=False, stop=True).then_inc(q_ps, 1)

            def shift(b):
                pe.wait_ge(part_ok, 3 * b + 3)
                wait(pe, mT_ok, b)
                for c in range(NC):
                    mm = pe.transpose(psR[0:96, c * P:(c + 1) * P], mpart[:, c, :], k.ident16[:, :])
                mm.then_inc(r_ps, 1)

            def fold(b):
                pe.wait_ge(mT_ok, b + 1)
                for c in range(NC):
                    pe.matmul(psQ[c][:, :], chunk(mT, c), k.ind[0:96, :], start=False, stop=True,
                              skip_group_check=True).then_inc(f_ps, 1)

            def turn(b, h, c):
                pe.wait_ge(qn_ok, NC * b + c + 1)
                wait(pe, qT_ok, NC * b + c - 1)
                for j in range(NC):
                    mm = pe.transpose(chunk(psX[c % 2], j), chunk(qn[h][:, c, :], j), k.ident[:, :])
                mm.then_inc(x_ps, 1)

            def out(b, h, j):
                if j == 0:
                    pe.wait_ge(msb_ok, b + 1)
                    pe.wait_ge(qT_ok, NC * b + NC)
                mm = pe.matmul(psF[HALF[h], :], m_sb[h][:, j, :], qT[h][:, j, :], start=j == 0, stop=j == NC - 1)
                if j == NC - 1:
                    mm.then_inc(o_ps, 1)

            def step(b, h, t):
                if exists(b + 1, BATCHES):
                    queries(b + 1, 1 - h, 0)
                for c in range(NC):
                    if c + 1 < NC and exists(b + 1, BATCHES):
                        queries(b + 1, 1 - h, c + 1)
                    if exists(b - 2, BATCHES):
                        turn(b - 2, h, c)
                    if c >= 2 and h == 1 and exists(b - 3, BATCHES):
                        out(b - 3, 0, c)
                    if c == 1 and h == 0 and exists(t - 2, TILES):
                        pe.wait_ge(sq_ok, t - 1)
                        pe.wait_ge(y_ok, t - 1)
                        pe.matmul(psF[:, :], k.blk[:, :], sq[:, :], start=True, stop=True).then_inc(ss_ps, 1)
                if h == 0:
                    if exists(b + 1, BATCHES):
                        shift(b + 1)
                    if exists(b - 2, BATCHES):
                        wait(pe, ln_ok, t - 1)
                        out(b - 2, 0, 0)
                    if exists(b + 1, BATCHES):
                        fold(b + 1)
                    if exists(b - 2, BATCHES):
                        out(b - 2, 0, 1)
                else:
                    if exists(b - 2, BATCHES):
                        out(b - 2, 1, 0)
                        out(b - 2, 1, 1)
                    if exists(b + 1, BATCHES):
                        shift(b + 1)
                    if exists(b - 2, BATCHES):
                        out(b - 2, 1, 2)
                        out(b - 2, 1, 3)
                    if exists(b + 1, BATCHES):
                        fold(b + 1)

            for c in range(NC):
                queries(0, 0, c)
            shift(0)
            fold(0)
            sweep(pe, step, BATCHES, 3, head=4, unroll=4)


def projection(nc, a, k):
    with ExitStack() as ctx:
        s = Scope(nc, ctx, "proj")
        x_s = [s.sb(f"x_s{p}", [P, L]) for p in range(2)]
        x_hi = [s.sb(f"x_hi{p}", [P, NC, P], F16) for p in range(2)]
        x_lo = [s.sb(f"x_lo{p}", [P, NC, P], F16) for p in range(2)]
        psT = [s.ps(f"psT{i}", [P, 512]) for i in range(2)]
        psH = [s.ps(f"psH{i}", [P, 512]) for i in range(2)]
        psZ = [s.ps(f"psZ{i}", [P, 512]) for i in range(2)]
        t_ps, xs_ok, xhi_ok, xlo_ok, z_ps, z_ok, h_ps, hs_ok, x_ok = (s.sem(n) for n in (
            "t_ps xs_ok xhi_ok xlo_ok z_ps z_ok h_ps hs_ok x_ok").split())
        vec_x, act_x = row_rstd(k, 3, lambda e: None)
        block = s.block()

        @block.scalar
        def _(act):
            def high(i, p):
                act.wait_ge(t_ps, i + 1)
                wait(act, h_ps, i - 1)
                act.activation(x_hi[p][:, :, :].rearrange("p a b -> p (a b)"), psT[p][:, :], ACT.Copy).then_inc(xhi_ok, 1)

            def step(i, p, j):
                if exists(i + 1, TILES):
                    high(i + 1, 1 - p)
                hold(act, z_ps, i + 1, k.passed)
                act.activation(k.zT[:, i, :], psZ[p][:, 0:P], ACT.Copy, scale=1.0 / W_SCALE).then_inc(z_ok, 1)

            act_x(act)
            high(0, 0)
            sweep(act, step, TILES, 0)

        @block.vector
        def _(dve):
            def normed(i, p):
                wait(dve, t_ps, i - 1)
                dve.tensor_scalar(x_s[p][:, :], k.x[:, i, :], k.mv[:, i, 0:1], k.rstd[:, bass.ds(i, 1)], ALU.subtract,
                                  ALU.mult).then_inc(xs_ok, 1)

            def low(i, p):
                dve.wait_ge(xhi_ok, i + 1)
                dve.tensor_tensor(x_lo[p][:, :, :].rearrange("p a b -> p (a b)"), psT[p][:, :],
                                  x_hi[p][:, :, :].rearrange("p a b -> p (a b)"), ALU.subtract).then_inc(xlo_ok, 1)

            def step(i, p, j):
                if exists(i + 1, TILES):
                    low(i + 1, 1 - p)
                if exists(i + 2, TILES):
                    normed(i + 2, p)
                dve.wait_ge(h_ps, i + 1)
                dve.tensor_scalar(k.Hs[:, i, :], psH[p][:, 0:EXPERTS], 1.0 / W_SCALE, None, ALU.mult).then_inc(hs_ok, 1)
                dve.scalar_tensor_tensor(out=k.x[:, i, :], in0=psH[p][:, :], scalar=1.0 / W_SCALE, in1=k.x[:, i, :],
                                         op0=ALU.mult, op1=ALU.add).then_inc(x_ok, 1)

            vec_x(dve)
            normed(0, 0)
            normed(1, 1)
            low(0, 0)
            sweep(dve, step, TILES, 0)

        @block.tensor
        def _(pe):
            def up(i, p):
                pe.wait_ge(xs_ok, i + 1)
                wait(pe, xlo_ok, i - 1)
                for c in range(NC):
                    mm = pe.transpose(chunk(psT[p], c), chunk(x_s[p], c), k.ident[:, :])
                mm.then_inc(t_ps, 1)

            def step(i, p, j):
                if exists(i + 1, TILES):
                    up(i + 1, 1 - p)
                pe.wait_ge(xlo_ok, i + 1)
                wait(pe, z_ok, i - 1)
                parts = ((k.A_hi, x_hi[p]), (k.A_lo, x_hi[p]), (k.A_hi, x_lo[p]))
                for m, (w, xT) in enumerate(parts):
                    for c in range(NC):
                        mm = pe.matmul(psZ[p][:, 0:P], w[:, c, :], xT[:, c, :], start=m == 0 and c == 0,
                                       stop=m == 2 and c == NC - 1)
                mm.then_inc(z_ps, 1)
                wait(pe, x_ok, i - 1)
                pe.matmul(psH[p][:, :], k.ones[:, :], k.bias_rows[2][:, :], start=True, stop=False)
                parts = ((x_hi[p], k.WT_hi), (x_hi[p], k.WT_lo), (x_lo[p], k.WT_hi))
                for m, (xT, w) in enumerate(parts):
                    for c in range(NC):
                        mm = pe.matmul(psH[p][:, :], xT[:, c, :], w[:, c, :], start=False,
                                       stop=m == 2 and c == NC - 1)
                mm.then_inc(h_ps, 1)

            up(0, 0)
            sweep(pe, step, TILES, 0)


def experts(nc, a, k):
    TE = [P, TILES, EXPERTS]
    with ExitStack() as ctx:
        s = Scope(nc, ctx, "exp")
        dl = s.sb("dl", TE)
        mx2 = s.sb("mx2", [P, 2])
        diag = s.sb("diag", [2, 3])
        ones2 = s.sb("ones2", [2, P])
        sc = s.sb("sc", [P, 2])
        lg, e, pr, w, u = (s.sb("d2" + n, TE) for n in "lepwu")
        r = s.sb("r", [P, TILES])
        top = s.sb("top", [P, TILES, 8])
        wf = s.sb("wf", [P, TILES, RANK])
        wT = s.sb("wT", [P, 4, P])
        zp = s.sb("zp", [P, TILES * P])
        zs = s.sb("zs", [P, TILES * P], F16)
        psA = s.ps("psA", [P, 512])
        psB = s.ps("psB", [P, 512])
        psP = s.ps("psP", [P, 4, 512])
        psD = [psA, psB, s.ps("psD2", [P, 512]), s.ps("psD3", [P, 512])]
        order = [4 * g + q for q in range(4) for g in range(TILES // 4)]
        a_ps, lnk, act_ok, p_ps, zp_ok, zs_ok, z_fin, d_ps, o_ok = (
            s.sem(n) for n in "a_ps lnk act_ok p_ps zp_ok zs_ok z_fin d_ps o_ok".split())
        wT_ps, wT_ok, done_v = (s.sem(n) for n in ("wT_ps", "wT_ok", "done_v"))
        store = s.sem("store")
        block = s.block()
        out = a["out"].rearrange("(t b) d l -> t (b d) l", b=2)

        def te(ap):
            return ap.unsqueeze(2).broadcast_to(TE)

        @block.vector
        def _(dve):
            n = [0]

            def link(ins):
                n[0] += 1
                ins.then_inc(lnk, 1)
                dve.wait_ge(lnk, n[0])

            link(dve.memset(ones2[:, :], 1.0))
            link(dve.memset(wf[:, :, :], 0.0))
            dve.wait_ge(a_ps, 1)
            link(dve.tensor_copy(dl[:, :, :], psA[:, 0:P].rearrange("p (t e) -> p t e", t=TILES)))
            for m, v in enumerate((k.Hs, dl)):
                link(dve.tensor_reduce(mx2[:, m:m + 1], v[:, :, :].rearrange("p a b -> p (a b)"), X, ALU.max,
                                       apply_absolute_value=True))
            link(dve.tensor_scalar(mx2[:, :], mx2[:, :], k.odd[:, :], None, ALU.mult))
            dve.sem_inc(done_v, 1)
            dve.wait_ge(a_ps, 2)
            link(dve.tensor_reduce(diag[:, 2:3], psB[0:2, 0:P], X, ALU.max))
            link(dve.tensor_scalar(diag[:, 2:3], diag[:, 2:3], 1e-6, None, ALU.max))
            link(dve.reciprocal(diag[:, 2:3], diag[:, 2:3]))
            link(dve.tensor_scalar(diag[:, 0:2], k.ident[0:2, 0:2], diag[:, 2:3], 0.5, ALU.mult, ALU.mult))
            dve.sem_inc(done_v, 1)
            dve.wait_ge(a_ps, 3)
            link(dve.tensor_copy(sc[:, :], psA[:, 256:258]))
            link(dve.tensor_scalar(lg[:, :, :], k.Hs[:, :, :], sc[:, 0:1], None, ALU.mult))
            link(dve.scalar_tensor_tensor(out=lg[:, :, :], in0=dl[:, :, :], scalar=sc[:, 1:2], in1=lg[:, :, :],
                                          op0=ALU.mult, op1=ALU.add))
            link(dve.tensor_reduce(r[:, :], lg[:, :, :], X, ALU.max))
            link(dve.tensor_tensor(lg[:, :, :], lg[:, :, :], te(r[:, :]), ALU.subtract))
            dve.sem_inc(done_v, 1)
            dve.wait_ge(act_ok, 1)
            link(dve.tensor_reduce(r[:, :], e[:, :, :], X, ALU.add))
            link(dve.reciprocal(r[:, :], r[:, :]))
            link(dve.tensor_tensor(pr[:, :, :], e[:, :, :], te(r[:, :]), ALU.mult))
            for t in range(TILES):
                dve.max(top[:, t, :], pr[:, t, :]).then_inc(lnk, 1)
            n[0] += TILES
            dve.wait_ge(lnk, n[0])
            link(dve.tensor_tensor(u[:, :, :], pr[:, :, :], top[:, :, 1:2].broadcast_to(TE), ALU.subtract))
            dve.sem_inc(done_v, 1)
            dve.wait_ge(act_ok, 2)
            link(dve.tensor_scalar(w[:, :, :], w[:, :, :], 1.0, None, ALU.add))
            link(dve.reciprocal(w[:, :, :], w[:, :, :]))
            link(dve.tensor_tensor(w[:, :, :], w[:, :, :], pr[:, :, :], ALU.mult))
            link(dve.tensor_reduce(r[:, :], w[:, :, :], X, ALU.add))
            link(dve.tensor_scalar(r[:, :], r[:, :], 1e-9, None, ALU.add))
            link(dve.reciprocal(r[:, :], r[:, :]))
            link(dve.tensor_tensor(wf[:, :, 0:EXPERTS], w[:, :, :], te(r[:, :]), ALU.mult))
            dve.sem_inc(done_v, 1)
            dve.wait_ge(wT_ps, 1)
            w4 = psB[:, :].rearrange("p (q n two) -> p q n two", q=4, two=2)[:, :, :, 1:2]
            for q in range(4):
                dve.tensor_copy(wT[:, q, :].rearrange("p (n two) -> p n two", two=2),
                                w4[:, q].broadcast_to([P, D, 2])).then_inc(wT_ok, 1)
            def tiles(buf, q):
                return buf[:, :].rearrange("p (g q n) -> p q g n", q=4, n=P)[:, q]

            def product(q):
                dve.wait_ge(p_ps, q + 1)
                dve.tensor_tensor(tiles(zp, q), psP[:, q, :].rearrange("p (g n) -> p g n", n=P), k.zT[:, q:TILES:4, :],
                                  ALU.mult).then_inc(zp_ok, 1)

            product(0)
            for q in range(4):
                if q < 3:
                    product(q + 1)
                dve.wait_ge(zs_ok, q + 1)
                dve.tensor_tensor(tiles(zs, q)[D:P], tiles(zp, q)[D:P], tiles(zs, q)[D:P], ALU.subtract).then_inc(z_fin, 1)
                for n in range(4 * q, 4 * q + 4):
                    dve.wait_ge(d_ps, n + 1)
                    t = order[n]
                    dve.scalar_tensor_tensor(out=k.x[:, t, :], in0=psD[n % 4][:, :], scalar=1.0 / W_SCALE,
                                             in1=k.x[:, t, :], op0=ALU.mult, op1=ALU.add).then_inc(o_ok, 1)

        @block.scalar
        def _(act):
            act.wait_ge(done_v, 3)
            act.activation(e[:, :, :], lg[:, :, :], ACT.Exp).then_inc(act_ok, 1)
            act.wait_ge(done_v, 4)
            act.activation(w[:, :, :], u[:, :, :], ACT.Exp, scale=-2.0).then_inc(act_ok, 1)
            for q in range(4):
                act.wait_ge(zp_ok, q + 1)
                act.activation(zs[:, :].rearrange("p (g q n) -> p q g n", q=4, n=P)[:, q],
                               zp[:, :].rearrange("p (g q n) -> p q g n", q=4, n=P)[:, q], ACT.Copy).then_inc(zs_ok, 1)

        @block.sync
        def _(sp):
            for n, t in enumerate(order):
                sp.wait_ge(o_ok, n + 1)
                sp.dma_start(out[t], k.x[:, t, :]).then_inc(store, 16)
            sp.wait_ge(store, 16 * TILES)

        @block.tensor
        def _(pe):
            for t in range(TILES):
                mm = pe.matmul(psA[:, t * EXPERTS:(t + 1) * EXPERTS], k.zT[0:RANK, t, :], k.limesT[:, :],
                               start=True, stop=True)
            mm.then_inc(a_ps, 1)
            pe.wait_ge(done_v, 1)
            pe.transpose(psB[0:2, 0:P], mx2[:, :], k.ident[:, :]).then_inc(a_ps, 1)
            pe.wait_ge(done_v, 2)
            pe.matmul(psA[:, 256:258], ones2[:, :], diag[:, 0:2], start=True, stop=True).then_inc(a_ps, 1)
            pe.wait_ge(done_v, 5)
            for q in range(4):
                mm = pe.transpose(chunk(psB, q), wf[:, 4 * q:4 * q + 4, :].rearrange("p a b -> p (a b)"), k.ident[:, :])
            mm.then_inc(wT_ps, 1)
            pe.wait_ge(wT_ok, 4)
            for n, t in enumerate(order):
                r0 = RANK * (t % 4)
                mm = pe.matmul(psP[:, t % 4, (t // 4) * P:(t // 4 + 1) * P],
                               k.limes4[r0:r0 + EXPERTS, :, :].rearrange("p a b -> p (a b)"),
                               wT[r0:r0 + EXPERTS, t // 4, :], start=True, stop=True)
                if n % 4 == 3:
                    mm.then_inc(p_ps, 1)
            for n, t in enumerate(order):
                pe.wait_ge(z_fin, n // 4 + 1)
                if n >= 4:
                    pe.wait_ge(o_ok, n - 3)
                pe.matmul(psD[n % 4][:, :], chunk(zs, t), k.bm_parts[:, :], start=True, stop=True).then_inc(d_ps, 1)


def program(nc, a):
    with ExitStack() as ctx:
        s = Scope(nc, ctx, "all")
        k = Shared()
        k.x = s.sb("x_res", [P, TILES, L])
        k.mv = s.sb("mv", [P, TILES, 2])
        k.rstd = s.sb("rstd", [P, TILES])
        k.rs = Shared()
        k.rs.v, k.rs.ln, k.rs.y, k.rs.t = (s.sb("rs_" + n, [P, TILES]) for n in ("v", "ln", "y", "t"))
        k.rs.v_ok, k.rs.ln_ok, k.rs.y_ok, k.rs.t_ok, k.rs.rstd_ok = (
            s.sem("rs_" + n) for n in ("v_ok", "ln_ok", "y_ok", "t_ok", "rstd_ok"))
        k.passed = s.sem("passed")
        k.xabs = s.sb("xabs", [P, TILES])
        k.ident = s.sb("ident", [P, P])
        k.ident16 = s.sb("ident16", [P, P], BF16)
        k.ident_h = s.sb("ident_h", [P, P], F16)
        k.ones = s.sb("ones", [P, P], BF16)
        k.ones32 = s.sb("ones32", [P, P])
        k.ind = s.sb("ind", [P, L], BF16)
        k.blk = s.sb("blk", [P, P])
        k.odd = s.sb("odd", [P, 1])
        k.m_round = s.sb("m_round", [P, 1])
        k.m_minus = s.sb("m_minus", [P, 1])
        k.half_ln = s.sb("half_ln", [P, 1])
        k.bias_rows = [s.sb(f"bias_rows{i}", [P, L], BF16) for i in range(3)]
        k.bv2, k.bo2, k.bo1, k.g8 = (s.sb(n, [P, 1]) for n in ("bv2", "bo2", "bo1", "g8"))
        k.wT0 = s.sb("wT0", [P, 4, P])
        k.wq_hi, k.wq_lo, k.wk_hi, k.wk_lo = (s.sb(n, [P, L], F16) for n in ("wq_hi", "wq_lo", "wk_hi", "wk_lo"))
        k.wv_wo = s.sb("wv_wo", [P, HEADS, D])
        k.WT_hi, k.WT_lo = (s.sb(n, [P, NC, L], F16) for n in ("WT_hi", "WT_lo"))
        k.A_hi, k.A_lo = (s.sb(n, [P, NC, P], F16) for n in ("A_hi", "A_lo"))
        k.bm_parts = s.sb("bm_parts", [P, L], F16)
        k.limes4 = s.sb("limes4", [P, 4, RANK])
        k.limesT = s.sb("limesT", [RANK, EXPERTS])
        k.ffs = s.sb("ffs", [P, 3])
        k.ffw = s.sb("ffw", [P, 3])
        k.s4, k.sg, k.su, k.su_abs, k.sd = (s.sb(n, [P, TILES]) for n in ("s4", "sg", "su", "su_abs", "sd"))
        k.wabs = s.sb("wabs", [P, 3, TILES // 2])
        k.late_in = s.sem("late_in")
        k.n_late = 1 + 4 + 4 + 3 + 12 + 1 + 3
        k.cf = s.sb("cf", [P, L])
        k.c_in = s.sem("c_in")
        k.ctx_in = [s.sem(f"ctx_in{p}") for p in range(2)]
        with ExitStack() as ctx_a:
            f = Scope(nc, ctx_a, "all")
            k.raw = [f.sb("raw_g", [P, FFC, L]), f.sb("raw_u", [P, FFC, L]), f.sb("raw_d", [P, NC, FF])]
            late = k.late = Shared()
            late.wdup = f.sb("wdup", [P, 2, NC, P])
            late.wo1 = f.sb("wo1", [D, L])
            late.wv1 = f.sb("wv1", [P, NC, D])
            late.wo1T = f.sb("wo1T", [P, NC, D])
            late.w_nat = f.sb("w_nat", [P, NC, L])
            late.A4 = f.sb("A4", [P, NC, P])
            late.brow = f.sb("brow", [1, L])
            late.part = f.sb("part", [1, L], BF16)
            late.bm = f.sb("bm", [P, L])
            with ExitStack() as ctx_n:
                g = Scope(nc, ctx_n, "all")
                k.ctx_n = [g.sb(f"ctx_n{p}", [P, L]) for p in range(2)]
                k.ctx_h = [g.sb(f"ctx_h{p}", [P, 2, NC, D]) for p in range(2)]
                setup(nc, a, k)
                attention0(nc, a, k)
            k.wgT = f.sb("wgT", [P, NC, FF], BF16)
            k.wuT = f.sb("wuT", [P, NC, FF], BF16)
            k.wdT = f.sb("wdT", [P, FFC, L], BF16)
            ternary_weights(nc, a, k)
            feed_forward(nc, a, k)
        with ExitStack() as ctx_c:
            c = Scope(nc, ctx_c, "all")
            k.M = c.sb("M", [P, BATCHES, NC, D])
            key_side(nc, a, k)
            query_side(nc, a, k)
        k.zT = s.sb("zT", [P, TILES, P])
        k.Hs = s.sb("Hs", [P, TILES, EXPERTS])
        projection(nc, a, k)
        experts(nc, a, k)


_INS = dict(x="x", ctx_4096="ctx", L0_xattn_Wq="Wq0", L0_xattn_bq="bq0", L0_xattn_Wk="Wk0", L0_xattn_bk="bk0",
            L0_xattn_Wv="Wv0", L0_xattn_bv="bv0", L0_xattn_Wo="Wo0", L0_xattn_bo="bo0", L0_ffn_w_gate="wg",
            L0_ffn_w_up="wu", L0_ffn_w_down="wd", L0_ffn_s_gate="sg", L0_ffn_s_up="su", L0_ffn_s_down="sd",
            L1_xattn_Wq="Wq1", L1_xattn_Wk="Wk1", L1_xattn_Wv="Wv1", L1_xattn_Wo="Wo1", L1_xattn_bo="bo1",
            L1_xattn_g="g1", L1_ffn_W="W1", L1_ffn_b="b1", L1_ffn_A="A1", L1_ffn_Bmat="Bm1", L1_ffn_LiMEs="Li1")


def kernel(**inputs):
    import numpy as _np
    import concourse.bacc as _bacc
    from concourse import mybir as _mybir
    from concourse.bass_utils import run_bass_kernel_spmd as _run

    nc = _bacc.Bacc("TRN2", target_bir_lowering=False, num_devices=1)
    arrays, args = {}, {}
    for name, short in _INS.items():
        v = _np.ascontiguousarray(inputs[name])
        arrays[f"in_{name}_dram"] = v
        args[short] = nc.dram_tensor(f"in_{name}_dram", v.shape, _mybir.dt.from_np(v.dtype), kind="ExternalInput").ap()
    args["out"] = nc.dram_tensor("out_0_dram", (BATCHES, D, L), F32, kind="ExternalOutput").ap()
    program(nc, args)
    r = _run(nc, [arrays], core_ids=[0])
    return r.results[0]["out_0_dram"]
```
